# Optimizing a Trainium2 kernel written in Bass

```python
import numpy as np
import jax
import jax.numpy as jnp

def _softmax(x, axis=-1):
    return jax.nn.softmax(x, axis=axis)

def _gelu(x):
    return jax.nn.gelu(x, approximate=True)

def _silu(x):
    return jax.nn.silu(x)

def _sigmoid(x):
    return jax.nn.sigmoid(x)

def _layernorm(x, axis=-1, eps=1e-05):
    m = jnp.mean(x, axis=axis, keepdims=True)
    v = jnp.var(x, axis=axis, keepdims=True)
    return (x - m) / jnp.sqrt(v + eps)

def _scatter_add(tgt, idx, src, axis=0):
    return tgt.at[idx].add(src)

def _segment_sum(src, seg, n):
    return jax.ops.segment_sum(src, seg, n)
kernel_name = 'mk_sandwich_d2_jaxref_r8_4eff46'

def setup_inputs(seed: int=0):
    np.random.seed(seed)
    _w = jnp.asarray

    def _L0_attn_setup():
        import jax, jax.numpy as jnp
        import numpy as np
        NF4 = jnp.array([-1.0, -0.6961928009986877, -0.5250730514526367, -0.39491748809814453, -0.28444138169288635, -0.18477343022823334, -0.09105003625154495, 0.0, 0.07958029955625534, 0.16093020141124725, 0.24611230194568634, 0.33791524171829224, 0.44070982933044434, 0.5626170039176941, 0.7229568362236023, 1.0], dtype=jnp.float32)
        BLOCK = 64

        def _dequant(codes, scales):
            w = NF4[codes]
            O, I = w.shape
            w = w.reshape(O, I // BLOCK, BLOCK) * scales[:, :, None]
            return w.reshape(O, I)

        def _lin_lora(x, W, A, B):
            base = jnp.einsum('bsh,oh->bso', x, W)
            lora = jnp.einsum('bsr,or->bso', jnp.einsum('bsh,rh->bsr', x, A), B)
            return base + lora
        H, I, R, BT, S = (512, 1792, 16, 2, 256)
        key = jax.random.key(seed)
        ks = jax.random.split(key, 12)
        x = jax.random.normal(ks[0], (BT, S, H), jnp.float32)
        codes_attn = jax.random.randint(ks[1], (4, H, H), 0, 16, jnp.int32)
        scales_attn = jax.random.uniform(ks[2], (4, H, H // BLOCK), jnp.float32) * 0.02
        codes_gu = jax.random.randint(ks[3], (2, I, H), 0, 16, jnp.int32)
        scales_gu = jax.random.uniform(ks[4], (2, I, H // BLOCK), jnp.float32) * 0.02
        codes_down = jax.random.randint(ks[5], (H, I), 0, 16, jnp.int32)
        scales_down = jax.random.uniform(ks[6], (H, I // BLOCK), jnp.float32) * 0.02
        lora_A_h = jax.random.normal(ks[7], (6, R, H), jnp.float32) * 0.02
        lora_A_down = jax.random.normal(ks[8], (R, I), jnp.float32) * 0.02
        lora_B_attn = jax.random.normal(ks[9], (4, H, R), jnp.float32) * 0.02
        lora_B_gu = jax.random.normal(ks[10], (2, I, R), jnp.float32) * 0.02
        lora_B_down = jax.random.normal(ks[11], (H, R), jnp.float32) * 0.02
        return dict(x=x, codes_attn=codes_attn, scales_attn=scales_attn, codes_gu=codes_gu, scales_gu=scales_gu, codes_down=codes_down, scales_down=scales_down, lora_A_h=lora_A_h, lora_A_down=lora_A_down, lora_B_attn=lora_B_attn, lora_B_gu=lora_B_gu, lora_B_down=lora_B_down)
    _L0_attn_in = _L0_attn_setup()

    def _L0_ffn_setup():
        import jax, jax.numpy as jnp
        import numpy as np

        def sparsemax(z):
            E = z.shape[-1]
            z_sorted = -jnp.sort(-z, axis=-1)
            z_cum = jnp.cumsum(z_sorted, axis=-1)
            k = jnp.arange(1, E + 1, dtype=z.dtype)
            support = 1.0 + k * z_sorted > z_cum
            k_z = jnp.sum(support, axis=-1, keepdims=True)
            tau_sum = jnp.take_along_axis(z_cum, k_z.astype(jnp.int32) - 1, axis=-1)
            tau = (tau_sum - 1.0) / k_z.astype(z.dtype)
            return jnp.maximum(z - tau, 0.0)
        key = jax.random.key(seed)
        ks = jax.random.split(key, 6)
        B, S, D_IN, D_OUT, E, R = (8, 256, 512, 512, 8, 16)
        x = jax.random.normal(ks[0], (B, S, D_IN), dtype=jnp.float32)
        W_base = jax.random.normal(ks[1], (D_OUT, D_IN), dtype=jnp.float32) * D_IN ** (-0.5)
        b_base = jax.random.normal(ks[2], (D_OUT,), dtype=jnp.float32) * 0.01
        W_router = jax.random.normal(ks[3], (E, D_IN), dtype=jnp.float32) * D_IN ** (-0.5)
        b_router = jnp.zeros((E,), dtype=jnp.float32)
        lora_A = jax.random.normal(ks[4], (E, D_IN, R), dtype=jnp.float32) * D_IN ** (-0.5)
        lora_B = jnp.zeros((E, R, D_OUT), dtype=jnp.float32)
        return {'x': x, 'W_base': W_base, 'b_base': b_base, 'W_router': W_router, 'b_router': b_router, 'lora_A': lora_A, 'lora_B': lora_B}
    _L0_ffn_in = _L0_ffn_setup()

    def _L1_attn_setup():
        import math
        import jax, jax.numpy as jnp
        import numpy as np
        NUM_HEADS = 32
        HIDDEN = 512
        HEAD_DIM = HIDDEN // NUM_HEADS
        NEG_INF = -1e+30

        def _alibi_slopes(n: int) -> jnp.ndarray:
            cp2 = 2 ** math.floor(math.log2(n))
            base = 2.0 ** (-2.0 ** (-(math.log2(cp2) - 3)))
            slopes = base ** np.arange(1, cp2 + 1, dtype=np.float64)
            if cp2 != n:
                extra_base = 2.0 ** (-2.0 ** (-(math.log2(2 * cp2) - 3)))
                rem = min(cp2, n - cp2)
                extra = extra_base ** np.arange(1, 1 + 2 * rem, 2, dtype=np.float64)
                slopes = np.concatenate([slopes, extra])
            return jnp.asarray(slopes, dtype=jnp.float32)
        key = jax.random.key(seed)
        k1, k2, k3 = jax.random.split(key, 3)
        B, S = (2, 256)
        hidden_states = jax.random.normal(k1, (B, S, HIDDEN), dtype=jnp.float32)
        Wqkv = jax.random.normal(k2, (HIDDEN, NUM_HEADS * HEAD_DIM + 2 * HEAD_DIM), dtype=jnp.float32) * 0.02
        Wo = jax.random.normal(k3, (HIDDEN, HIDDEN), dtype=jnp.float32) * 0.02
        return {'hidden_states': hidden_states, 'Wqkv': Wqkv, 'Wo': Wo}
    _L1_attn_in = _L1_attn_setup()

    def _L1_ffn_setup():
        import jax, jax.numpy as jnp
        import numpy as np
        TOP_K = 2
        key = jax.random.key(seed)
        k0, k1, k2 = jax.random.split(key, 3)
        B, S, D, H, E = (4, 256, 512, 512, 8)
        sc = 1.0 / np.sqrt(D).astype(np.float32)
        x = jax.random.normal(k0, (B, S, D), dtype=jnp.float32)
        W_gate = jax.random.normal(k1, (D, E), dtype=jnp.float32) * sc
        b_gate = jnp.zeros((E,), dtype=jnp.float32)
        W_e = jax.random.normal(k2, (E, D, H), dtype=jnp.float32) * sc
        b_e = jnp.zeros((E, H), dtype=jnp.float32)
        return {'x': x, 'W_gate': W_gate, 'b_gate': b_gate, 'W_e': W_e, 'b_e': b_e}
    _L1_ffn_in = _L1_ffn_setup()
    _d = {'L0_attn_x': _L0_attn_in['x'], 'L0_attn_codes_attn': _L0_attn_in['codes_attn'], 'L0_attn_scales_attn': _L0_attn_in['scales_attn'], 'L0_attn_codes_gu': _L0_attn_in['codes_gu'], 'L0_attn_scales_gu': _L0_attn_in['scales_gu'], 'L0_attn_codes_down': _L0_attn_in['codes_down'], 'L0_attn_scales_down': _L0_attn_in['scales_down'], 'L0_attn_lora_A_h': _L0_attn_in['lora_A_h'], 'L0_attn_lora_A_down': _L0_attn_in['lora_A_down'], 'L0_attn_lora_B_attn': _L0_attn_in['lora_B_attn'], 'L0_attn_lora_B_gu': _L0_attn_in['lora_B_gu'], 'L0_attn_lora_B_down': _L0_attn_in['lora_B_down'], 'L0_ffn_W_base': _L0_ffn_in['W_base'], 'L0_ffn_b_base': _L0_ffn_in['b_base'], 'L0_ffn_W_router': _L0_ffn_in['W_router'], 'L0_ffn_b_router': _L0_ffn_in['b_router'], 'L0_ffn_lora_A': _L0_ffn_in['lora_A'], 'L0_ffn_lora_B': _L0_ffn_in['lora_B'], 'L1_attn_Wqkv': _L1_attn_in['Wqkv'], 'L1_attn_Wo': _L1_attn_in['Wo'], 'L1_ffn_W_gate': _L1_ffn_in['W_gate'], 'L1_ffn_b_gate': _L1_ffn_in['b_gate'], 'L1_ffn_W_e': _L1_ffn_in['W_e'], 'L1_ffn_b_e': _L1_ffn_in['b_e']}
    _x0 = _d['L0_attn_x']
    _d['L0_attn_x'] = jax.random.normal(jax.random.fold_in(jax.random.key(seed), 1), (2, 512, 512), dtype=_x0.dtype)
    del _x0
    return _d

def reference(L0_attn_x, L0_attn_codes_attn, L0_attn_scales_attn, L0_attn_codes_gu, L0_attn_scales_gu, L0_attn_codes_down, L0_attn_scales_down, L0_attn_lora_A_h, L0_attn_lora_A_down, L0_attn_lora_B_attn, L0_attn_lora_B_gu, L0_attn_lora_B_down, L0_ffn_W_base, L0_ffn_b_base, L0_ffn_W_router, L0_ffn_b_router, L0_ffn_lora_A, L0_ffn_lora_B, L1_attn_Wqkv, L1_attn_Wo, L1_ffn_W_gate, L1_ffn_b_gate, L1_ffn_W_e, L1_ffn_b_e):

    def _L0_attn_ref(x, codes_attn, scales_attn, codes_gu, scales_gu, codes_down, scales_down, lora_A_h, lora_A_down, lora_B_attn, lora_B_gu, lora_B_down):
        import jax, jax.numpy as jnp
        import numpy as np
        NF4 = jnp.array([-1.0, -0.6961928009986877, -0.5250730514526367, -0.39491748809814453, -0.28444138169288635, -0.18477343022823334, -0.09105003625154495, 0.0, 0.07958029955625534, 0.16093020141124725, 0.24611230194568634, 0.33791524171829224, 0.44070982933044434, 0.5626170039176941, 0.7229568362236023, 1.0], dtype=jnp.float32)
        BLOCK = 64

        def _dequant(codes, scales):
            w = NF4[codes]
            O, I = w.shape
            w = w.reshape(O, I // BLOCK, BLOCK) * scales[:, :, None]
            return w.reshape(O, I)

        def _lin_lora(x, W, A, B):
            base = jnp.einsum('bsh,oh->bso', x, W)
            lora = jnp.einsum('bsr,or->bso', jnp.einsum('bsh,rh->bsr', x, A), B)
            return base + lora
        q = _lin_lora(x, _dequant(codes_attn[0], scales_attn[0]), lora_A_h[0], lora_B_attn[0])
        k = _lin_lora(x, _dequant(codes_attn[1], scales_attn[1]), lora_A_h[1], lora_B_attn[1])
        v = _lin_lora(x, _dequant(codes_attn[2], scales_attn[2]), lora_A_h[2], lora_B_attn[2])
        attn = (q + k + v) / 3.0
        o = _lin_lora(attn, _dequant(codes_attn[3], scales_attn[3]), lora_A_h[3], lora_B_attn[3])
        x1 = x + o
        g = _lin_lora(x1, _dequant(codes_gu[0], scales_gu[0]), lora_A_h[4], lora_B_gu[0])
        u = _lin_lora(x1, _dequant(codes_gu[1], scales_gu[1]), lora_A_h[5], lora_B_gu[1])
        h = jax.nn.silu(g) * u
        d = _lin_lora(h, _dequant(codes_down, scales_down), lora_A_down, lora_B_down)
        return x1 + d

    def _L0_ffn_ref(x, W_base, b_base, W_router, b_router, lora_A, lora_B):
        import jax, jax.numpy as jnp
        import numpy as np

        def sparsemax(z):
            E = z.shape[-1]
            z_sorted = -jnp.sort(-z, axis=-1)
            z_cum = jnp.cumsum(z_sorted, axis=-1)
            k = jnp.arange(1, E + 1, dtype=z.dtype)
            support = 1.0 + k * z_sorted > z_cum
            k_z = jnp.sum(support, axis=-1, keepdims=True)
            tau_sum = jnp.take_along_axis(z_cum, k_z.astype(jnp.int32) - 1, axis=-1)
            tau = (tau_sum - 1.0) / k_z.astype(z.dtype)
            return jnp.maximum(z - tau, 0.0)
        base_out = jnp.einsum('bsd,od->bso', x, W_base) + b_base
        logits = jnp.einsum('bsd,ed->bse', x, W_router) + b_router
        weights = sparsemax(logits)
        h = jnp.einsum('bsd,edr->bser', x, lora_A)
        expert_out = jnp.einsum('bser,bse,ero->bso', h, weights, lora_B)
        return base_out + expert_out

    def _L1_attn_ref(hidden_states, Wqkv, Wo):
        import math
        import jax, jax.numpy as jnp
        import numpy as np
        NUM_HEADS = 32
        HIDDEN = 512
        HEAD_DIM = HIDDEN // NUM_HEADS
        NEG_INF = -1e+30

        def _alibi_slopes(n: int) -> jnp.ndarray:
            cp2 = 2 ** math.floor(math.log2(n))
            base = 2.0 ** (-2.0 ** (-(math.log2(cp2) - 3)))
            slopes = base ** np.arange(1, cp2 + 1, dtype=np.float64)
            if cp2 != n:
                extra_base = 2.0 ** (-2.0 ** (-(math.log2(2 * cp2) - 3)))
                rem = min(cp2, n - cp2)
                extra = extra_base ** np.arange(1, 1 + 2 * rem, 2, dtype=np.float64)
                slopes = np.concatenate([slopes, extra])
            return jnp.asarray(slopes, dtype=jnp.float32)
        B, S, H = hidden_states.shape
        nH, d = (NUM_HEADS, HEAD_DIM)
        scale = d ** (-0.5)
        qkv = hidden_states @ Wqkv
        q = qkv[..., :nH * d].reshape(B, S, nH, d)
        k = qkv[..., nH * d:nH * d + d]
        v = qkv[..., nH * d + d:]
        scores = jnp.einsum('bqhd,bkd->bhqk', q, k) * scale
        pos_q = jnp.arange(S)[:, None]
        pos_k = jnp.arange(S)[None, :]
        slopes = _alibi_slopes(nH)
        alibi = slopes[:, None, None] * (pos_k - pos_q).astype(jnp.float32)
        causal = pos_k <= pos_q
        scores = jnp.where(causal[None, None], scores + alibi[None], NEG_INF)
        probs = jax.nn.softmax(scores, axis=-1)
        attn = jnp.einsum('bhqk,bkd->bqhd', probs, v).reshape(B, S, H)
        return attn @ Wo

    def _L1_ffn_ref(x, W_gate, b_gate, W_e, b_e):
        import jax, jax.numpy as jnp
        import numpy as np
        TOP_K = 2
        logits = x @ W_gate + b_gate
        _, top_idx = jax.lax.top_k(logits, TOP_K)
        y_all = jax.nn.relu(jnp.einsum('bsd,edh->bseh', x, W_e) + b_e)
        y = jnp.take_along_axis(y_all, top_idx[..., None], axis=2)
        return y.mean(axis=2)
    x = L0_attn_x
    x = x + _layernorm(_L0_attn_ref(_layernorm(x, axis=-1), L0_attn_codes_attn, L0_attn_scales_attn, L0_attn_codes_gu, L0_attn_scales_gu, L0_attn_codes_down, L0_attn_scales_down, L0_attn_lora_A_h, L0_attn_lora_A_down, L0_attn_lora_B_attn, L0_attn_lora_B_gu, L0_attn_lora_B_down), axis=-1)
    x = x + _layernorm(_L0_ffn_ref(_layernorm(x, axis=-1), L0_ffn_W_base, L0_ffn_b_base, L0_ffn_W_router, L0_ffn_b_router, L0_ffn_lora_A, L0_ffn_lora_B), axis=-1)
    x = x + _layernorm(_L1_attn_ref(_layernorm(x, axis=-1), L1_attn_Wqkv, L1_attn_Wo), axis=-1)
    x = x + _layernorm(_L1_ffn_ref(_layernorm(x, axis=-1), L1_ffn_W_gate, L1_ffn_b_gate, L1_ffn_W_e, L1_ffn_b_e), axis=-1)
    return x

_drawn_inputs = setup_inputs


def setup_inputs(seed=0):
    import zlib

    import numpy as np

    out = dict(_drawn_inputs(seed))
    spreads = {'L0_ffn_b_router': (0.0, 0.27),
     'L0_ffn_lora_B': (0.0, 0.1),
     'L1_ffn_b_gate': (0.0, 0.1),
     'L1_ffn_b_e': (0.0, 0.1)}
    factors = {'L0_attn_scales_attn': 2.68,
     'L0_attn_scales_gu': 3.852,
     'L0_attn_scales_down': 4.837,
     'L0_attn_lora_A_h': 2.788,
     'L0_attn_lora_A_down': 6.757,
     'L0_attn_lora_B_attn': 2.69,
     'L0_attn_lora_B_gu': 4.841,
     'L0_attn_lora_B_down': 6.855}
    for name, (base, spread) in spreads.items():
        noise = np.random.default_rng([zlib.crc32(name.encode()), seed]).standard_normal(out[name].shape)
        drawn = base * np.exp(spread * noise) if base else spread * noise
        out[name] = jnp.asarray(drawn.astype(out[name].dtype))
    for name, factor in factors.items():
        out[name] = (out[name] * factor).astype(out[name].dtype)
    return out
```

```python
from contextlib import ExitStack

import concourse.bass as bass
from concourse import mybir

F32 = mybir.dt.float32
F16 = mybir.dt.float16
BF16 = mybir.dt.bfloat16
I32 = mybir.dt.int32
U32 = mybir.dt.uint32
ALU = mybir.AluOpType
ACT = mybir.ActivationFunctionType
AX_X = mybir.AxisListType.X

P = 128
T = 1024
TT = T // P
D = 512
KC = D // P
HF = T // 512
INTER = 1792
OC = INTER // P
HEADS, HD = 32, 16
NE = 8
R = 16
WSCALE = 256.0
EPS = 1e-5
NEG = -1e30
NF4 = [-1.0, -0.6961928009986877, -0.5250730514526367, -0.39491748809814453, -0.28444138169288635,
       -0.18477343022823334, -0.09105003625154495, 0.0, 0.07958029955625534, 0.16093020141124725,
       0.24611230194568634, 0.33791524171829224, 0.44070982933044434, 0.5626170039176941,
       0.7229568362236023, 1.0]

LA = {"qk": 0, "v": 512, "o": 1024, "gu": 1536, "down": 2048}
LA_N = 2048 + INTER
LB = {"qk": 0, "v": 512, "o": 1024, "gu": 1536, "down": 1536 + 2 * INTER}
LB_N = 2048 + 2 * INTER

N_ATTN, N_GU, N_DOWN = 8, 14, 7
N_HU = N_ATTN + N_GU + N_DOWN


def nf4_line(i, j):
    s = (NF4[j] - NF4[i]) / (j - i)
    return s, NF4[i] - s * i


POS = [nf4_line(8, 9), nf4_line(10, 11), nf4_line(12, 13), nf4_line(14, 15)]
MINUS = [tuple(-a for a in nf4_line(i, i + 1)) for i in (6, 4, 2, 0)]


class Ring:

    def __init__(self, sem, name, slots, keys):
        self.slots = slots
        self.n = len(slots)
        self.index = {k: i for i, k in enumerate(keys)}
        assert len(self.index) == len(keys)
        self.full_sems = [sem(f"{name}_full{s}") for s in range(self.n)]
        self.free_sems = [sem(f"{name}_free{s}") for s in range(self.n)]

    def at(self, key):
        return self.slots[self.index[key] % self.n]

    def full(self, key):
        return self.full_sems[self.index[key] % self.n]

    def free(self, key):
        return self.free_sems[self.index[key] % self.n]

    def wait_free(self, eng, key):
        use = self.index[key] // self.n
        if use:
            eng.wait_ge(self.free(key), use)

    def wait_full(self, eng, key):
        eng.wait_ge(self.full(key), self.index[key] // self.n + 1)

    def wait_read(self, eng, key):
        eng.wait_ge(self.free(key), self.index[key] // self.n + 1)

    def wait_all_free(self, eng):
        total = len(self.index)
        for s in range(self.n):
            uses = (total - s + self.n - 1) // self.n
            if uses:
                eng.wait_ge(self.free_sems[s], uses)


def sandwich(nc, I, out):
    ctx = ExitStack()
    with ctx:
        sems = {}

        def S(name):
            if name not in sems:
                sems[name] = ctx.enter_context(nc.semaphore(name))
            return sems[name]

        ARENA = 207 * 1024
        arena = ctx.enter_context(nc.sbuf_tensor("arena", [P, ARENA // 4], F32))
        K = 1024

        def at(offset, cols, dt=F32):
            size = cols * {F32: 4, I32: 4, U32: 4, F16: 2, BF16: 2}[dt]
            assert offset % 4 == 0 and size % 4 == 0 and offset + size <= ARENA, (offset, size)
            v = arena[:, offset // 4:(offset + size) // 4]
            return v if dt == F32 else v.bitcast(dt)

        def grid(offset, a, b, dt=F32):
            return at(offset, a * b, dt).rearrange("p (a b) -> p a b", a=a)

        X = grid(0, TT, D)
        M16 = [grid(0, KC, T, F16), grid(8 * K, KC, T, F16)]
        SG = grid(0, 2, 512)
        HFULL = grid(4 * K, 2, 512)
        XT = [grid(16 * K, KC, T, F16), grid(24 * K, KC, T, F16)]
        GUW = [[grid((o + 4 * h) * K, KC, 512, F16) for h in range(2)] for o in (96, 88, 64, 16, 24, 8, 16)]
        X1T = [grid(32 * K, KC, T, F16), grid(40 * K, KC, T, F16)]
        XN_A = grid(32 * K, 2, D)
        H16 = [grid(48 * K, OC, T, F16), grid(76 * K, OC, T, F16)]
        MW = [grid(48 * K, KC, D, F16), grid(52 * K, KC, D, F16)]
        OW = [grid(56 * K, KC, D, F16), grid(60 * K, KC, D, F16)]
        L32 = at(64 * K, LA_N + LB_N)
        DW = [grid(104 * K, OC, D, F16), grid(118 * K, OC, D, F16)]
        MSUM = grid(104 * K, KC, D)
        PB = grid(132 * K, 4, 1024)
        NB = grid(148 * K, 2, 1024)
        LN_ = grid(156 * K, 3, 1024)
        CODES = grid(168 * K, 2, 1024, I32)
        SC = grid(176 * K, 2, 1024)
        L16 = at(184 * K, LA_N + LB_N, F16)
        STAGE = grid(132 * K, 2, 2048)
        PT4 = at(132 * K, 4096).rearrange("p (s h t) -> p s h t", s=2, h=4)
        XN_C = grid(132 * K, 2, D)
        YN_B = grid(136 * K, 2, D)
        XN_B = grid(148 * K, 2, D)
        YN = grid(152 * K, 2, D)
        OT = grid(148 * K, 2, D)
        o = 156 * K
        BW = [grid(o, KC, D, F16), grid(o + 4 * K, KC, D, F16)]
        o += 8 * K
        QW = [grid(o, KC, D, F16), grid(o + 4 * K, KC, D, F16)]
        o += 8 * K
        WOW = [grid(o, KC, D, F16), grid(o + 4 * K, KC, D, F16)]
        o += 8 * K
        BE = at(o, NE * D, F16)
        o += 8 * K
        RN = NE + NE * R
        RW = [grid(o, KC, RN, F16), grid(o + KC * RN * 2, KC, RN, F16)]
        o += KC * RN * 4
        LBW = [at(o, D, F16), at(o + K, D, F16)]
        o += 2 * K
        BB = at(o, D, F16)
        o += K
        KW = [grid(o, KC, P, F16), grid(o + K, KC, P, F16)]
        o += 2 * K
        VW = [grid(o, KC, HD, F16), grid(o + KC * HD * 2, KC, HD, F16)]
        o += KC * HD * 4
        GW = [grid(o, KC, NE, F16), grid(o + KC * NE * 2, KC, NE, F16)]
        o += KC * NE * 4
        assert o <= 199 * K
        HWF = grid(o, 2, P)
        o += K
        RSB = grid(o + K, 2, RN)
        HWT = grid(o, 2, 2 * P, F16)
        o += K
        o = 203 * K
        assert 184 * K + 2 * (LA_N + LB_N) <= o
        IDF = at(o, P)
        o += 4 * P
        I256 = at(o, P, F16)
        o += 2 * P
        ONES = at(o, P, F16)
        o += 2 * P
        IDB = at(o, P, BF16)
        o += 2 * P
        MASKQ = at(o, P, BF16)
        o += 2 * P
        MASKK = at(o, P, BF16)
        o += 2 * P
        SMALL = at(o, (ARENA - o) // 4)
        so = [0]

        def small(a, b=1):
            v = SMALL[:, so[0]:so[0] + a * b].rearrange("p (a b) -> p a b", a=a)
            so[0] += a * b
            return v

        STAT = {(s, w): small(2, 6) for s in "ABCD" for w in "xy"}
        MV = {(s, w): small(2, 2) for s in "ABCD" for w in "xy"}
        SD = {(s, w): small(2, 1) for s in "ABCD" for w in "xy"}
        RS = {(s, w): small(2, 1) for s in "ABCD" for w in "xy"}
        NM = {(s, w): small(2, 1) for s in "ABCD" for w in "xy"}
        EPSX = small(1, 1)[:, 0, :]
        EPSY = small(1, 1)[:, 0, :]
        RB = small(1, NE)[:, 0, :]
        GB = small(1, NE)[:, 0, :]
        INVK = small(1, NE)[:, 0, :]
        CUM = small(3, 4 + NE)
        ZB = small(6, NE)
        GS = small(TT, NE)
        LT = small(NE, NE)
        CMP = small(2, NE * NE)

        QX = [grid(32 * K + 32 * K * b, HEADS, 512, F16) for b in range(HF)]
        ATTN = grid(96 * K, TT, D)
        Q16 = [grid(112 * K, KC, T, F16), grid(120 * K, KC, T, F16)]
        K16 = [at(128 * K, T, F16), at(130 * K, T, F16)]
        KX = at(201 * K, T, F16)
        V1 = grid(152 * K, TT, 32)
        MX = grid(153 * K, TT, HEADS)
        MROW = at(154 * K, T, F16)
        RDEN = grid(128 * K, 2, 16)
        EW = [[grid(32 * K + 8 * K * s + 4 * K * h, KC, D, F16) for h in range(2)] for s in range(2)]
        YACC = grid(48 * K, TT, D)
        YE = grid(64 * K, 2, D)

        psum = ctx.enter_context(nc.psum_tensor("psum", [P, 8, 512], F32))

        def banks(first, count, each=1):
            return [psum[:, i, :] if each == 1 else psum[:, i:i + each, :] for i in range(first, first + count * each, each)]

        j_hf = [(j, hf) for j in range(KC) for hf in range(HF)]
        main = [("T", tt) for tt in range(TT)] + [("m", *t) for t in j_hf] + [("o", *t) for t in j_hf]
        for oc in range(OC):
            for hf in range(HF):
                main += [("g", oc, hf), ("u", oc, hf)]
        ring_main = Ring(S, "main", banks(0, 4), main)
        ring_lora = Ring(S, "lora", banks(4, 2, 2), range(4, N_HU))
        ring_d = Ring(S, "down", banks(0, 2), range(TT))
        ring_b = Ring(S, "mix", banks(2, 4), range(TT))
        STEPS_B = TT + 6
        small_tiles = []
        for s in range(STEPS_B):
            small_tiles += [("TC", s - 6)] if 0 <= s - 6 < TT else []
            small_tiles += [("TB", s - 2), ("r", s - 2)] if 0 <= s - 2 < TT else []
            small_tiles += [("H", s - 3)] if 0 <= s - 3 < TT else []
        ring_s = Ring(S, "small", banks(6, 2), small_tiles)
        ring_p = Ring(S, "proj", banks(0, 4), [("k", 0), ("k", 1)] + [("v", tt) for tt in range(TT)]
                      + [("q", j, hf) for hf in range(HF) for j in range(KC)])
        max_tiles = []
        for tt in range(TT):
            max_tiles += [(tt, h) for h in range(HEADS)] + [(tt, "t")]
        ring_max = Ring(S, "max", banks(0, 2), max_tiles)
        score_tiles = [(b, hg, j, hp) for b in range(HF) for hg in range(8) for j in range(4) for hp in range(2)]
        ring_sc = Ring(S, "score", banks(2, 2, 2), score_tiles)
        groups = [(b, hg) for b in range(HF) for hg in range(8)]
        ring_pv = Ring(S, "pv", banks(6, 2), [k for g in groups for k in (("pv", *g), ("pt", *g))])
        STEPS_D = TT + 3
        tail = []
        for s in range(STEPS_D):
            tail += [("aT", s)] if s < TT else []
            tail += [("w", s - 1)] if 0 <= s - 1 < TT else []
            tail += [("TD", s - 3), ("z", s - 3)] if 0 <= s - 3 < TT else []
        tail += [("e", e, tt) for e in range(NE) for tt in range(TT)]
        ring_tail = Ring(S, "tail", banks(0, 6), tail)

        pieces = [("base", I["w_base"], KC * D, BW), ("router", I["w_rl"], KC * RN, RW), ("lorab", I["lora_b"], D, LBW),
                  ("bias", I["b_base"], D, BB), ("q", I["w_q"], KC * D, QW), ("k", I["w_k"], KC * P, KW),
                  ("v", I["w_v"], KC * HD, VW), ("wo", I["w_o"], KC * D, WOW), ("gate", I["w_gate"], KC * NE, GW),
                  ("be0", I["b_e"][:, 0:2048], 2048, BE[:, 0:2048]), ("be1", I["b_e"][:, 2048:4096], 2048, BE[:, 2048:4096])]
        pieces += [(f"e{e}", I["w_e"][e], KC * D, EW[e % 2]) for e in range(NE)]
        piece_at = {p[0]: i for i, p in enumerate(pieces)}
        NW = len(pieces) - NE

        lora_loads = []
        for name, row, col, n in (("a_q", 0, LA["qk"], D), ("a_k", R, LA["qk"], D), ("a_v", 0, LA["v"], D),
                                  ("a_o", 0, LA["o"], D), ("a_g", 0, LA["gu"], D), ("a_u", R, LA["gu"], D),
                                  ("a_down", 0, LA["down"], INTER), ("b_q", 0, LA_N + LB["qk"], D),
                                  ("b_k", R, LA_N + LB["qk"], D), ("b_v", 0, LA_N + LB["v"], D),
                                  ("b_o", 0, LA_N + LB["o"], D), ("b_down", 0, LA_N + LB["down"], D)):
            lora_loads.append((name, row, lambda p, col=col, n=n: L32[p:p + R, col:col + n]))
        for g, name in enumerate(("b_g", "b_u")):
            lora_loads.append((name, g * R, lambda p, g=g: L32[p:p + R, LA_N + LB["gu"]:LA_N + LB["down"]]
                               .rearrange("p (c g o) -> p c g o", c=OC // 2, g=2)[:, :, g, :]))

        taken_at = {}
        for i, t in enumerate(j_hf):
            taken_at.setdefault(N_ATTN + (i // 3), []).append(("m", *t))
            taken_at.setdefault(N_ATTN + 3 + (i // 3), []).append(("o", *t))
        for oc in range(OC):
            for hf in range(HF):
                taken_at.setdefault(N_ATTN + 6 + oc, []).append(("g", oc, hf))
        STEPS_A = N_HU + 2
        assert max(taken_at) < STEPS_A

        def flat(v):
            return v.rearrange("p a b -> p (a b)") if len(v.shape) == 3 else v

        def cols(n):
            return n // 2, n % 2

        def hu_weight(n, half):
            if n < N_ATTN:
                m, kh = cols(n)
                return (OW if m == 3 else MW)[half][:, 2 * kh:2 * kh + 2, :]
            if n < N_ATTN + N_GU:
                c, kh = cols(n - N_ATTN)
                return GUW[c][half][:, 2 * kh:2 * kh + 2, :]
            j = 2 * (n - N_ATTN - N_GU)
            return DW[half][:, j:j + 2, :]

        def n_scale_dmas(n):
            return sum(2 if i >= N_ATTN + N_GU else 1 for i in range(n % 2, n + 1, 2))

        q_dram = [nc.dram_tensor(f"q_half{i}", (D, T), F16, kind="Internal").ap() for i in range(2)]
        k_dram = [nc.dram_tensor(f"k_half{i}", (HD, T), F16, kind="Internal").ap() for i in range(2)]
        m_dram = nc.dram_tensor("minus_max", (HEADS, T), F16, kind="Internal").ap()

        block = ctx.enter_context(nc.Block())

        @block.sync
        def _(sp):
            for h in range(2):
                sp.dma_start(X[:, 4 * h:4 * h + 4, :], I["x"][:, 4 * h:4 * h + 4, :]).then_inc(S(f"x_in{h}"), 16)
            sp.dma_start(IDF, I["ident"]).then_inc(S("ident_in"), 16)

            def load_half_unit(n):
                c2 = CODES[:, n % 2, :]
                s2 = SC[:, n % 2, :]
                if n >= 2:
                    sp.wait_ge(S("line"), 8 * (n - 1))
                if n < N_ATTN:
                    m, kh = cols(n)
                    src, scale = I["codes_attn"][m][:, 1024 * kh:1024 * kh + 1024], I["scales_attn"][m]
                elif n < N_ATTN + N_GU:
                    c, kh = cols(n - N_ATTN)
                    src, scale = I["codes_gu"][c][:, 1024 * kh:1024 * kh + 1024], I["scales_gu"][c]
                else:
                    d = n - N_ATTN - N_GU
                    src, scale = I["codes_down"][d], None
                sp.dma_start(c2, src).then_inc(S(f"codes{n % 2}"), 16)
                if n >= 2:
                    sp.wait_ge(S("scaled"), n - 1)
                if scale is not None:
                    sp.dma_start(s2[:, 0:512], broadcast(scale, 16)).then_inc(S(f"scales{n % 2}"), 16)
                else:
                    for q in range(2):
                        sp.dma_start(s2[64 * q:64 * q + 64, :].rearrange("p (j o) -> p j o", j=2),
                                     repeat(I["scales_down"][4 * d + q:4 * d + 4:2], 64)).then_inc(S(f"scales{n % 2}"), 16)

            load_half_unit(0)
            load_half_unit(1)
            sp.dma_start(I256, I["ident256"]).then_inc(S("consts"), 16)
            sp.dma_start(ONES, I["ones_rows"]).then_inc(S("consts"), 16)
            sp.dma_start(INVK, I["inv_k"]).then_inc(S("consts"), 16)
            sp.dma_start(RB, broadcast(I["b_router"], P)).then_inc(S("consts"), 16)
            sp.dma_start(GB, broadcast(I["b_gate"], P)).then_inc(S("consts"), 16)
            sp.dma_start(flat(LT), I["before"]).then_inc(S("consts"), 16)
            sp.wait_ge(S("lora_zero_a"), 1)
            sp.wait_ge(S("lora_zero_b"), 1)
            for g in range(4):
                for name, row, dst in lora_loads:
                    sp.dma_start(dst(32 * g + row), I[name]).then_inc(S("lora_in"), 16)
            for n in range(2, N_HU - 1):
                load_half_unit(n)
            sp.wait_ge(S("h_low"), OC * HF)
            for h in range(2):
                sp.dma_start(X[:, 4 * h:4 * h + 4, :], I["x"][:, 4 * h:4 * h + 4, :]).then_inc(S(f"x_again{h}"), 16)
            load_half_unit(N_HU - 1)

            def load_piece(i):
                name, src, n, _ = pieces[i]
                if i < 2:
                    sp.wait_ge(S("w_low"), N_HU - 4)
                else:
                    sp.wait_ge(S("piece"), i - 1)
                sp.dma_start(STAGE[:, i % 2, 0:n], src).then_inc(S(f"stage{i % 2}"), 16)

            for i in range(NW):
                load_piece(i)

            with nc.allow_non_contiguous_dma(reason="rows of 1 KiB"):
                sp.wait_ge(S("qx_zero"), 2)
                sp.wait_ge(S("v1_zero"), 1)
                for b in range(HF):
                    sp.dma_start(QX[b][0:16], I["alibi_q"]).then_inc(S("qx_const"), 16)
                sp.dma_start(KX[0:16], I["alibi_k"]).then_inc(S("qx_const"), 16)
                for b in range(HF):
                    ring_p.wait_read(sp, ("k", b))
                    for half in range(2):
                        sp.dma_start(k_dram[half][:, 512 * b:512 * b + 512],
                                     K16[half][0:16, 512 * b:512 * b + 512]).then_inc(S("k_out"), 16)
                sp.wait_ge(S("k_out"), 64)
                for row, half in ((16, 0), (32, 0), (48, 1), (64, 1)):
                    sp.dma_start(KX[row:row + 16], k_dram[half]).then_inc(S("kx"), 16)
                for b in range(HF):
                    for j in range(KC):
                        ring_p.wait_read(sp, ("q", j, b))
                        for half in range(2):
                            sp.dma_start(q_dram[half][P * j:P * j + P, 512 * b:512 * b + 512],
                                         Q16[half][:, j, 512 * b:512 * b + 512]).then_inc(S(f"q_out{b}"), 16)
                    sp.wait_ge(S(f"q_out{b}"), 16 * 2 * KC)
                    for j in range(KC):
                        for row, half in ((16, 1), (32, 0), (48, 0), (64, 1)):
                            src = q_dram[half][P * j:P * j + P, 512 * b:512 * b + 512].rearrange("(h d) t -> d h t", d=HD)
                            sp.dma_start(QX[b][row:row + 16, 8 * j:8 * j + 8, :], src).then_inc(S(f"qx{b}"), 16)
                for tt in range(TT):
                    b, qt = tt // 4, tt % 4
                    ring_max.wait_read(sp, (tt, "t"))
                    sp.dma_start(m_dram[:, P * tt:P * tt + P], MROW[0:HEADS, P * tt:P * tt + P]).then_inc(S("m_out"), 16)
                    sp.wait_ge(S("m_out"), 16 * (tt + 1))
                    sp.dma_start(QX[b][6:7, :, P * qt:P * qt + P],
                                 m_dram[:, P * tt:P * tt + P].rearrange("(a h) t -> a h t", a=1)).then_inc(S(f"m_in{b}"), 16)
            ring_pv.wait_full(sp, ("pv", HF - 1, 7))
            for e in range(NE):
                i = NW + e
                name, src, n, _ = pieces[i]
                if e >= 2:
                    sp.wait_ge(S("piece"), i - 1)
                sp.dma_start(STAGE[:, i % 2, 0:n], src).then_inc(S(f"stage{i % 2}"), 16)
            for tt in range(TT):
                sp.wait_ge(S("Dx_new"), tt + 1)
                sp.dma_start(out[:, tt, :], X[:, tt, :]).then_inc(S("out"), 16)
            sp.wait_ge(S("out"), 16 * TT)

        @block.gpsimd
        def _(pool):
            nc.gpsimd.memset(L32[:, 0:LA_N], 0.0).then_inc(S("lora_zero_a"), 1)

            def scaled(n):
                pool.wait_ge(S("table"), n + 1)
                pool.wait_ge(S(f"scales{n % 2}"), 16 * n_scale_dmas(n))
                v = PB[:, n % 4, :].rearrange("p (k o) -> p k o", k=2)
                dst = MSUM[:, 2 * n:2 * n + 2, :] if n < 2 else v
                sc = SC[:, n % 2, :]
                s = sc.rearrange("p (k o) -> p k o", k=2) if n >= N_ATTN + N_GU else \
                    sc[:, 0:512].rearrange("p (a o) -> p a o", a=1).to_broadcast([P, 2, 512])
                nc.gpsimd.tensor_tensor(dst, v, s, ALU.mult).then_inc(S("scaled"), 1)

            def low(n):
                pool.wait_ge(S("w_high"), n - 3)
                nc.gpsimd.tensor_tensor(hu_weight(n, 1), PB[:, n % 4, :].rearrange("p (k o) -> p k o", k=2),
                                        hu_weight(n, 0), ALU.subtract).then_inc(S("w_low"), 1)

            for n in range(N_HU + 2):
                if n < N_HU:
                    scaled(n)
                if n - 2 >= 4:
                    low(n - 2)
                if n == 2:
                    nc.gpsimd.memset(IDB, 0.0).then_inc(S("cst"), 1)
                    nc.gpsimd.memset(MASKQ, 0.0).then_inc(S("cst"), 1)
                    nc.gpsimd.memset(MASKK, 0.0).then_inc(S("cst"), 1)
                    pool.wait_ge(S("cst"), 3)
                    nc.gpsimd.affine_select(out=IDB, in_=IDB, compare_op=ALU.not_equal, fill=1.0, base=0,
                                            pattern=[[-1, P]], channel_multiplier=1).then_inc(S("masks"), 1)
                    nc.gpsimd.affine_select(out=MASKQ, in_=MASKQ, compare_op=ALU.is_ge, fill=NEG, base=0,
                                            pattern=[[-1, P]], channel_multiplier=1).then_inc(S("masks"), 1)
                    nc.gpsimd.affine_select(out=MASKK, in_=MASKK, compare_op=ALU.is_ge, fill=NEG, base=0,
                                            pattern=[[1, P]], channel_multiplier=-1).then_inc(S("masks"), 1)
            ring_d.wait_full(pool, TT - 1)
            for b in range(HF):
                nc.gpsimd.memset(at(32 * K + 32 * K * b, 8192)[64:128, :], 0.0).then_inc(S("qx_zero"), 1)
            nc.gpsimd.memset(at(201 * K, 512)[64:128, :], 0.0).then_inc(S("v1_zero"), 1)

        @block.scalar
        def _(act):
            def ln_out(s, tt, src, eps, out_tile, sig):
                act.wait_ge(S(s + "y_stat"), 4 * tt + 2)
                nc.scalar.activation(SD[s, "y"][:, tt % 2, :], MV[s, "y"][:, tt % 2, 1:2], ACT.Sqrt, bias=eps).then_inc(S(s + "y_sd"), 1)
                act.wait_ge(S(s + "y_stat"), 4 * tt + 4)
                if tt >= 2:
                    act.wait_ge(S(s + "x_new"), tt - 1)
                nc.scalar.activation(out_tile, src, ACT.Identity, bias=NM[s, "y"][:, tt % 2, :],
                                     scale=RS[s, "y"][:, tt % 2, :]).then_inc(sig, 1)

            def ln_in_sd(s, tt):
                act.wait_ge(S(s + "x_stat"), 4 * tt + 2)
                nc.scalar.activation(SD[s, "x"][:, tt % 2, :], MV[s, "x"][:, tt % 2, 1:2], ACT.Sqrt, bias=EPS).then_inc(S(s + "x_sd"), 1)

            def ln_in(s, tt, xn, ring, key):
                act.wait_ge(S(s + "x_stat"), 4 * tt + 4)
                if tt >= 2:
                    ring.wait_full(act, key(tt - 2))
                nc.scalar.activation(xn[:, tt % 2, :], X[:, tt, :], ACT.Identity, bias=NM[s, "x"][:, tt % 2, :],
                                     scale=RS[s, "x"][:, tt % 2, :]).then_inc(S(s + "xn"), 1)

            def high(dst, src, scale, sig):
                nc.scalar.activation(dst, src, ACT.Copy, scale=scale).then_inc(sig, 1)

            def t_high(s, tt, ring, key):
                ring.wait_full(act, key)
                high(XT[0][:, :, P * tt:P * tt + P], ring.at(key).rearrange("p (k t) -> p k t", k=KC), 1.0, S(s + "t_high"))

            def lines(n):
                act.wait_ge(S(f"codes{n % 2}"), 16 * (n // 2 + 1))
                if n >= 4 + 4:
                    act.wait_ge(S("w_low"), n - 7)
                elif n >= 4:
                    act.wait_ge(S("scaled"), n - 3)
                    if n >= 6:
                        act.wait_ge(S("sum"), n - 5)
                for i in range(8):
                    sgn, q = i % 2, i // 2
                    slope, offset = (MINUS if sgn else POS)[q]
                    k = 6 * n + i - 2
                    dst = PB[:, n % 4, :] if i == 0 else NB[:, n % 2, :] if i == 1 else LN_[:, k % 3, :]
                    if i >= 2 and k >= 3:
                        act.wait_ge(S("fold"), k - 2)
                    if i == 1 and n >= 2:
                        act.wait_ge(S("table"), n - 1)
                    nc.scalar.activation(dst, CODES[:, n % 2, :], ACT.Relu if q == 0 else ACT.Identity,
                                         bias=WSCALE * offset, scale=WSCALE * slope).then_inc(S("line"), 1)

            def w_high(n):
                ring_lora.wait_read(act, n)
                unit = (n - N_ATTN) // 2
                if n == 4:
                    act.wait_ge(S("lora_low"), 3)
                if unit == 3:
                    ring_main.wait_full(act, ("o", KC - 1, HF - 1))
                if unit == 6:
                    ring_main.wait_full(act, ("u", 7, HF - 1))
                if n == N_ATTN + N_GU:
                    act.wait_ge(S("sum"), 4)
                high(hu_weight(n, 0), PB[:, n % 4, :].rearrange("p (k o) -> p k o", k=2), 1.0, S("w_high"))

            for tt in range(TT + 2):
                if tt < TT:
                    ln_in_sd("A", tt)
                    ln_in("A", tt, XN_A, ring_main, lambda t: ("T", t))
                if tt >= 2:
                    t_high("A", tt - 2, ring_main, ("T", tt - 2))
            for n in range(STEPS_A):
                if n < N_HU:
                    lines(n)
                if n == 1:
                    act.wait_ge(S("lora_in"), 16 * 4 * len(lora_loads))
                    high(L16, L32, 1.0, S("lora_high"))
                if 4 <= n - 2 < N_HU:
                    w_high(n - 2)
                for kind, j, hf in taken_at.get(n, []):
                    key = (kind, j, hf)
                    tokens = slice(512 * hf, 512 * hf + 512)
                    ring_main.wait_full(act, key)
                    if kind == "m":
                        high(M16[0][:, j, tokens], ring_main.at(key), 1 / (3 * WSCALE), S("m_high"))
                    elif kind == "o":
                        high(X1T[0][:, j, tokens], ring_main.at(key), 1 / WSCALE, S("x1_high"))
                    else:
                        i = j * HF + hf
                        if i >= 2:
                            ring_main.wait_read(act, ("u", (i - 2) // HF, (i - 2) % HF))
                        nc.scalar.activation(SG[:, i % 2, :], ring_main.at(key), ACT.Silu,
                                             scale=1 / WSCALE).then_inc(ring_main.free(key), 1)
                        ring_main.wait_read(act, ("u", j, hf))
                        high(H16[0][:, j, tokens], HFULL[:, i % 2, :], 1.0, S("h_high"))

            def piece_high(i):
                name, src, n, dst = pieces[i]
                act.wait_ge(S(f"stage{i % 2}"), 16 * (i // 2 + 1))
                d = flat(dst[0]) if isinstance(dst, list) else dst
                high(d, STAGE[:, i % 2, 0:n], WSCALE, S("piece_high"))

            for i in range(NW):
                piece_high(i)

            for s in range(STEPS_B):
                if 0 <= s - 4 < TT:
                    t = s - 4
                    ring_s.wait_full(act, ("H", t))
                    high(HWT[:, t % 2, 0:P], ring_s.at(("H", t))[:, 0:P], 1.0, S("hw_high"))
                if 0 <= s - 6 < TT:
                    t_high("C", s - 6, ring_s, ("TC", s - 6))
                if 0 <= s - 2 < TT:
                    t_high("B", s - 2, ring_s, ("TB", s - 2))
                t = s - 1
                if 0 <= t < TT:
                    ring_d.wait_full(act, t)
                    ln_out("A", t, ring_d.at(t), EPS * WSCALE ** 2, YN[:, t % 2, :], ring_d.free(t))
                    ln_in_sd("B", t)
                    ln_in("B", t, XN_B, ring_s, lambda i: ("TB", i))
                t = s - 5
                if 0 <= t < TT:
                    ring_b.wait_full(act, t)
                    ln_out("B", t, ring_b.at(t), EPS * WSCALE ** 2, YN_B[:, t % 2, :], ring_b.free(t))
                    ln_in_sd("C", t)
                    ln_in("C", t, XN_C, ring_s, lambda i: ("TC", i))
                if 0 <= s - 2 < TT:
                    t = s - 2
                    ring_s.wait_full(act, ("r", t))
                    if t >= 2:
                        act.wait_ge(S("hw"), t - 1)
                    nc.scalar.activation(RSB[:, t % 2, :], ring_s.at(("r", t))[:, 0:RN], ACT.Copy,
                                         scale=1 / WSCALE).then_inc(ring_s.free(("r", t)), 1)

            for b in range(HF):
                ring_p.wait_full(act, ("k", b))
                high(K16[0][:, 512 * b:512 * b + 512], ring_p.at(("k", b)), HD ** -0.5 / WSCALE, S("k_high"))
            for tt in range(TT):
                ring_p.wait_full(act, ("v", tt))
                if tt == 0:
                    act.wait_ge(S("v1_ones"), 2)
                nc.scalar.activation(V1[:, tt, 0:HD], ring_p.at(("v", tt))[:, 0:HD], ACT.Copy,
                                     scale=1 / WSCALE).then_inc(ring_p.free(("v", tt)), 1)
            for b in range(HF):
                for j in range(KC):
                    ring_p.wait_full(act, ("q", j, b))
                    high(Q16[0][:, j, 512 * b:512 * b + 512], ring_p.at(("q", j, b)), 1 / WSCALE, S("q_high"))

            def minus_max(tt):
                ring_max.wait_full(act, (tt, "t"))
                nc.scalar.activation(MROW[0:HEADS, P * tt:P * tt + P], ring_max.at((tt, "t"))[0:HEADS, 0:P],
                                     ACT.Copy, scale=-1.0).then_inc(ring_max.free((tt, "t")), 1)

            def probs(b, hg, j):
                i = (b * 8 + hg) * 4 + j
                w = 512 - P * j
                if i >= 2:
                    pb, phg, pj = (i - 2) // 32, (i - 2) // 4 % 8, (i - 2) % 4
                    if pj == 3:
                        ring_pv.wait_full(act, ("pv", pb, phg))
                    else:
                        act.wait_ge(S("pv_done"), 3 * (pb * 8 + phg) + pj + 1)
                for hp in range(2):
                    ring_sc.wait_full(act, (b, hg, j, hp))
                    nc.scalar.activation(PT4[:, i % 2, 2 * hp:2 * hp + 2, 0:w], ring_sc.at((b, hg, j, hp))[:, :, 0:w],
                                         ACT.Exp).then_inc(ring_sc.free((b, hg, j, hp)), 1)

            for tt in range(4):
                minus_max(tt)
            for b in range(HF):
                for hg in range(8):
                    for j in range(4):
                        probs(b, hg, j)
                    if b == 0 and hg % 2 == 1:
                        minus_max(4 + hg // 2)

            def a_high(tt):
                ring_tail.wait_full(act, ("aT", tt))
                high(XT[0][:, :, P * tt:P * tt + P], ring_tail.at(("aT", tt)).rearrange("p (k t) -> p k t", k=KC), 1.0, S("a_high"))

            for s in range(STEPS_D):
                if s < TT:
                    a_high(s)
                if 0 <= s - 3 < TT:
                    t_high("D", s - 3, ring_tail, ("TD", s - 3))
                t = s - 2
                if 0 <= t < TT:
                    ring_tail.wait_full(act, ("w", t))
                    ln_out("C", t, ring_tail.at(("w", t)), EPS * WSCALE ** 2, YN[:, t % 2, :], ring_tail.free(("w", t)))
                    ln_in_sd("D", t)
                    ln_in("D", t, XN_B, ring_tail, lambda i: ("TD", i))

            def last_ln(tt):
                act.wait_ge(S("Dy_stat"), 4 * tt + 2)
                nc.scalar.activation(SD["D", "y"][:, tt % 2, :], MV["D", "y"][:, tt % 2, 1:2], ACT.Sqrt, bias=EPS).then_inc(S("Dy_sd"), 1)
                act.wait_ge(S("Dy_stat"), 4 * tt + 4)
                if tt >= 2:
                    act.wait_ge(S("Dx_new"), tt - 1)
                nc.scalar.activation(YN[:, tt % 2, :], YACC[:, tt, :], ACT.Identity, bias=NM["D", "y"][:, tt % 2, :],
                                     scale=RS["D", "y"][:, tt % 2, :]).then_inc(S("Dyn"), 1)

            piece_high(NW)
            for e in range(NE):
                for tt in range(TT):
                    i = (e - 1) * TT + tt
                    if tt == 2 and e + 1 < NE:
                        if e >= 1:
                            ring_tail.wait_full(act, ("e", e - 1, TT - 1))
                        piece_high(NW + e + 1)
                    ring_tail.wait_full(act, ("e", e, tt))
                    if e == 0:
                        act.wait_ge(S("gates"), tt + 1)
                    if e >= 1 and i >= 2:
                        act.wait_ge(S("acc"), i - 1)
                    nc.scalar.activation(YACC[:, tt, :] if e == 0 else YE[:, i % 2, :], ring_tail.at(("e", e, tt)),
                                         ACT.Relu, scale=GS[:, tt, e:e + 1]).then_inc(ring_tail.free(("e", e, tt)), 1)
                    if e == NE - 1 and tt:
                        last_ln(tt - 1)
            last_ln(TT - 1)

        @block.vector
        def _(dve):
            V = nc.vector

            def stats(s, w, tt, src):
                i = tt % 2
                done = S(s + w + "_stat")
                V.bn_stats(STAT[s, w][:, i, :], src).then_inc(done, 1)
                dve.wait_ge(done, 4 * tt + 1)
                V.bn_aggr(MV[s, w][:, i, :], STAT[s, w][:, i, :]).then_inc(done, 1)
                dve.wait_ge(S(s + w + "_sd"), tt + 1)
                V.reciprocal(RS[s, w][:, i, :], SD[s, w][:, i, :]).then_inc(done, 1)
                dve.wait_ge(done, 4 * tt + 3)
                V.scalar_tensor_tensor(out=NM[s, w][:, i, :], in0=MV[s, w][:, i, 0:1], scalar=-1.0, in1=RS[s, w][:, i, :],
                                       op0=ALU.mult, op1=ALU.mult).then_inc(done, 1)

            def add_residual(s, tt, yn):
                V.tensor_tensor(X[:, tt, :], X[:, tt, :], yn[:, tt % 2, :], ALU.add).then_inc(S(s + "x_new"), 1)
                dve.wait_ge(S(s + "x_new"), tt + 1)

            def low(dst, src, scale, hi, sig):
                V.scalar_tensor_tensor(out=dst, in0=src, scalar=scale, in1=hi, op0=ALU.mult,
                                       op1=ALU.subtract).then_inc(sig, 1)

            def t_low(s, tt, ring, key):
                cols_ = slice(P * tt, P * tt + P)
                dve.wait_ge(S(s + "t_high"), tt + 1)
                low(XT[1][:, :, cols_], ring.at(key).rearrange("p (k t) -> p k t", k=KC), 1.0,
                    XT[0][:, :, cols_], ring.free(key))

            V.memset(L32[:, LA_N:LA_N + LB_N], 0.0).then_inc(S("lora_zero_b"), 1)
            V.memset(CUM, 0.0).then_inc(S("cum_zero"), 1)
            for tt in range(TT + 2):
                if tt < TT:
                    if tt % 4 == 0:
                        dve.wait_ge(S(f"x_in{tt // 4}"), 16)
                    stats("A", "x", tt, X[:, tt, :])
                if tt >= 2:
                    t_low("A", tt - 2, ring_main, ("T", tt - 2))

            def fold(n):
                for i in range(2, 8):
                    k = 6 * n + i - 2
                    acc = NB[:, n % 2, :] if i % 2 else PB[:, n % 4, :]
                    dve.wait_ge(S("line"), 8 * n + i + 1)
                    if i >= 4:
                        dve.wait_ge(S("fold"), k - 1)
                    V.tensor_tensor(acc, acc, LN_[:, k % 3, :], ALU.max).then_inc(S("fold"), 1)
                dve.wait_ge(S("fold"), 6 * n + 6)
                V.tensor_tensor(PB[:, n % 4, :], PB[:, n % 4, :], NB[:, n % 2, :], ALU.subtract).then_inc(S("table"), 1)

            def add_lora(n):
                v = PB[:, n % 4, :].rearrange("p (k o) -> p k o", k=2)
                m = MSUM[:, 2 * (n % 2):2 * (n % 2) + 2, :]
                dve.wait_ge(S("scaled"), n + 1)
                if n in (2, 3):
                    V.tensor_tensor(m, m, v, ALU.add).then_inc(S("sum"), 1)
                    return
                if n in (4, 5):
                    dve.wait_ge(S("sum"), n - 3)
                    V.tensor_tensor(v, v, m, ALU.add).then_inc(S("sum"), 1)
                    dve.wait_ge(S("sum"), n - 1)
                ring_lora.wait_full(dve, n)
                V.scalar_tensor_tensor(out=v, in0=ring_lora.at(n), scalar=WSCALE, in1=v, op0=ALU.mult,
                                       op1=ALU.add).then_inc(ring_lora.free(n), 1)

            for n in range(STEPS_A):
                if n < N_HU:
                    fold(n)
                if 2 <= n - 1 < N_HU:
                    add_lora(n - 1)
                if n == 2:
                    dve.wait_ge(S("lora_high"), 1)
                    for p0, n_p, c0, c1 in ((32, 32, 0, LA_N), (96, 32, 0, LA_N), (64, 64, LA_N, LA_N + LB_N)):
                        v16, v32 = L16[p0:p0 + n_p, c0:c1], L32[p0:p0 + n_p, c0:c1]
                        V.tensor_tensor(v16, v32, v16, ALU.subtract).then_inc(S("lora_low"), 1)
                for kind, j, hf in taken_at.get(n, []):
                    key = (kind, j, hf)
                    tokens = slice(512 * hf, 512 * hf + 512)
                    i = j * HF + hf
                    if kind == "m":
                        dve.wait_ge(S("m_high"), i + 1)
                        low(M16[1][:, j, tokens], ring_main.at(key), 1 / (3 * WSCALE), M16[0][:, j, tokens], ring_main.free(key))
                    elif kind == "o":
                        dve.wait_ge(S("x1_high"), i + 1)
                        low(X1T[1][:, j, tokens], ring_main.at(key), 1 / WSCALE, X1T[0][:, j, tokens], ring_main.free(key))
                    else:
                        u = ("u", j, hf)
                        ring_main.wait_read(dve, key)
                        ring_main.wait_full(dve, u)
                        if i >= 2:
                            dve.wait_ge(S("h_low"), i - 1)
                        V.scalar_tensor_tensor(out=HFULL[:, i % 2, :], in0=ring_main.at(u), scalar=1 / WSCALE,
                                               in1=SG[:, i % 2, :], op0=ALU.mult, op1=ALU.mult).then_inc(ring_main.free(u), 1)
                        dve.wait_ge(S("h_high"), i + 1)
                        V.tensor_tensor(H16[1][:, j, tokens], HFULL[:, i % 2, :], H16[0][:, j, tokens],
                                        ALU.subtract).then_inc(S("h_low"), 1)

            def piece_low(i):
                name, src, n, dst = pieces[i]
                dve.wait_ge(S("piece_high"), i + 1)
                if isinstance(dst, list):
                    low(flat(dst[1]), STAGE[:, i % 2, 0:n], WSCALE, flat(dst[0]), S("piece"))
                else:
                    low(dst[32:64, :], STAGE[32:64, i % 2, 0:n], WSCALE, dst[32:64, :], S("piece"))

            for i in range(NW):
                piece_low(i)

            def sparsemax(t):
                z, zs, f, tau, w = (ZB[:, i, :] for i in range(5))
                count = [8 * t]

                def done(ins):
                    count[0] += 1
                    ins.then_inc(S("sparse"), 1)
                    dve.wait_ge(S("sparse"), count[0])

                ring_s.wait_read(dve, ("r", t))
                r = RSB[:, t % 2, :]
                if t == 0:
                    dve.wait_ge(S("cum_zero"), 1)
                    dve.wait_ge(S("consts"), 16 * 6)
                done(V.tensor_tensor(z, r[:, 0:NE], RB, ALU.add))
                done(V.max(CUM[:, 0, 4:4 + NE], z))
                done(V.tensor_tensor(CUM[:, 1, 4:4 + NE], CUM[:, 0, 4:4 + NE], CUM[:, 0, 3:3 + NE], ALU.add))
                done(V.tensor_tensor(CUM[:, 2, 4:4 + NE], CUM[:, 1, 4:4 + NE], CUM[:, 1, 2:2 + NE], ALU.add))
                done(V.tensor_tensor(zs, CUM[:, 2, 4:4 + NE], CUM[:, 2, 0:NE], ALU.add))
                done(V.scalar_tensor_tensor(out=f, in0=zs, scalar=-1.0, in1=INVK, op0=ALU.add, op1=ALU.mult))
                done(V.tensor_reduce(tau[:, 0:1], f, AX_X, ALU.max))
                done(V.tensor_scalar(w, z, tau[:, 0:1], 0.0, ALU.subtract, ALU.max))
                if t >= 2:
                    ring_s.wait_full(dve, ("H", t - 2))
                V.tensor_tensor(HWF[:, t % 2, :].rearrange("p (e r) -> p e r", e=NE),
                                r[:, NE:RN].rearrange("p (e r) -> p e r", e=NE),
                                w.rearrange("p (e a) -> p e a", a=1).to_broadcast([P, NE, R]), ALU.mult).then_inc(S("hw"), 1)

            dve.wait_ge(S("x_again0"), 16)
            dve.wait_ge(S("x_again1"), 16)
            for s in range(STEPS_B):
                if 0 <= s - 4 < TT:
                    t = s - 4
                    dve.wait_ge(S("hw_high"), t + 1)
                    low(HWT[:, t % 2, P:2 * P], ring_s.at(("H", t))[:, 0:P], 1.0, HWT[:, t % 2, 0:P], ring_s.free(("H", t)))
                if 0 <= s - 3 < TT:
                    sparsemax(s - 3)
                if 0 <= s - 6 < TT:
                    t_low("C", s - 6, ring_s, ("TC", s - 6))
                if 0 <= s - 2 < TT:
                    t_low("B", s - 2, ring_s, ("TB", s - 2))
                t = s - 1
                if 0 <= t < TT:
                    ring_d.wait_full(dve, t)
                    stats("A", "y", t, ring_d.at(t))
                    ring_d.wait_read(dve, t)
                    add_residual("A", t, YN)
                    stats("B", "x", t, X[:, t, :])
                t = s - 5
                if 0 <= t < TT:
                    ring_b.wait_full(dve, t)
                    stats("B", "y", t, ring_b.at(t))
                    ring_b.wait_read(dve, t)
                    add_residual("B", t, YN_B)
                    stats("C", "x", t, X[:, t, :])

            for b in range(HF):
                cols_ = slice(512 * b, 512 * b + 512)
                dve.wait_ge(S("k_high"), b + 1)
                low(K16[1][:, cols_], ring_p.at(("k", b)), HD ** -0.5 / WSCALE, K16[0][:, cols_], ring_p.free(("k", b)))
            V.memset(V1[:, :, HD:HD + 1], 1.0).then_inc(S("v1_ones"), 1)
            V.memset(V1[:, :, HD + 1:32], 0.0).then_inc(S("v1_ones"), 1)
            for b in range(HF):
                cols_ = slice(512 * b, 512 * b + 512)
                for j in range(KC):
                    dve.wait_ge(S("q_high"), KC * b + j + 1)
                    low(Q16[1][:, j, cols_], ring_p.at(("q", j, b)), 1 / WSCALE, Q16[0][:, j, cols_], ring_p.free(("q", j, b)))

            def row_max(tt, h):
                ring_max.wait_full(dve, (tt, h))
                V.tensor_reduce(MX[:, tt, h:h + 1], ring_max.at((tt, h))[:, 0:P * (tt % 4 + 1)], AX_X,
                                ALU.max).then_inc(ring_max.free((tt, h)), 1)

            def sums(b, hg):
                i = b * 8 + hg
                ring_pv.wait_full(dve, ("pv", b, hg))
                if i >= 2:
                    ring_pv.wait_full(dve, ("pt", *groups[i - 2]))
                V.tensor_copy(OT[:, i % 2, :], ring_pv.at(("pv", b, hg))).then_inc(ring_pv.free(("pv", b, hg)), 1)

            def divide(b, hg):
                i = b * 8 + hg
                ring_pv.wait_full(dve, ("pt", b, hg))
                pt = ring_pv.at(("pt", b, hg)).rearrange("p (g d) -> p g d", d=32)
                V.reciprocal(RDEN[:, i % 2, :].rearrange("p (g a) -> p g a", a=1), pt[:, :, HD:HD + 1]).then_inc(S("rden"), 1)
                dve.wait_ge(S("rden"), i + 1)
                for qt in range(4):
                    o_ = ATTN[:, 4 * b + qt, 64 * hg:64 * hg + 64].rearrange("p (h d) -> p h d", d=HD)
                    ins = V.tensor_tensor(o_, pt[:, 4 * qt:4 * qt + 4, 0:HD],
                                          RDEN[:, i % 2, 4 * qt:4 * qt + 4].rearrange("p (g a) -> p g a", a=1)
                                          .to_broadcast([P, 4, HD]), ALU.mult)
                    ins.then_inc(ring_pv.free(("pt", b, hg)) if qt == 3 else S("divided"), 1)

            for tt in range(4):
                for h in range(HEADS):
                    row_max(tt, h)
            for b in range(HF):
                for hg in range(8):
                    i = b * 8 + hg
                    for q in range(16 if b == 0 else 0):
                        m = 16 * hg + q
                        row_max(4 + m // HEADS, m % HEADS)
                        if q == 3 and i >= 1:
                            sums(*groups[i - 1])
                    if b:
                        sums(*groups[i - 1])
                    if i >= 2:
                        divide(*groups[i - 2])
            sums(*groups[-1])
            divide(*groups[-2])
            divide(*groups[-1])

            def gate(tt):
                count = [6 * tt]

                def done(ins):
                    count[0] += 1
                    ins.then_inc(S("rank"), 1)
                    dve.wait_ge(S("rank"), count[0])

                z, rank = ZB[:, 5, :], ZB[:, 0, :]
                a, b_ = (CMP[:, i, :].rearrange("p (e j) -> p e j", e=NE) for i in range(2))
                zj = z.rearrange("p (a j) -> p a j", a=1).to_broadcast([P, NE, NE])
                ze = z.rearrange("p (e a) -> p e a", a=1).to_broadcast([P, NE, NE])
                ring_tail.wait_full(dve, ("z", tt))
                V.scalar_tensor_tensor(out=z, in0=ring_tail.at(("z", tt))[:, 0:NE], scalar=1 / WSCALE, in1=GB,
                                       op0=ALU.mult, op1=ALU.add).then_inc(ring_tail.free(("z", tt)), 1)
                ring_tail.wait_read(dve, ("z", tt))
                done(V.tensor_tensor(a, zj, ze, ALU.is_gt))
                done(V.tensor_tensor(b_, zj, ze, ALU.is_equal))
                done(V.tensor_tensor(b_, b_, LT, ALU.mult))
                done(V.tensor_tensor(a, a, b_, ALU.add))
                done(V.tensor_reduce(rank, a, AX_X, ALU.add))
                done(V.tensor_scalar(GS[:, tt, :], rank, 1.5, 0.5 / WSCALE, ALU.is_lt, ALU.mult))
                V.tensor_copy(rank, GS[:, tt, :]).then_inc(S("gates"), 1)

            for s in range(STEPS_D):
                if s < TT:
                    cols_ = slice(P * s, P * s + P)
                    dve.wait_ge(S("a_high"), s + 1)
                    low(XT[1][:, :, cols_], ring_tail.at(("aT", s)).rearrange("p (k t) -> p k t", k=KC), 1.0,
                        XT[0][:, :, cols_], ring_tail.free(("aT", s)))
                if 0 <= s - 3 < TT:
                    t_low("D", s - 3, ring_tail, ("TD", s - 3))
                t = s - 2
                if 0 <= t < TT:
                    ring_tail.wait_full(dve, ("w", t))
                    stats("C", "y", t, ring_tail.at(("w", t)))
                    ring_tail.wait_read(dve, ("w", t))
                    add_residual("C", t, YN)
                    stats("D", "x", t, X[:, t, :])
                if 0 <= s - 3 < TT:
                    gate(s - 3)

            def last(tt):
                dve.wait_ge(S("acc"), TT * (NE - 2) + tt + 1)
                stats("D", "y", tt, YACC[:, tt, :])
                dve.wait_ge(S("Dyn"), tt + 1)
                add_residual("D", tt, YN)

            piece_low(NW)
            for e in range(NE):
                for tt in range(TT):
                    if tt == 2 and e + 1 < NE:
                        piece_low(NW + e + 1)
                    if e:
                        i = (e - 1) * TT + tt
                        ring_tail.wait_read(dve, ("e", e, tt))
                        if e == 1:
                            ring_tail.wait_read(dve, ("e", 0, tt))
                        else:
                            dve.wait_ge(S("acc"), i - TT + 1)
                        V.tensor_tensor(YACC[:, tt, :], YACC[:, tt, :], YE[:, i % 2, :], ALU.add).then_inc(S("acc"), 1)
                    if e == NE - 1 and tt:
                        last(tt - 1)
            last(TT - 1)

        @block.tensor
        def _(pe):
            mm = nc.tensor.matmul

            def transposes(ring, key, src):
                ring.wait_free(pe, key)
                for k in range(KC):
                    ins = nc.tensor.transpose(ring.at(key)[:, P * k:P * k + P], src[:, P * k:P * k + P], IDF)
                ins.then_inc(ring.full(key), 1)

            def product(dst, lhs, rhs, more=()):
                pairs = [(l[a], r[b]) for l, r in zip(lhs, rhs) for a, b in ((0, 0), (0, 1), (1, 0))]
                pairs += list(more)
                for i, (l, r) in enumerate(pairs):
                    ins = mm(dst, l, r, start=(i == 0), stop=(i == len(pairs) - 1))
                return ins

            def halves(w, k, c):
                return w[0][:, k, c], w[1][:, k, c]

            pe.wait_ge(S("ident_in"), 16)
            for tt in range(TT):
                pe.wait_ge(S("Axn"), tt + 1)
                transposes(ring_main, ("T", tt), XN_A[:, tt % 2, :])

            def lora(n):
                ring_lora.wait_free(pe, n)
                if n == 4:
                    pe.wait_ge(S("lora_low"), 3)
                for i in range(2):
                    if n < N_ATTN:
                        m, kh = cols(n)
                        names = ("qk", "v") if m == 2 else ("o",)
                        pairs = [(LA[w] + P * (2 * kh + i), LA_N + LB[w]) for w in names]
                    elif n < N_ATTN + N_GU:
                        c, kh = cols(n - N_ATTN)
                        pairs = [(LA["gu"] + P * (2 * kh + i), LA_N + LB["gu"] + 512 * c)]
                    else:
                        pairs = [(LA["down"] + P * (2 * (n - N_ATTN - N_GU) + i), LA_N + LB["down"])]
                    for q, (a, b) in enumerate(pairs):
                        ins = mm(ring_lora.at(n)[:, i, :], L16[:, a:a + P], L16[:, b:b + 512],
                                 start=(q == 0), stop=(q == len(pairs) - 1))
                ins.then_inc(ring_lora.full(n), 1)

            waited = {"w": 0}

            def weights_ready(n):
                if waited["w"] < n - 3:
                    waited["w"] = n - 3
                    pe.wait_ge(S("w_low"), n - 3)

            for n in range(STEPS_A):
                if 4 <= n < N_HU:
                    lora(n)
                for kind, j, hf in taken_at.get(n, []):
                    tokens = slice(512 * hf, 512 * hf + 512)
                    key = (kind, j, hf)
                    if kind == "m":
                        weights_ready(5)
                        if (j, hf) == (0, 0):
                            ring_main.wait_read(pe, ("T", TT - 2))
                            ring_main.wait_read(pe, ("T", TT - 1))
                        ring_main.wait_free(pe, key)
                        product(ring_main.at(key), [halves(MW, k, slice(P * j, P * j + P)) for k in range(KC)],
                                [halves(XT, k, tokens) for k in range(KC)]).then_inc(ring_main.full(key), 1)
                    elif kind == "o":
                        weights_ready(7)
                        if (j, hf) == (0, 0):
                            for i in range(len(j_hf) - 4, len(j_hf)):
                                ring_main.wait_read(pe, ("m", *j_hf[i]))
                            pe.wait_ge(S("consts"), 16 * 6)
                        ring_main.wait_free(pe, key)
                        product(ring_main.at(key), [halves(OW, k, slice(P * j, P * j + P)) for k in range(KC)],
                                [halves(M16, k, tokens) for k in range(KC)],
                                [(I256, XT[0][:, j, tokens]), (I256, XT[1][:, j, tokens])]).then_inc(ring_main.full(key), 1)
                    else:
                        c = j // 2
                        weights_ready(N_ATTN + 2 * c + 1)
                        if (j, hf) == (0, 0):
                            for i in range(len(j_hf) - 4, len(j_hf)):
                                ring_main.wait_read(pe, ("o", *j_hf[i]))
                        for g, what in enumerate("gu"):
                            w = slice(256 * g + P * (j % 2), 256 * g + P * (j % 2) + P)
                            key = (what, j, hf)
                            ring_main.wait_free(pe, key)
                            product(ring_main.at(key), [halves(GUW[c], k, w) for k in range(KC)],
                                    [halves(X1T, k, tokens) for k in range(KC)]).then_inc(ring_main.full(key), 1)

            ring_main.wait_all_free(pe)
            ring_lora.wait_all_free(pe)
            weights_ready(N_HU - 1)
            pe.wait_ge(S("h_low"), OC * HF)

            for s in range(STEPS_B):
                if 0 <= s - 6 < TT:
                    pe.wait_ge(S("Cxn"), s - 5)
                    transposes(ring_s, ("TC", s - 6), XN_C[:, (s - 6) % 2, :])
                if 0 <= s - 2 < TT:
                    pe.wait_ge(S("Bxn"), s - 1)
                    transposes(ring_s, ("TB", s - 2), XN_B[:, (s - 2) % 2, :])
                if s < TT:
                    tile = slice(P * s, P * s + P)
                    ring_d.wait_free(pe, s)
                    dst = ring_d.at(s)
                    pairs = [(H16[a][:, j, tile], DW[b][:, j, :]) for j in range(OC) for a, b in ((0, 0), (0, 1), (1, 0))]
                    for i, (l, r) in enumerate(pairs[:-1]):
                        mm(dst, l, r, start=(i == 0), stop=False)
                    for k in range(KC):
                        for half in range(2):
                            mm(dst[:, P * k:P * k + P], X1T[half][:, k, tile], I256, start=False, stop=False,
                               skip_group_check=True)
                    mm(dst, *pairs[-1], start=False, stop=True).then_inc(ring_d.full(s), 1)
                t = s - 2
                if 0 <= t < TT:
                    tile = slice(P * t, P * t + P)
                    if t == 0:
                        pe.wait_ge(S("piece"), NW)
                    ring_s.wait_read(pe, ("TB", t))
                    ring_s.wait_free(pe, ("r", t))
                    product(ring_s.at(("r", t))[:, 0:RN], [halves(XT, k, tile) for k in range(KC)],
                            [halves(RW, k, slice(0, RN)) for k in range(KC)]).then_inc(ring_s.full(("r", t)), 1)
                    ring_b.wait_free(pe, t)
                    dst = ring_b.at(t)
                    i = 0
                    for k in range(KC):
                        for a, b in ((0, 0), (0, 1), (1, 0)):
                            mm(dst, XT[a][:, k, tile], BW[b][:, k, :], start=(i == 0), stop=False)
                            i += 1
                    mm(dst, ONES, BB, start=False, stop=False)
                t = s - 3
                if 0 <= t < TT:
                    pe.wait_ge(S("hw"), t + 1)
                    ring_s.wait_free(pe, ("H", t))
                    nc.tensor.transpose(ring_s.at(("H", t))[:, 0:P], HWF[:, t % 2, :], IDF).then_inc(ring_s.full(("H", t)), 1)
                t = s - 4
                if 0 <= t < TT:
                    ring_s.wait_read(pe, ("H", t))
                    dst = ring_b.at(t)
                    hi, lo = HWT[:, t % 2, 0:P], HWT[:, t % 2, P:2 * P]
                    mm(dst, hi, LBW[0], start=False, stop=False)
                    mm(dst, hi, LBW[1], start=False, stop=False)
                    mm(dst, lo, LBW[0], start=False, stop=True).then_inc(ring_b.full(t), 1)

            ring_d.wait_all_free(pe)
            ring_b.wait_all_free(pe)
            ring_s.wait_all_free(pe)
            for b in range(HF):
                key = ("k", b)
                product(ring_p.at(key), [halves(KW, k, slice(0, P)) for k in range(KC)],
                        [halves(XT, k, slice(512 * b, 512 * b + 512)) for k in range(KC)]).then_inc(ring_p.full(key), 1)
            for tt in range(TT):
                key = ("v", tt)
                ring_p.wait_free(pe, key)
                product(ring_p.at(key)[:, 0:HD], [halves(XT, k, slice(P * tt, P * tt + P)) for k in range(KC)],
                        [halves(VW, k, slice(0, HD)) for k in range(KC)]).then_inc(ring_p.full(key), 1)
            for b in range(HF):
                for j in range(KC):
                    key = ("q", j, b)
                    ring_p.wait_free(pe, key)
                    product(ring_p.at(key), [halves(QW, k, slice(P * j, P * j + P)) for k in range(KC)],
                            [halves(XT, k, slice(512 * b, 512 * b + 512)) for k in range(KC)]).then_inc(ring_p.full(key), 1)
            ring_p.wait_all_free(pe)

            def max_scores(tt, h):
                b, qt = tt // 4, tt % 4
                key = (tt, h)
                w = P * (qt + 1)
                ring_max.wait_free(pe, key)
                q = QX[b][:, h, P * qt:P * qt + P]
                mm(ring_max.at(key)[:, 0:w], q, KX[:, 512 * b:512 * b + w], start=True, stop=True)
                mm(ring_max.at(key)[:, w - P:w], IDB, MASKQ, start=False, stop=True,
                   skip_group_check=True).then_inc(ring_max.full(key), 1)

            def max_transpose(tt):
                key = (tt, "t")
                for h in (HEADS - 2, HEADS - 1):
                    ring_max.wait_read(pe, (tt, h))
                ring_max.wait_free(pe, key)
                nc.tensor.transpose(ring_max.at(key)[0:HEADS, 0:P], MX[:, tt, :], IDF).then_inc(ring_max.full(key), 1)

            def score(b, hg, j):
                w = 512 - P * j
                for hp in range(2):
                    key = (b, hg, j, hp)
                    ring_sc.wait_free(pe, key)
                    for i in range(2):
                        h = 4 * hg + 2 * hp + i
                        dst = ring_sc.at(key)[:, i, :]
                        mm(dst[:, 0:w], KX[:, 512 * b + P * j:512 * b + P * j + P], QX[b][:, h, P * j:512], start=True, stop=True)
                        ins = mm(dst[:, 0:P], IDB, MASKK, start=False, stop=True, skip_group_check=True)
                    ins.then_inc(ring_sc.full(key), 1)

            def weigh(b, hg, j):
                i = (b * 8 + hg) * 4 + j
                w = 512 - P * j
                key = ("pv", b, hg)
                if j == 0:
                    ring_pv.wait_free(pe, key)
                for hp in range(2):
                    ring_sc.wait_read(pe, (b, hg, j, hp))
                for h in range(4):
                    ins = mm(ring_pv.at(key)[32 * h:32 * h + 32, P * j:512], V1[:, 4 * b + j, :], PT4[:, i % 2, h, 0:w],
                             start=(j == 0), stop=(j == 3), skip_group_check=True)
                    if h == 3:
                        ins.then_inc(ring_pv.full(key) if j == 3 else S("pv_done"), 1)

            def turn(b, hg):
                key = ("pt", b, hg)
                i = b * 8 + hg
                ring_pv.wait_free(pe, key)
                ring_pv.wait_read(pe, ("pv", b, hg))
                for qt in range(4):
                    ins = nc.tensor.transpose(ring_pv.at(key)[:, P * qt:P * qt + P], OT[:, i % 2, P * qt:P * qt + P], IDF)
                ins.then_inc(ring_pv.full(key), 1)

            pe.wait_ge(S("masks"), 3)
            pe.wait_ge(S("v1_zero"), 1)
            pe.wait_ge(S("kx"), 64)
            pe.wait_ge(S("qx_const"), 48)
            pe.wait_ge(S("qx0"), 16 * 16)
            for tt in range(4):
                for h in range(HEADS):
                    max_scores(tt, h)
                max_transpose(tt)
            pe.wait_ge(S("qx1"), 16 * 16)
            for b in range(HF):
                if b == 0:
                    pe.wait_ge(S("m_in0"), 64)
                else:
                    pe.wait_ge(S("m_in1"), 64)
                for hg in range(8):
                    for j in range(4):
                        if b == 0:
                            for m in range(16 * hg + 4 * j, 16 * hg + 4 * j + 4):
                                max_scores(4 + m // HEADS, m % HEADS)
                        score(b, hg, j)
                        if j:
                            weigh(b, hg, j - 1)
                        elif (b, hg) != (0, 0):
                            weigh(*groups[b * 8 + hg - 1], 3)
                    if b == 0 and hg % 2 == 1:
                        max_transpose(4 + hg // 2)
                    if (b, hg) != (0, 0):
                        turn(*groups[b * 8 + hg - 1])
            weigh(HF - 1, 7, 3)
            turn(HF - 1, 7)

            ring_max.wait_all_free(pe)
            ring_sc.wait_all_free(pe)
            ring_pv.wait_all_free(pe)
            for s in range(STEPS_D):
                if s < TT:
                    transposes(ring_tail, ("aT", s), ATTN[:, s, :])
                if 0 <= s - 3 < TT:
                    t = s - 3
                    pe.wait_ge(S("Dxn"), t + 1)
                    transposes(ring_tail, ("TD", t), XN_B[:, t % 2, :])
                t = s - 1
                if 0 <= t < TT:
                    key = ("w", t)
                    ring_tail.wait_read(pe, ("aT", t))
                    ring_tail.wait_free(pe, key)
                    product(ring_tail.at(key), [halves(XT, k, slice(P * t, P * t + P)) for k in range(KC)],
                            [halves(WOW, k, slice(0, D)) for k in range(KC)]).then_inc(ring_tail.full(key), 1)
                t = s - 3
                if 0 <= t < TT:
                    key = ("z", t)
                    ring_tail.wait_read(pe, ("TD", t))
                    ring_tail.wait_free(pe, key)
                    product(ring_tail.at(key)[:, 0:NE], [halves(XT, k, slice(P * t, P * t + P)) for k in range(KC)],
                            [halves(GW, k, slice(0, NE)) for k in range(KC)]).then_inc(ring_tail.full(key), 1)
            for e in range(NE):
                pe.wait_ge(S("piece"), NW + e + 1)
                for tt in range(TT):
                    key = ("e", e, tt)
                    ring_tail.wait_free(pe, key)
                    product(ring_tail.at(key), [halves(XT, k, slice(P * tt, P * tt + P)) for k in range(KC)],
                            [halves(EW[e % 2], k, slice(0, D)) for k in range(KC)],
                            [(ONES, BE[:, D * e:D * e + D])]).then_inc(ring_tail.full(key), 1)


def broadcast(src, n):
    if len(src.shape) == 1:
        src = src.rearrange("(a o) -> a o", a=1)
    rows, width = src.shape
    return bass.AP(tensor=src.tensor, offset=src.offset, ap=[list(src.ap[0]), [0, n], list(src.ap[1])])


def repeat(src, n):
    return bass.AP(tensor=src.tensor, offset=src.offset, ap=[[0, n], list(src.ap[0]), list(src.ap[1])])


def kernel(**inputs):
    import numpy as np
    import concourse.bacc as bacc
    from concourse.bass_utils import run_bass_kernel_spmd

    a = {k: np.asarray(v) for k, v in inputs.items()}
    perm = (4 * np.arange(P)[None, :] + np.arange(KC)[:, None]).reshape(-1)

    def rows(w):
        return w[perm].reshape(KC, P, -1).transpose(1, 0, 2).reshape(P, -1)

    def plain_rows(w):
        return w.reshape(-1, P, w.shape[-1]).transpose(1, 0, 2).reshape(P, -1)

    def bias_rows(b):
        t = np.zeros((P, b.shape[-1]), np.float32)
        t[0] = t[32] = b
        return t

    x = a["L0_attn_x"].reshape(TT, P, D)[:, :, perm].transpose(1, 0, 2)
    ca = a["L0_attn_codes_attn"]
    cg = a["L0_attn_codes_gu"].reshape(2, OC // 2, 256, D)
    sg = a["L0_attn_scales_gu"].reshape(2, OC // 2, 256, 8)
    cd = a["L0_attn_codes_down"][perm].T
    wr, la = a["L0_ffn_W_router"].T, a["L0_ffn_lora_A"].transpose(1, 0, 2).reshape(D, NE * R)
    wqkv = a["L1_attn_Wqkv"]
    A, B = a["L0_attn_lora_A_h"], a["L0_attn_lora_B_attn"]
    bgu = a["L0_attn_lora_B_gu"].reshape(2, OC // 2, 256, R)
    pos = np.arange(512, dtype=np.float64)
    base = 2.0 ** (-2.0 ** (-(5 - 3)))
    slopes = (base ** np.arange(1, HEADS + 1, dtype=np.float64)).astype(np.float32).astype(np.float64)
    s_hi = slopes.astype(np.float16)
    s_lo = (slopes - s_hi).astype(np.float16)
    alibi_q = np.zeros((16, HEADS, 512), np.float16)
    for i, s in ((0, s_hi), (3, s_lo)):
        s = s.astype(np.float64)[:, None]
        alibi_q[i] = s
        alibi_q[i + 1] = -s * pos
        alibi_q[i + 2] = -s * pos - alibi_q[i + 1].astype(np.float64)
    alibi_k = np.zeros((16, T), np.float16)
    alibi_k[0] = alibi_k[3] = np.tile(pos, HF)
    alibi_k[[1, 2, 4, 5, 6]] = 1.0
    ones_rows = np.zeros((P, P), np.float16)
    ones_rows[[0, 32]] = 1.0

    data = {
        "x": x,
        "codes_attn": np.stack([rows(ca[m][perm].T) for m in range(4)]),
        "scales_attn": np.stack([a["L0_attn_scales_attn"][m][perm].T for m in range(4)]),
        "codes_gu": np.stack([rows(cg[:, c].reshape(512, D).T) for c in range(OC // 2)]),
        "scales_gu": np.stack([sg[:, c].reshape(512, 8).T for c in range(OC // 2)]),
        "codes_down": np.stack([plain_rows(cd[256 * d:256 * d + 256]) for d in range(N_DOWN)]),
        "scales_down": a["L0_attn_scales_down"][perm].T,
        "a_q": A[0][:, perm], "a_k": A[1][:, perm], "a_v": A[2][:, perm], "a_o": A[3][:, perm],
        "a_g": A[4][:, perm], "a_u": A[5][:, perm], "a_down": a["L0_attn_lora_A_down"],
        "b_q": B[0][perm].T, "b_k": B[1][perm].T, "b_v": B[2][perm].T, "b_o": B[3][perm].T,
        "b_g": bgu[0].transpose(2, 0, 1), "b_u": bgu[1].transpose(2, 0, 1),
        "b_down": a["L0_attn_lora_B_down"][perm].T,
        "w_base": rows(a["L0_ffn_W_base"][perm].T), "b_base": bias_rows(a["L0_ffn_b_base"][perm]),
        "w_rl": rows(np.concatenate([wr, la], axis=1)), "b_router": a["L0_ffn_b_router"],
        "lora_b": a["L0_ffn_lora_B"].reshape(NE * R, D)[:, perm],
        "w_q": rows(wqkv[:, :D]), "w_k": rows(np.tile(wqkv[:, D:D + HD], (1, NE))), "w_v": rows(wqkv[:, D + HD:]),
        "w_o": plain_rows(a["L1_attn_Wo"][:, perm]),
        "w_gate": rows(a["L1_ffn_W_gate"]), "b_gate": a["L1_ffn_b_gate"],
        "w_e": np.stack([rows(a["L1_ffn_W_e"][e][:, perm]) for e in range(NE)]),
        "b_e": bias_rows(a["L1_ffn_b_e"][:, perm].reshape(-1)),
        "ident": np.eye(P, dtype=np.float32), "ident256": np.eye(P, dtype=np.float16) * np.float16(WSCALE),
        "ones_rows": ones_rows, "inv_k": np.tile((1.0 / np.arange(1, NE + 1)).astype(np.float32), (P, 1)),
        "before": np.tile(np.tril(np.ones((NE, NE), np.float32), -1).reshape(1, -1), (P, 1)),
        "alibi_q": alibi_q, "alibi_k": alibi_k,
    }
    nc = bacc.Bacc("TRN2", target_bir_lowering=False, num_devices=1)
    arrays, handles = {}, {}
    for name, v in data.items():
        arrays[f"in_{name}"] = np.ascontiguousarray(v)
        handles[name] = nc.dram_tensor(f"in_{name}", arrays[f"in_{name}"].shape, mybir.dt.from_np(v.dtype), kind="ExternalInput").ap()
    out = nc.dram_tensor("out", (P, TT, D), F32, kind="ExternalOutput").ap()
    sandwich(nc, handles, out)
    r = run_bass_kernel_spmd(nc, [arrays], core_ids=[0])
    got = np.asarray(r.results[0]["out"])
    y = np.empty((TT, P, D), np.float32)
    y[:, :, perm] = got.transpose(1, 0, 2)
    return y.reshape(HF, 512, D)
```

```python
from contextlib import ExitStack

import concourse.bass as bass
from concourse import mybir

F32 = mybir.dt.float32
F16 = mybir.dt.float16
BF16 = mybir.dt.bfloat16
I32 = mybir.dt.int32
U32 = mybir.dt.uint32
ALU = mybir.AluOpType
ACT = mybir.ActivationFunctionType
AX_X = mybir.AxisListType.X

P = 128
T = 1024
TT = T // P
D = 512
KC = D // P
HF = T // 512
INTER = 1792
OC = INTER // P
HEADS, HD = 32, 16
NE = 8
R = 16
WSCALE = 256.0
EPS = 1e-5
NEG = -1e30
NF4 = [-1.0, -0.6961928009986877, -0.5250730514526367, -0.39491748809814453, -0.28444138169288635,
       -0.18477343022823334, -0.09105003625154495, 0.0, 0.07958029955625534, 0.16093020141124725,
       0.24611230194568634, 0.33791524171829224, 0.44070982933044434, 0.5626170039176941,
       0.7229568362236023, 1.0]

LA = {"qk": 0, "v": 512, "o": 1024, "gu": 1536, "down": 2048}
LA_N = 2048 + INTER
LB = {"qk": 0, "v": 512, "o": 1024, "gu": 1536, "down": 1536 + 2 * INTER}
LB_N = 2048 + 2 * INTER

N_ATTN, N_GU, N_DOWN = 8, 14, 7
N_HU = N_ATTN + N_GU + N_DOWN


def nf4_line(i, j):
    s = (NF4[j] - NF4[i]) / (j - i)
    return s, NF4[i] - s * i


POS = [nf4_line(8, 9), nf4_line(10, 11), nf4_line(12, 13), nf4_line(14, 15)]
MINUS = [tuple(-a for a in nf4_line(i, i + 1)) for i in (6, 4, 2, 0)]


class Ring:

    def __init__(self, sem, name, slots, keys):
        self.slots = slots
        self.n = len(slots)
        self.index = {k: i for i, k in enumerate(keys)}
        assert len(self.index) == len(keys)
        self.full_sems = [sem(f"{name}_full{s}") for s in range(self.n)]
        self.free_sems = [sem(f"{name}_free{s}") for s in range(self.n)]

    def at(self, key):
        return self.slots[self.index[key] % self.n]

    def full(self, key):
        return self.full_sems[self.index[key] % self.n]

    def free(self, key):
        return self.free_sems[self.index[key] % self.n]

    def wait_free(self, eng, key):
        use = self.index[key] // self.n
        if use:
            eng.wait_ge(self.free(key), use)

    def wait_full(self, eng, key):
        eng.wait_ge(self.full(key), self.index[key] // self.n + 1)

    def wait_read(self, eng, key):
        eng.wait_ge(self.free(key), self.index[key] // self.n + 1)

    def wait_all_free(self, eng):
        total = len(self.index)
        for s in range(self.n):
            uses = (total - s + self.n - 1) // self.n
            if uses:
                eng.wait_ge(self.free_sems[s], uses)


def sandwich(nc, I, out):
    ctx = ExitStack()
    with ctx:
        sems = {}

        def S(name):
            if name not in sems:
                sems[name] = ctx.enter_context(nc.semaphore(name))
            return sems[name]

        ARENA = 207 * 1024
        arena = ctx.enter_context(nc.sbuf_tensor("arena", [P, ARENA // 4], F32))
        K = 1024

        def at(offset, cols, dt=F32):
            size = cols * {F32: 4, I32: 4, U32: 4, F16: 2, BF16: 2}[dt]
            assert offset % 4 == 0 and size % 4 == 0 and offset + size <= ARENA, (offset, size)
            v = arena[:, offset // 4:(offset + size) // 4]
            return v if dt == F32 else v.bitcast(dt)

        def grid(offset, a, b, dt=F32):
            return at(offset, a * b, dt).rearrange("p (a b) -> p a b", a=a)

        X = grid(0, TT, D)
        M16 = [grid(0, KC, T, F16), grid(8 * K, KC, T, F16)]
        SG = grid(0, 4, 512)
        HFULL = grid(8 * K, 4, 512)
        XT = [grid(16 * K, KC, T, F16), grid(24 * K, KC, T, F16)]
        GUW = [[grid(o * K, KC, 512, F16) for o in halves_at]
               for halves_at in ((96, 100), (88, 92), (64, 68), (16, 20), (24, 28), (72, 100), (16, 20))]
        X1T = [grid(32 * K, KC, T, F16), grid(40 * K, KC, T, F16)]
        XN_A = grid(32 * K, 4, D)
        H16 = [grid(48 * K, OC, T, F16), grid(76 * K, OC, T, F16)]
        MW = [grid(48 * K, KC, D, F16), grid(52 * K, KC, D, F16)]
        OW = [grid(56 * K, KC, D, F16), grid(60 * K, KC, D, F16)]
        L32 = at(64 * K, LA_N + LB_N)
        DW = [grid(104 * K, OC, D, F16), grid(118 * K, OC, D, F16)]
        MSUM = grid(104 * K, KC, D)
        PB = grid(132 * K, 4, 1024)
        NB = grid(148 * K, 2, 1024)
        LN_ = grid(156 * K, 3, 1024)
        CODES = grid(168 * K, 2, 1024, I32)
        SC = grid(176 * K, 2, 1024)
        L16 = at(184 * K, LA_N + LB_N, F16)
        STAGE = [at(132 * K, 2048), at(140 * K, 2048)]
        PT4 = at(132 * K, 4096).rearrange("p (s h t) -> p s h t", s=2, h=4)
        XN_C = grid(132 * K, 2, D)
        YN_B = grid(136 * K, 2, D)
        XN_B = grid(148 * K, 2, D)
        YN = grid(152 * K, 2, D)
        OT = grid(148 * K, 2, D)
        STAGE_E = [at(156 * K, 2048), at(164 * K, 2048)]
        o = 156 * K
        BW = [grid(o, KC, D, F16), grid(o + 4 * K, KC, D, F16)]
        o += 8 * K
        QW = [grid(o, KC, D, F16), grid(o + 4 * K, KC, D, F16)]
        o += 8 * K
        WOW = [grid(o, KC, D, F16), grid(o + 4 * K, KC, D, F16)]
        o += 8 * K
        BE = at(o, NE * D, F16)
        o += 8 * K
        RN = NE + NE * R
        RW = [grid(o, KC, RN, F16), grid(o + KC * RN * 2, KC, RN, F16)]
        o += KC * RN * 4
        LBW = [at(o, D, F16), at(o + K, D, F16)]
        o += 2 * K
        BB = at(o, D, F16)
        o += K
        KW = [grid(o, KC, P, F16), grid(o + K, KC, P, F16)]
        o += 2 * K
        VW = [grid(o, KC, HD, F16), grid(o + KC * HD * 2, KC, HD, F16)]
        o += KC * HD * 4
        GW = [grid(o, KC, NE, F16), grid(o + KC * NE * 2, KC, NE, F16)]
        o += KC * NE * 4
        assert o <= 199 * K
        HWF = grid(o, 2, P)
        o += K
        RSB = grid(o + K, 2, RN)
        HWT = grid(o, 2, 2 * P, F16)
        o += K
        o = 203 * K
        assert 184 * K + 2 * (LA_N + LB_N) <= o
        IDF = at(o, P)
        o += 4 * P
        I256 = at(o, P, F16)
        o += 2 * P
        ONES = at(o, P, F16)
        o += 2 * P
        IDB = at(o, P, BF16)
        o += 2 * P
        MASKQ = at(o, P, BF16)
        o += 2 * P
        MASKK = at(o, P, BF16)
        o += 2 * P
        SMALL = at(o, (ARENA - o) // 4)
        so = [0]

        def small(a, b=1):
            v = SMALL[:, so[0]:so[0] + a * b].rearrange("p (a b) -> p a b", a=a)
            so[0] += a * b
            return v

        norms = [(s, w) for s in "ABCD" for w in "xy"]
        slots = {k: 4 if k == ("A", "x") else 2 for k in norms}
        STAT = {k: small(slots[k], 6) for k in norms}
        MV = {k: small(slots[k], 2) for k in norms}
        SD = {k: small(slots[k], 1) for k in norms}
        RS = {k: small(slots[k], 1) for k in norms}
        NM = {k: small(slots[k], 1) for k in norms}
        EPSX = small(1, 1)[:, 0, :]
        EPSY = small(1, 1)[:, 0, :]
        RB = small(1, NE)[:, 0, :]
        GB = small(1, NE)[:, 0, :]
        INVK = small(1, NE)[:, 0, :]
        CUM = small(3, 4 + NE)
        ZB = small(6, NE)
        GS = small(TT, NE)
        LT = small(NE, NE)
        CMP = small(2, NE * NE)

        QX = [grid(32 * K + 32 * K * b, HEADS, 512, F16) for b in range(HF)]
        ATTN = grid(96 * K, TT, D)
        Q16 = [grid(112 * K, KC, T, F16), grid(120 * K, KC, T, F16)]
        K16 = [at(128 * K, T, F16), at(130 * K, T, F16)]
        KX = at(201 * K, T, F16)
        V1 = grid(152 * K, TT, 32)
        MX = grid(153 * K, TT, HEADS)
        MROW = at(154 * K, T, F16)
        RDEN = grid(128 * K, 2, 16)
        EW = [[grid((o + 4 * h) * K, KC, D, F16) for h in range(2)] for o in (112, 120, 32, 40, 48, 56, 64, 72)]
        YACC = grid(80 * K, 2, D)
        YE = grid(84 * K, 2, D)
        YZ = grid(88 * K, 2, D)

        psum = ctx.enter_context(nc.psum_tensor("psum", [P, 8, 512], F32))

        def banks(first, count, each=1):
            return [psum[:, i, :] if each == 1 else psum[:, i:i + each, :] for i in range(first, first + count * each, each)]

        j_hf = [(j, hf) for j in range(KC) for hf in range(HF)]
        main = [("T", tt) for tt in range(TT)] + [("m", *t) for t in j_hf] + [("o", *t) for t in j_hf]
        for oc in range(OC):
            for hf in range(HF):
                main += [("g", oc, hf), ("u", oc, hf)]
        ring_main = Ring(S, "main", banks(0, 4), main)
        ring_lora = Ring(S, "lora", banks(4, 2, 2), range(4, N_HU))
        ring_d = Ring(S, "down", banks(0, 2), range(TT))
        ring_b = Ring(S, "mix", banks(2, 4), range(TT))
        STEPS_B = TT + 6
        small_tiles = []
        for s in range(STEPS_B):
            small_tiles += [("TC", s - 6)] if 0 <= s - 6 < TT else []
            small_tiles += [("TB", s - 2), ("r", s - 2)] if 0 <= s - 2 < TT else []
            small_tiles += [("H", s - 3)] if 0 <= s - 3 < TT else []
        ring_s = Ring(S, "small", banks(6, 2), small_tiles)
        proj = [[("k", b)] + [("v", 4 * b + i) for i in range(4)] + [("q", j, b) for j in range(KC)] for b in range(HF)]
        ring_p = Ring(S, "proj", banks(0, 2), proj[0] + proj[1])
        proj_split = [key for p in proj for key in p if key[0] != "v"]
        proj_at = {TT + 2: proj[0][:5], TT + 3: proj[0][5:7], TT + 4: proj[0][7:]}
        max_tiles = []
        for tt in range(TT):
            max_tiles += [(tt, h) for h in range(HEADS)] + [(tt, "t")]
        ring_max = Ring(S, "max", banks(0, 2), max_tiles)
        score_tiles = [(b, hg, j, hp) for b in range(HF) for hg in range(8) for j in range(4) for hp in range(2)]
        ring_sc = Ring(S, "score", banks(2, 2, 2), score_tiles)
        groups = [(b, hg) for b in range(HF) for hg in range(8)]
        ring_pv = Ring(S, "pv", banks(6, 2), [k for g in groups for k in (("pv", *g), ("pt", *g))])
        STEPS_D = TT + 3
        tail = []
        for s in range(STEPS_D):
            tail += [("aT", s)] if s < TT else []
            tail += [("TD", s - 2)] if 0 <= s - 2 < TT else []
            tail += [("e", e, s - 3) for e in range(NE)] if 0 <= s - 3 else []
            tail += [("z", s - 2)] if 0 <= s - 2 < TT else []
            tail += [("w", s)] if s < TT else []
        ring_tail = Ring(S, "tail", banks(0, 8), tail)

        pieces = [("base", I["w_base"], KC * D, BW), ("router", I["w_rl"], KC * RN, RW), ("lorab", I["lora_b"], D, LBW),
                  ("bias", I["b_base"], D, BB), ("q", I["w_q"], KC * D, QW), ("k", I["w_k"], KC * P, KW),
                  ("v", I["w_v"], KC * HD, VW), ("wo", I["w_o"], KC * D, WOW), ("gate", I["w_gate"], KC * NE, GW),
                  ("be0", I["b_e"][:, 0:2048], 2048, BE[:, 0:2048]), ("be1", I["b_e"][:, 2048:4096], 2048, BE[:, 2048:4096])]
        pieces += [(f"e{e}", I["w_e"][e], KC * D, EW[e]) for e in range(NE)]
        piece_at = {p[0]: i for i, p in enumerate(pieces)}
        NW = len(pieces) - NE
        N_FIRST = 4

        def stage(i):
            if i >= NW:
                q = i - NW
                return STAGE_E[q % 2], S(f"stage_e{q % 2}"), q // 2 + 1, i - 2 if q >= 2 else None
            if i >= N_FIRST:
                return STAGE[1], S("stage1"), N_FIRST // 2 + i - N_FIRST + 1, i - 1
            return STAGE[i % 2], S(f"stage{i % 2}"), i // 2 + 1, i - 2 if i >= 2 else None

        lora_loads = []
        for name, row, col, n in (("a_q", 0, LA["qk"], D), ("a_k", R, LA["qk"], D), ("a_v", 0, LA["v"], D),
                                  ("a_o", 0, LA["o"], D), ("a_g", 0, LA["gu"], D), ("a_u", R, LA["gu"], D),
                                  ("a_down", 0, LA["down"], INTER), ("b_q", 0, LA_N + LB["qk"], D),
                                  ("b_k", R, LA_N + LB["qk"], D), ("b_v", 0, LA_N + LB["v"], D),
                                  ("b_o", 0, LA_N + LB["o"], D), ("b_down", 0, LA_N + LB["down"], D)):
            lora_loads.append((name, row, lambda p, col=col, n=n: L32[p:p + R, col:col + n]))
        for g, name in enumerate(("b_g", "b_u")):
            lora_loads.append((name, g * R, lambda p, g=g: L32[p:p + R, LA_N + LB["gu"]:LA_N + LB["down"]]
                               .rearrange("p (c g o) -> p c g o", c=OC // 2, g=2)[:, :, g, :]))

        taken_at = {}
        for i, t in enumerate(j_hf):
            taken_at.setdefault(N_ATTN + i // 4, []).append(("m", *t))
            taken_at.setdefault(N_ATTN + 3 + i // 4, []).append(("o", *t))
        for oc in range(OC):
            for hf in range(HF):
                taken_at.setdefault(N_ATTN + 5 + oc, []).append(("g", oc, hf))
        inner_at = {n: [t for t in ts if t[0] == "g"] for n, ts in taken_at.items()}
        STEPS_A = N_HU + 2
        assert max(taken_at) < STEPS_A

        def two_tiles(i):
            return range(2 * i, 2 * i + 2) if 0 <= i < TT // 2 else ()

        def flat(v):
            return v.rearrange("p a b -> p (a b)") if len(v.shape) == 3 else v

        def cols(n):
            return n // 2, n % 2

        def hu_weight(n, half):
            if n < N_ATTN:
                m, kh = cols(n)
                return (OW if m == 3 else MW)[half][:, 2 * kh:2 * kh + 2, :]
            if n < N_ATTN + N_GU:
                c, kh = cols(n - N_ATTN)
                return GUW[c][half][:, 2 * kh:2 * kh + 2, :]
            j = 2 * (n - N_ATTN - N_GU)
            return DW[half][:, j:j + 2, :]

        def n_scale_dmas(n):
            return sum(2 if i >= N_ATTN + N_GU else 1 for i in range(n % 2, n + 1, 2))

        q_dram = [nc.dram_tensor(f"q_half{i}", (D, T), F16, kind="Internal").ap() for i in range(2)]
        k_dram = [nc.dram_tensor(f"k_half{i}", (HD, T), F16, kind="Internal").ap() for i in range(2)]
        m_dram = nc.dram_tensor("minus_max", (HEADS, T), F16, kind="Internal").ap()

        block = ctx.enter_context(nc.Block())

        @block.sync
        def _(sp):
            def load_half_unit(n):
                c2 = CODES[:, n % 2, :]
                s2 = SC[:, n % 2, :]
                if n >= 2:
                    sp.wait_ge(S("line"), 8 * (n - 1))
                if n < N_ATTN:
                    m, kh = cols(n)
                    src, scale = I["codes_attn"][m][:, 1024 * kh:1024 * kh + 1024], I["scales_attn"][m]
                elif n < N_ATTN + N_GU:
                    c, kh = cols(n - N_ATTN)
                    src, scale = I["codes_gu"][c][:, 1024 * kh:1024 * kh + 1024], I["scales_gu"][c]
                else:
                    d = n - N_ATTN - N_GU
                    src, scale = I["codes_down"][d], None
                sp.dma_start(c2, src).then_inc(S(f"codes{n % 2}"), 16)
                if n >= 2:
                    sp.wait_ge(S("scaled"), n - 1)
                if scale is not None:
                    sp.dma_start(s2[:, 0:512], broadcast(scale, 16)).then_inc(S(f"scales{n % 2}"), 16)
                else:
                    for q in range(2):
                        sp.dma_start(s2[64 * q:64 * q + 64, :].rearrange("p (j o) -> p j o", j=2),
                                     repeat(I["scales_down"][4 * d + q:4 * d + 4:2], 64)).then_inc(S(f"scales{n % 2}"), 16)

            load_half_unit(0)
            for h in range(2):
                sp.dma_start(X[:, 4 * h:4 * h + 4, :], I["x"][:, 4 * h:4 * h + 4, :]).then_inc(S(f"x_in{h}"), 16)
                if h == 0:
                    sp.dma_start(IDF, I["ident"]).then_inc(S("ident_in"), 16)
                    load_half_unit(1)
            sp.dma_start(I256, I["ident256"]).then_inc(S("consts"), 16)
            sp.dma_start(ONES, I["ones_rows"]).then_inc(S("consts"), 16)
            sp.dma_start(INVK, I["inv_k"]).then_inc(S("consts"), 16)
            sp.dma_start(RB, broadcast(I["b_router"], P)).then_inc(S("consts"), 16)
            sp.dma_start(GB, broadcast(I["b_gate"], P)).then_inc(S("consts"), 16)
            sp.dma_start(flat(LT), I["before"]).then_inc(S("consts"), 16)
            sp.wait_ge(S("lora_zero_a"), 1)
            sp.wait_ge(S("lora_zero_b"), 1)
            for g in range(4):
                for name, row, dst in lora_loads:
                    sp.dma_start(dst(32 * g + row), I[name]).then_inc(S("lora_in"), 16)
                if g:
                    load_half_unit(1 + g)
            for n in range(5, N_HU):
                load_half_unit(n)
            sp.wait_ge(S("h_low"), OC * HF)
            for h in range(2):
                sp.dma_start(X[:, 4 * h:4 * h + 4, :], I["x"][:, 4 * h:4 * h + 4, :]).then_inc(S(f"x_again{h}"), 16)

            def load_piece(i):
                name, src, n, _ = pieces[i]
                slot, loaded, _, previous = stage(i)
                if previous is None:
                    if i < NW:
                        sp.wait_ge(S("w_low"), N_HU - 4)
                else:
                    sp.wait_ge(S("piece"), previous + 1)
                sp.dma_start(slot[:, 0:n], src).then_inc(loaded, 16)

            for i in range(NW):
                load_piece(i)

            with nc.allow_non_contiguous_dma(reason="rows of 1 KiB"):
                for b in range(HF):
                    tokens = slice(512 * b, 512 * b + 512)
                    ring_p.wait_read(sp, ("k", b))
                    for half in range(2):
                        sp.dma_start(k_dram[half][:, tokens], K16[half][0:HD, tokens]).then_inc(S(f"qk_out{b}"), 16)
                    for j in range(KC):
                        ring_p.wait_read(sp, ("q", j, b))
                        for half in range(2):
                            sp.dma_start(q_dram[half][P * j:P * j + P, tokens],
                                         Q16[half][:, j, tokens]).then_inc(S(f"qk_out{b}"), 16)
                    sp.wait_ge(S("qx_zero"), b + 1)
                    sp.dma_start(QX[b][0:16], I["alibi_q"]).then_inc(S(f"qx{b}"), 16)
                    if b == 0:
                        sp.wait_ge(S("kx_zero"), 1)
                        sp.dma_start(KX[0:16], I["alibi_k"]).then_inc(S(f"qx{b}"), 16)
                    sp.wait_ge(S(f"qk_out{b}"), 16 * (2 + 2 * KC))
                    for row, half in ((16, 0), (32, 0), (48, 1), (64, 1)):
                        sp.dma_start(KX[row:row + 16, tokens], k_dram[half][:, tokens]).then_inc(S(f"qx{b}"), 16)
                    for j in range(KC):
                        for row, half in ((16, 1), (32, 0), (48, 0), (64, 1)):
                            src = q_dram[half][P * j:P * j + P, tokens].rearrange("(h d) t -> d h t", d=HD)
                            sp.dma_start(QX[b][row:row + 16, 8 * j:8 * j + 8, :], src).then_inc(S(f"qx{b}"), 16)
                load_piece(NW)
                load_piece(NW + 1)
                for tt in range(TT):
                    b, qt = tt // 4, tt % 4
                    ring_max.wait_read(sp, (tt, "t"))
                    sp.dma_start(m_dram[:, P * tt:P * tt + P], MROW[0:HEADS, P * tt:P * tt + P]).then_inc(S("m_out"), 16)
                    sp.wait_ge(S("m_out"), 16 * (tt + 1))
                    sp.dma_start(QX[b][6:7, :, P * qt:P * qt + P],
                                 m_dram[:, P * tt:P * tt + P].rearrange("(a h) t -> a h t", a=1)).then_inc(S(f"m_in{b}"), 16)
            for i in range(NW + 2, NW + NE):
                load_piece(i)
            for tt in range(TT):
                sp.wait_ge(S("Dx_new"), tt + 1)
                sp.dma_start(out[:, tt, :], X[:, tt, :]).then_inc(S("out"), 16)
            sp.wait_ge(S("out"), 16 * TT)

        @block.gpsimd
        def _(pool):
            nc.gpsimd.memset(L32[:, 0:LA_N], 0.0).then_inc(S("lora_zero_a"), 1)

            def scaled(n):
                pool.wait_ge(S("table"), n + 1)
                pool.wait_ge(S(f"scales{n % 2}"), 16 * n_scale_dmas(n))
                v = PB[:, n % 4, :].rearrange("p (k o) -> p k o", k=2)
                dst = MSUM[:, 2 * n:2 * n + 2, :] if n < 2 else v
                sc = SC[:, n % 2, :]
                s = sc.rearrange("p (k o) -> p k o", k=2) if n >= N_ATTN + N_GU else \
                    sc[:, 0:512].rearrange("p (a o) -> p a o", a=1).to_broadcast([P, 2, 512])
                nc.gpsimd.tensor_tensor(dst, v, s, ALU.mult).then_inc(S("scaled"), 1)

            def low(n):
                pool.wait_ge(S("w_high"), n - 3)
                nc.gpsimd.tensor_tensor(hu_weight(n, 1), PB[:, n % 4, :].rearrange("p (k o) -> p k o", k=2),
                                        hu_weight(n, 0), ALU.subtract).then_inc(S("w_low"), 1)

            n_low = [0]

            def lora_low(c_first, c_last):
                (a0, b0), (a1, b1) = c_first, c_last
                for p0, n_p, c0, c1 in ((32, 32, a0, a1), (96, 32, a0, a1), (64, 64, LA_N + b0, LA_N + b1)):
                    v16, v32 = L16[p0:p0 + n_p, c0:c1], L32[p0:p0 + n_p, c0:c1]
                    nc.gpsimd.tensor_tensor(v16, v32, v16, ALU.subtract).then_inc(S("lora_low"), 1)
                    n_low[0] += 1
                    pool.wait_ge(S("lora_low"), n_low[0])

            for n in range(STEPS_A):
                if n < N_HU:
                    scaled(n)
                if 0 <= n - 2 < N_HU and n - 2 >= 4:
                    low(n - 2)
                if n in (3, 5):
                    pool.wait_ge(S("scaled"), n + 1)
                if n == 3:
                    pool.wait_ge(S("lora_high"), 1)
                    lora_low((0, 0), (LA["gu"], LB["gu"]))
                if n == 5:
                    lora_low((LA["gu"], LB["gu"]), (LA_N, LB_N))
                for _, j, hf in inner_at.get(n - 1, []):
                    i = j * HF + hf
                    pool.wait_ge(S("h_high"), i + 1)
                    nc.gpsimd.tensor_tensor(H16[1][:, j, 512 * hf:512 * hf + 512], HFULL[:, i % 4, :],
                                            H16[0][:, j, 512 * hf:512 * hf + 512], ALU.subtract).then_inc(S("h_low"), 1)
                if n == 2:
                    nc.gpsimd.memset(IDB, 0.0).then_inc(S("cst"), 1)
                    nc.gpsimd.memset(MASKQ, 0.0).then_inc(S("cst"), 1)
                    nc.gpsimd.memset(MASKK, 0.0).then_inc(S("cst"), 1)
                    pool.wait_ge(S("cst"), 3)
                    nc.gpsimd.affine_select(out=IDB, in_=IDB, compare_op=ALU.not_equal, fill=1.0, base=0,
                                            pattern=[[-1, P]], channel_multiplier=1).then_inc(S("masks"), 1)
                    nc.gpsimd.affine_select(out=MASKQ, in_=MASKQ, compare_op=ALU.is_ge, fill=NEG, base=0,
                                            pattern=[[-1, P]], channel_multiplier=1).then_inc(S("masks"), 1)
                    nc.gpsimd.affine_select(out=MASKK, in_=MASKK, compare_op=ALU.is_ge, fill=NEG, base=0,
                                            pattern=[[1, P]], channel_multiplier=-1).then_inc(S("masks"), 1)
            ring_d.wait_full(pool, TT - 1)
            for b in range(HF):
                nc.gpsimd.memset(at(32 * K + 32 * K * b, 8192)[64:128, :], 0.0).then_inc(S("qx_zero"), 1)
            nc.gpsimd.memset(at(201 * K, 512)[64:128, :], 0.0).then_inc(S("kx_zero"), 1)

        @block.scalar
        def _(act):
            def ln_out(s, tt, src, eps, out_tile, sig):
                act.wait_ge(S(s + "y_stat"), 4 * tt + 2)
                nc.scalar.activation(SD[s, "y"][:, tt % 2, :], MV[s, "y"][:, tt % 2, 1:2], ACT.Sqrt, bias=eps).then_inc(S(s + "y_sd"), 1)
                act.wait_ge(S(s + "y_stat"), 4 * tt + 4)
                if tt >= 2:
                    act.wait_ge(S(s + "x_new"), tt - 1)
                nc.scalar.activation(out_tile, src, ACT.Identity, bias=NM[s, "y"][:, tt % 2, :],
                                     scale=RS[s, "y"][:, tt % 2, :]).then_inc(sig, 1)

            def ln_in_sd(s, tt):
                act.wait_ge(S(s + "x_stat"), 4 * tt + 2)
                nc.scalar.activation(SD[s, "x"][:, tt % 2, :], MV[s, "x"][:, tt % 2, 1:2], ACT.Sqrt, bias=EPS).then_inc(S(s + "x_sd"), 1)

            def ln_in(s, tt, xn, ring, key):
                act.wait_ge(S(s + "x_stat"), 4 * tt + 4)
                if tt >= 2:
                    ring.wait_full(act, key(tt - 2))
                nc.scalar.activation(xn[:, tt % 2, :], X[:, tt, :], ACT.Identity, bias=NM[s, "x"][:, tt % 2, :],
                                     scale=RS[s, "x"][:, tt % 2, :]).then_inc(S(s + "xn"), 1)

            def high(dst, src, scale, sig):
                nc.scalar.activation(dst, src, ACT.Copy, scale=scale).then_inc(sig, 1)

            def t_high(s, tt, ring, key):
                ring.wait_full(act, key)
                high(XT[0][:, :, P * tt:P * tt + P], ring.at(key).rearrange("p (k t) -> p k t", k=KC), 1.0, S(s + "t_high"))

            def lines(n):
                act.wait_ge(S(f"codes{n % 2}"), 16 * (n // 2 + 1))
                if n >= 4 + 4:
                    act.wait_ge(S("w_low"), n - 7)
                elif n >= 4:
                    act.wait_ge(S("scaled"), n - 3)
                    if n >= 6:
                        act.wait_ge(S("sum"), n - 5)
                for i in range(8):
                    sgn, q = i % 2, i // 2
                    slope, offset = (MINUS if sgn else POS)[q]
                    k = 6 * n + i - 2
                    dst = PB[:, n % 4, :] if i == 0 else NB[:, n % 2, :] if i == 1 else LN_[:, k % 3, :]
                    if i >= 2 and k >= 3:
                        act.wait_ge(S("fold"), k - 2)
                    if i == 1 and n >= 2:
                        act.wait_ge(S("table"), n - 1)
                    nc.scalar.activation(dst, CODES[:, n % 2, :], ACT.Relu if q == 0 else ACT.Identity,
                                         bias=WSCALE * offset, scale=WSCALE * slope).then_inc(S("line"), 1)

            def w_high(n):
                ring_lora.wait_read(act, n)
                unit = (n - N_ATTN) // 2
                if n == N_ATTN:
                    act.wait_ge(S("lora_low"), 6)
                if n - N_ATTN == 2 * unit and unit == 5:
                    ring_main.wait_full(act, ("u", 5, HF - 1))
                if unit == 3:
                    ring_main.wait_full(act, ("o", KC - 1, HF - 1))
                if unit == 6:
                    ring_main.wait_full(act, ("u", 7, HF - 1))
                if n == N_ATTN + N_GU:
                    act.wait_ge(S("sum"), 4)
                high(hu_weight(n, 0), PB[:, n % 4, :].rearrange("p (k o) -> p k o", k=2), 1.0, S("w_high"))

            for n in range(STEPS_A):
                if n < N_HU:
                    lines(n)
                for tt in two_tiles(n - 1):
                    act.wait_ge(S("Ax_stat"), 2 * tt + 2)
                    nc.scalar.activation(SD["A", "x"][:, tt % 4, :], MV["A", "x"][:, tt % 4, 1:2], ACT.Sqrt,
                                         bias=EPS).then_inc(S("Ax_sd"), 1)
                for tt in two_tiles(n - 2):
                    act.wait_ge(S("Ax_norm"), 2 * tt + 2)
                    if tt >= 4:
                        ring_main.wait_full(act, ("T", tt - 4))
                    nc.scalar.activation(XN_A[:, tt % 4, :], X[:, tt, :], ACT.Identity, bias=NM["A", "x"][:, tt % 4, :],
                                         scale=RS["A", "x"][:, tt % 4, :]).then_inc(S("Axn"), 1)
                for tt in two_tiles(n - 3):
                    t_high("A", tt, ring_main, ("T", tt))
                if n == 3:
                    act.wait_ge(S("lora_in"), 16 * 4 * len(lora_loads))
                    high(L16, L32, 1.0, S("lora_high"))
                if 4 <= n - 2 < N_HU:
                    w_high(n - 2)
                for _, j, hf in inner_at.get(n - 1, []):
                    ring_main.wait_read(act, ("u", j, hf))
                    high(H16[0][:, j, 512 * hf:512 * hf + 512], HFULL[:, (j * HF + hf) % 4, :], 1.0, S("h_high"))
                for kind, j, hf in taken_at.get(n, []):
                    key = (kind, j, hf)
                    tokens = slice(512 * hf, 512 * hf + 512)
                    ring_main.wait_full(act, key)
                    if kind == "m":
                        high(M16[0][:, j, tokens], ring_main.at(key), 1 / (3 * WSCALE), S("m_high"))
                    elif kind == "o":
                        high(X1T[0][:, j, tokens], ring_main.at(key), 1 / WSCALE, S("x1_high"))
                    else:
                        i = j * HF + hf
                        if i >= 4:
                            ring_main.wait_read(act, ("u", (i - 4) // HF, (i - 4) % HF))
                        nc.scalar.activation(SG[:, i % 4, :], ring_main.at(key), ACT.Silu,
                                             scale=1 / WSCALE).then_inc(ring_main.free(key), 1)

            def piece_high(i):
                name, src, n, dst = pieces[i]
                slot, loaded, count, _ = stage(i)
                act.wait_ge(loaded, 16 * count)
                d = flat(dst[0]) if isinstance(dst, list) else dst
                high(d, slot[:, 0:n], WSCALE, S("piece_high"))

            for i in range(N_FIRST):
                piece_high(i)

            def take_projection(key):
                ring_p.wait_full(act, key)
                if key[0] == "v":
                    if key[1] == 0:
                        act.wait_ge(S("v1_ones"), 2)
                    nc.scalar.activation(V1[:, key[1], 0:HD], ring_p.at(key)[:, 0:HD], ACT.Copy,
                                         scale=1 / WSCALE).then_inc(ring_p.free(key), 1)
                elif key[0] == "k":
                    high(K16[0][:, 512 * key[1]:512 * key[1] + 512], ring_p.at(key), HD ** -0.5 / WSCALE, S("proj_high"))
                else:
                    high(Q16[0][:, key[1], 512 * key[2]:512 * key[2] + 512], ring_p.at(key), 1 / WSCALE, S("proj_high"))

            for s in range(STEPS_B):
                if 0 <= s - 4 < TT:
                    t = s - 4
                    ring_s.wait_full(act, ("H", t))
                    high(HWT[:, t % 2, 0:P], ring_s.at(("H", t))[:, 0:P], 1.0, S("hw_high"))
                if 0 <= s - 6 < TT:
                    t_high("C", s - 6, ring_s, ("TC", s - 6))
                if 0 <= s - 2 < TT:
                    t_high("B", s - 2, ring_s, ("TB", s - 2))
                t = s - 1
                if 0 <= t < TT:
                    ring_d.wait_full(act, t)
                    ln_out("A", t, ring_d.at(t), EPS * WSCALE ** 2, YN[:, t % 2, :], ring_d.free(t))
                    ln_in_sd("B", t)
                    ln_in("B", t, XN_B, ring_s, lambda i: ("TB", i))
                t = s - 5
                if 0 <= t < TT:
                    ring_b.wait_full(act, t)
                    ln_out("B", t, ring_b.at(t), EPS * WSCALE ** 2, YN_B[:, t % 2, :], ring_b.free(t))
                    ln_in_sd("C", t)
                    ln_in("C", t, XN_C, ring_s, lambda i: ("TC", i))
                if 0 <= s - 2 < TT:
                    t = s - 2
                    ring_s.wait_full(act, ("r", t))
                    if t >= 2:
                        act.wait_ge(S("hw"), t - 1)
                    nc.scalar.activation(RSB[:, t % 2, :], ring_s.at(("r", t))[:, 0:RN], ACT.Copy,
                                         scale=1 / WSCALE).then_inc(ring_s.free(("r", t)), 1)

                if 2 <= s < 2 + NW - N_FIRST:
                    piece_high(N_FIRST + s - 2)
                for key in proj_at.get(s, []):
                    take_projection(key)
            for key in proj[1]:
                take_projection(key)

            def minus_max(tt):
                ring_max.wait_full(act, (tt, "t"))
                nc.scalar.activation(MROW[0:HEADS, P * tt:P * tt + P], ring_max.at((tt, "t"))[0:HEADS, 0:P],
                                     ACT.Copy, scale=-1.0).then_inc(ring_max.free((tt, "t")), 1)

            def probs(b, hg, j):
                i = (b * 8 + hg) * 4 + j
                w = 512 - P * j
                if i >= 2:
                    pb, phg, pj = (i - 2) // 32, (i - 2) // 4 % 8, (i - 2) % 4
                    if pj == 3:
                        ring_pv.wait_full(act, ("pv", pb, phg))
                    else:
                        act.wait_ge(S("pv_done"), 3 * (pb * 8 + phg) + pj + 1)
                for hp in range(2):
                    ring_sc.wait_full(act, (b, hg, j, hp))
                    nc.scalar.activation(PT4[:, i % 2, 2 * hp:2 * hp + 2, 0:w], ring_sc.at((b, hg, j, hp))[:, :, 0:w],
                                         ACT.Exp).then_inc(ring_sc.free((b, hg, j, hp)), 1)

            for tt in range(4):
                minus_max(tt)
            for b in range(HF):
                for hg in range(8):
                    for j in range(4):
                        probs(b, hg, j)
                    if b == 1 and hg < NE - 2:
                        if hg == 0:
                            act.wait_ge(S("qk_out0"), 16 * (2 + 2 * KC))
                            act.wait_ge(S("qk_out1"), 16 * (2 + 2 * KC))
                        if hg == 2:
                            ring_sc.wait_full(act, (0, 7, 3, 1))
                        piece_high(NW + hg)
                    if b == 0 and hg % 2 == 1:
                        minus_max(4 + hg // 2)

            def a_high(tt):
                ring_tail.wait_full(act, ("aT", tt))
                high(XT[0][:, :, P * tt:P * tt + P], ring_tail.at(("aT", tt)).rearrange("p (k t) -> p k t", k=KC), 1.0, S("a_high"))

            def last_ln(tt):
                act.wait_ge(S("Dy_stat"), 4 * tt + 2)
                nc.scalar.activation(SD["D", "y"][:, tt % 2, :], MV["D", "y"][:, tt % 2, 1:2], ACT.Sqrt, bias=EPS).then_inc(S("Dy_sd"), 1)
                act.wait_ge(S("Dy_stat"), 4 * tt + 4)
                if tt >= 2:
                    act.wait_ge(S("Dx_new"), tt - 1)
                nc.scalar.activation(YZ[:, tt % 2, :], YACC[:, tt % 2, :], ACT.Identity, bias=NM["D", "y"][:, tt % 2, :],
                                     scale=RS["D", "y"][:, tt % 2, :]).then_inc(S("Dyn"), 1)

            for s in range(STEPS_D):
                if s < TT:
                    a_high(s)
                if s < 2:
                    if s == 0:
                        ring_sc.wait_full(act, (1, 7, 3, 1))
                    piece_high(NW + NE - 2 + s)
                if 0 <= s - 2 < TT:
                    t_high("D", s - 2, ring_tail, ("TD", s - 2))
                t = s - 1
                if 0 <= t < TT:
                    ring_tail.wait_full(act, ("w", t))
                    ln_out("C", t, ring_tail.at(("w", t)), EPS * WSCALE ** 2, YN[:, t % 2, :], ring_tail.free(("w", t)))
                    ln_in_sd("D", t)
                    ln_in("D", t, XN_B, ring_tail, lambda i: ("TD", i))
                t = s - 3
                for e in range(NE if t >= 0 else 0):
                    i = t * (NE - 1) + e - 1
                    if e == 0:
                        act.wait_ge(S("gates"), t + 1)
                        if t >= 2:
                            act.wait_ge(S("Dyn"), t - 1)
                    elif i >= 2:
                        act.wait_ge(S("acc"), i - 1)
                    ring_tail.wait_full(act, ("e", e, t))
                    nc.scalar.activation(YE[:, i % 2, :] if e else YACC[:, t % 2, :], ring_tail.at(("e", e, t)),
                                         ACT.Relu, scale=GS[:, t, e:e + 1]).then_inc(ring_tail.free(("e", e, t)), 1)
                    if e == 2 and t:
                        last_ln(t - 1)
            last_ln(TT - 1)

        @block.vector
        def _(dve):
            V = nc.vector

            def stats(s, w, tt, src):
                i = tt % 2
                done = S(s + w + "_stat")
                V.bn_stats(STAT[s, w][:, i, :], src).then_inc(done, 1)
                dve.wait_ge(done, 4 * tt + 1)
                V.bn_aggr(MV[s, w][:, i, :], STAT[s, w][:, i, :]).then_inc(done, 1)
                dve.wait_ge(S(s + w + "_sd"), tt + 1)
                V.reciprocal(RS[s, w][:, i, :], SD[s, w][:, i, :]).then_inc(done, 1)
                dve.wait_ge(done, 4 * tt + 3)
                V.scalar_tensor_tensor(out=NM[s, w][:, i, :], in0=MV[s, w][:, i, 0:1], scalar=-1.0, in1=RS[s, w][:, i, :],
                                       op0=ALU.mult, op1=ALU.mult).then_inc(done, 1)

            def add_residual(s, tt, yn):
                V.tensor_tensor(X[:, tt, :], X[:, tt, :], yn[:, tt % 2, :], ALU.add).then_inc(S(s + "x_new"), 1)
                dve.wait_ge(S(s + "x_new"), tt + 1)

            def low(dst, src, scale, hi, sig):
                V.scalar_tensor_tensor(out=dst, in0=src, scalar=scale, in1=hi, op0=ALU.mult,
                                       op1=ALU.subtract).then_inc(sig, 1)

            def t_low(s, tt, ring, key):
                cols_ = slice(P * tt, P * tt + P)
                dve.wait_ge(S(s + "t_high"), tt + 1)
                low(XT[1][:, :, cols_], ring.at(key).rearrange("p (k t) -> p k t", k=KC), 1.0,
                    XT[0][:, :, cols_], ring.free(key))

            V.memset(L32[:, LA_N:LA_N + LB_N], 0.0).then_inc(S("lora_zero_b"), 1)
            V.memset(CUM, 0.0).then_inc(S("cum_zero"), 1)
            def fold(n):
                for i in range(2, 8):
                    k = 6 * n + i - 2
                    acc = NB[:, n % 2, :] if i % 2 else PB[:, n % 4, :]
                    dve.wait_ge(S("line"), 8 * n + i + 1)
                    if i >= 4:
                        dve.wait_ge(S("fold"), k - 1)
                    V.tensor_tensor(acc, acc, LN_[:, k % 3, :], ALU.max).then_inc(S("fold"), 1)
                dve.wait_ge(S("fold"), 6 * n + 6)
                V.tensor_tensor(PB[:, n % 4, :], PB[:, n % 4, :], NB[:, n % 2, :], ALU.subtract).then_inc(S("table"), 1)

            def add_lora(n):
                v = PB[:, n % 4, :].rearrange("p (k o) -> p k o", k=2)
                m = MSUM[:, 2 * (n % 2):2 * (n % 2) + 2, :]
                dve.wait_ge(S("scaled"), n + 1)
                if n in (2, 3):
                    V.tensor_tensor(m, m, v, ALU.add).then_inc(S("sum"), 1)
                    return
                if n in (4, 5):
                    dve.wait_ge(S("sum"), n - 3)
                    V.tensor_tensor(v, v, m, ALU.add).then_inc(S("sum"), 1)
                    dve.wait_ge(S("sum"), n - 1)
                ring_lora.wait_full(dve, n)
                V.scalar_tensor_tensor(out=v, in0=ring_lora.at(n), scalar=WSCALE, in1=v, op0=ALU.mult,
                                       op1=ALU.add).then_inc(ring_lora.free(n), 1)

            for n in range(STEPS_A):
                if n < N_HU:
                    fold(n)
                if 2 <= n - 1 < N_HU:
                    add_lora(n - 1)
                for tt in two_tiles(n - 3):
                    t_low("A", tt, ring_main, ("T", tt))
                for tt in two_tiles(n - 1):
                    i = tt % 4
                    dve.wait_ge(S("Ax_sd"), tt + 1)
                    V.reciprocal(RS["A", "x"][:, i, :], SD["A", "x"][:, i, :]).then_inc(S("Ax_norm"), 1)
                    dve.wait_ge(S("Ax_norm"), 2 * tt + 1)
                    V.scalar_tensor_tensor(out=NM["A", "x"][:, i, :], in0=MV["A", "x"][:, i, 0:1], scalar=-1.0,
                                           in1=RS["A", "x"][:, i, :], op0=ALU.mult, op1=ALU.mult).then_inc(S("Ax_norm"), 1)
                for tt in two_tiles(n):
                    if tt % 4 == 0:
                        dve.wait_ge(S(f"x_in{tt // 4}"), 16)
                    V.bn_stats(STAT["A", "x"][:, tt % 4, :], X[:, tt, :]).then_inc(S("Ax_stat"), 1)
                    dve.wait_ge(S("Ax_stat"), 2 * tt + 1)
                    V.bn_aggr(MV["A", "x"][:, tt % 4, :], STAT["A", "x"][:, tt % 4, :]).then_inc(S("Ax_stat"), 1)
                for kind, j, hf in taken_at.get(n, []):
                    key = (kind, j, hf)
                    tokens = slice(512 * hf, 512 * hf + 512)
                    i = j * HF + hf
                    if kind == "m":
                        dve.wait_ge(S("m_high"), i + 1)
                        low(M16[1][:, j, tokens], ring_main.at(key), 1 / (3 * WSCALE), M16[0][:, j, tokens], ring_main.free(key))
                    elif kind == "o":
                        dve.wait_ge(S("x1_high"), i + 1)
                        low(X1T[1][:, j, tokens], ring_main.at(key), 1 / WSCALE, X1T[0][:, j, tokens], ring_main.free(key))
                    else:
                        u = ("u", j, hf)
                        ring_main.wait_read(dve, key)
                        ring_main.wait_full(dve, u)
                        if i >= 4:
                            dve.wait_ge(S("h_low"), i - 3)
                        V.scalar_tensor_tensor(out=HFULL[:, i % 4, :], in0=ring_main.at(u), scalar=1 / WSCALE,
                                               in1=SG[:, i % 4, :], op0=ALU.mult, op1=ALU.mult).then_inc(ring_main.free(u), 1)

            def piece_low(i):
                name, src, n, dst = pieces[i]
                dve.wait_ge(S("piece_high"), i + 1)
                if isinstance(dst, list):
                    low(flat(dst[1]), stage(i)[0][:, 0:n], WSCALE, flat(dst[0]), S("piece"))
                else:
                    low(dst[32:64, :], stage(i)[0][32:64, 0:n], WSCALE, dst[32:64, :], S("piece"))

            for i in range(N_FIRST):
                piece_low(i)

            def split_projection(key):
                i = proj_split.index(key)
                dve.wait_ge(S("proj_high"), i + 1)
                if key[0] == "k":
                    c = slice(512 * key[1], 512 * key[1] + 512)
                    low(K16[1][:, c], ring_p.at(key), HD ** -0.5 / WSCALE, K16[0][:, c], ring_p.free(key))
                else:
                    c = slice(512 * key[2], 512 * key[2] + 512)
                    low(Q16[1][:, key[1], c], ring_p.at(key), 1 / WSCALE, Q16[0][:, key[1], c], ring_p.free(key))

            def sparsemax(t):
                z, zs, f, tau, w = (ZB[:, i, :] for i in range(5))
                count = [8 * t]

                def done(ins):
                    count[0] += 1
                    ins.then_inc(S("sparse"), 1)
                    dve.wait_ge(S("sparse"), count[0])

                ring_s.wait_read(dve, ("r", t))
                r = RSB[:, t % 2, :]
                if t == 0:
                    dve.wait_ge(S("cum_zero"), 1)
                    dve.wait_ge(S("consts"), 16 * 6)
                done(V.tensor_tensor(z, r[:, 0:NE], RB, ALU.add))
                done(V.max(CUM[:, 0, 4:4 + NE], z))
                done(V.tensor_tensor(CUM[:, 1, 4:4 + NE], CUM[:, 0, 4:4 + NE], CUM[:, 0, 3:3 + NE], ALU.add))
                done(V.tensor_tensor(CUM[:, 2, 4:4 + NE], CUM[:, 1, 4:4 + NE], CUM[:, 1, 2:2 + NE], ALU.add))
                done(V.tensor_tensor(zs, CUM[:, 2, 4:4 + NE], CUM[:, 2, 0:NE], ALU.add))
                done(V.scalar_tensor_tensor(out=f, in0=zs, scalar=-1.0, in1=INVK, op0=ALU.add, op1=ALU.mult))
                done(V.tensor_reduce(tau[:, 0:1], f, AX_X, ALU.max))
                done(V.tensor_scalar(w, z, tau[:, 0:1], 0.0, ALU.subtract, ALU.max))
                if t >= 2:
                    ring_s.wait_full(dve, ("H", t - 2))
                V.tensor_tensor(HWF[:, t % 2, :].rearrange("p (e r) -> p e r", e=NE),
                                r[:, NE:RN].rearrange("p (e r) -> p e r", e=NE),
                                w.rearrange("p (e a) -> p e a", a=1).to_broadcast([P, NE, R]), ALU.mult).then_inc(S("hw"), 1)

            dve.wait_ge(S("x_again0"), 16)
            dve.wait_ge(S("x_again1"), 16)
            for s in range(STEPS_B):
                if 0 <= s - 4 < TT:
                    t = s - 4
                    dve.wait_ge(S("hw_high"), t + 1)
                    low(HWT[:, t % 2, P:2 * P], ring_s.at(("H", t))[:, 0:P], 1.0, HWT[:, t % 2, 0:P], ring_s.free(("H", t)))
                if 0 <= s - 3 < TT:
                    sparsemax(s - 3)
                if 0 <= s - 6 < TT:
                    t_low("C", s - 6, ring_s, ("TC", s - 6))
                if 0 <= s - 2 < TT:
                    t_low("B", s - 2, ring_s, ("TB", s - 2))
                t = s - 1
                if 0 <= t < TT:
                    ring_d.wait_full(dve, t)
                    stats("A", "y", t, ring_d.at(t))
                    ring_d.wait_read(dve, t)
                    add_residual("A", t, YN)
                    stats("B", "x", t, X[:, t, :])
                t = s - 5
                if 0 <= t < TT:
                    ring_b.wait_full(dve, t)
                    stats("B", "y", t, ring_b.at(t))
                    ring_b.wait_read(dve, t)
                    add_residual("B", t, YN_B)
                    stats("C", "x", t, X[:, t, :])

                if 2 <= s < 2 + NW - N_FIRST:
                    piece_low(N_FIRST + s - 2)
                if s == TT + 1:
                    V.memset(V1[:, :, HD:HD + 1], 1.0).then_inc(S("v1_ones"), 1)
                    V.memset(V1[:, :, HD + 1:32], 0.0).then_inc(S("v1_ones"), 1)
                for key in proj_at.get(s, []):
                    if key[0] != "v":
                        split_projection(key)
            for key in proj[1]:
                if key[0] != "v":
                    split_projection(key)

            def row_max(tt, h):
                ring_max.wait_full(dve, (tt, h))
                V.tensor_reduce(MX[:, tt, h:h + 1], ring_max.at((tt, h))[:, 0:P * (tt % 4 + 1)], AX_X,
                                ALU.max).then_inc(ring_max.free((tt, h)), 1)

            def sums(b, hg):
                i = b * 8 + hg
                ring_pv.wait_full(dve, ("pv", b, hg))
                if i >= 2:
                    ring_pv.wait_full(dve, ("pt", *groups[i - 2]))
                V.tensor_copy(OT[:, i % 2, :], ring_pv.at(("pv", b, hg))).then_inc(ring_pv.free(("pv", b, hg)), 1)

            def divide(b, hg):
                i = b * 8 + hg
                ring_pv.wait_full(dve, ("pt", b, hg))
                pt = ring_pv.at(("pt", b, hg)).rearrange("p (g d) -> p g d", d=32)
                V.reciprocal(RDEN[:, i % 2, :].rearrange("p (g a) -> p g a", a=1), pt[:, :, HD:HD + 1]).then_inc(S("rden"), 1)
                dve.wait_ge(S("rden"), i + 1)
                for qt in range(4):
                    o_ = ATTN[:, 4 * b + qt, 64 * hg:64 * hg + 64].rearrange("p (h d) -> p h d", d=HD)
                    ins = V.tensor_tensor(o_, pt[:, 4 * qt:4 * qt + 4, 0:HD],
                                          RDEN[:, i % 2, 4 * qt:4 * qt + 4].rearrange("p (g a) -> p g a", a=1)
                                          .to_broadcast([P, 4, HD]), ALU.mult)
                    ins.then_inc(ring_pv.free(("pt", b, hg)) if qt == 3 else S("divided"), 1)

            for tt in range(4):
                for h in range(HEADS):
                    row_max(tt, h)
            for b in range(HF):
                for hg in range(8):
                    i = b * 8 + hg
                    for q in range(16 if b == 0 else 0):
                        m = 16 * hg + q
                        row_max(4 + m // HEADS, m % HEADS)
                        if q == 3 and i >= 1:
                            sums(*groups[i - 1])
                    if b:
                        sums(*groups[i - 1])
                    if i >= 2:
                        divide(*groups[i - 2])
                    if b == 1 and hg < NE - 2:
                        piece_low(NW + hg)
            sums(*groups[-1])
            divide(*groups[-2])
            divide(*groups[-1])

            def gate(tt):
                count = [6 * tt]

                def done(ins):
                    count[0] += 1
                    ins.then_inc(S("rank"), 1)
                    dve.wait_ge(S("rank"), count[0])

                z, rank = ZB[:, 5, :], ZB[:, 0, :]
                a, b_ = (CMP[:, i, :].rearrange("p (e j) -> p e j", e=NE) for i in range(2))
                zj = z.rearrange("p (a j) -> p a j", a=1).to_broadcast([P, NE, NE])
                ze = z.rearrange("p (e a) -> p e a", a=1).to_broadcast([P, NE, NE])
                ring_tail.wait_full(dve, ("z", tt))
                V.scalar_tensor_tensor(out=z, in0=ring_tail.at(("z", tt))[:, 0:NE], scalar=1 / WSCALE, in1=GB,
                                       op0=ALU.mult, op1=ALU.add).then_inc(ring_tail.free(("z", tt)), 1)
                ring_tail.wait_read(dve, ("z", tt))
                done(V.tensor_tensor(a, zj, ze, ALU.is_gt))
                done(V.tensor_tensor(b_, zj, ze, ALU.is_equal))
                done(V.tensor_tensor(b_, b_, LT, ALU.mult))
                done(V.tensor_tensor(a, a, b_, ALU.add))
                done(V.tensor_reduce(rank, a, AX_X, ALU.add))
                done(V.tensor_scalar(GS[:, tt, :], rank, 1.5, 0.5 / WSCALE, ALU.is_lt, ALU.mult))
                V.tensor_copy(rank, GS[:, tt, :]).then_inc(S("gates"), 1)

            def last(tt):
                dve.wait_ge(S("acc"), (NE - 1) * (tt + 1))
                stats("D", "y", tt, YACC[:, tt % 2, :])
                dve.wait_ge(S("Dyn"), tt + 1)
                add_residual("D", tt, YZ)

            for s in range(STEPS_D):
                if s < TT:
                    cols_ = slice(P * s, P * s + P)
                    dve.wait_ge(S("a_high"), s + 1)
                    low(XT[1][:, :, cols_], ring_tail.at(("aT", s)).rearrange("p (k t) -> p k t", k=KC), 1.0,
                        XT[0][:, :, cols_], ring_tail.free(("aT", s)))
                if s < 2:
                    piece_low(NW + NE - 2 + s)
                if 0 <= s - 2 < TT:
                    t_low("D", s - 2, ring_tail, ("TD", s - 2))
                t = s - 1
                if 0 <= t < TT:
                    ring_tail.wait_full(dve, ("w", t))
                    stats("C", "y", t, ring_tail.at(("w", t)))
                    ring_tail.wait_read(dve, ("w", t))
                    add_residual("C", t, YN)
                    stats("D", "x", t, X[:, t, :])
                t = s - 3
                for e in range(NE if t >= 0 else 0):
                    if e:
                        i = t * (NE - 1) + e - 1
                        ring_tail.wait_read(dve, ("e", e, t))
                        if e == 1:
                            ring_tail.wait_read(dve, ("e", 0, t))
                        else:
                            dve.wait_ge(S("acc"), i)
                        V.tensor_tensor(YACC[:, t % 2, :], YACC[:, t % 2, :], YE[:, i % 2, :], ALU.add).then_inc(S("acc"), 1)
                    if e == 2 and t:
                        last(t - 1)
                if 0 <= s - 2 < TT:
                    gate(s - 2)
            last(TT - 1)

        @block.tensor
        def _(pe):
            mm = nc.tensor.matmul

            def transposes(ring, key, src):
                ring.wait_free(pe, key)
                for k in range(KC):
                    ins = nc.tensor.transpose(ring.at(key)[:, P * k:P * k + P], src[:, P * k:P * k + P], IDF)
                ins.then_inc(ring.full(key), 1)

            def product(dst, lhs, rhs, more=()):
                pairs = [(l[a], r[b]) for l, r in zip(lhs, rhs) for a, b in ((0, 0), (0, 1), (1, 0))]
                pairs += list(more)
                for i, (l, r) in enumerate(pairs):
                    ins = mm(dst, l, r, start=(i == 0), stop=(i == len(pairs) - 1))
                return ins

            def halves(w, k, c):
                return w[0][:, k, c], w[1][:, k, c]

            pe.wait_ge(S("ident_in"), 16)
            def lora(n):
                ring_lora.wait_free(pe, n)
                if n in (4, N_ATTN):
                    pe.wait_ge(S("lora_low"), 3 if n == 4 else 6)
                for i in range(2):
                    if n < N_ATTN:
                        m, kh = cols(n)
                        names = ("qk", "v") if m == 2 else ("o",)
                        pairs = [(LA[w] + P * (2 * kh + i), LA_N + LB[w]) for w in names]
                    elif n < N_ATTN + N_GU:
                        c, kh = cols(n - N_ATTN)
                        pairs = [(LA["gu"] + P * (2 * kh + i), LA_N + LB["gu"] + 512 * c)]
                    else:
                        pairs = [(LA["down"] + P * (2 * (n - N_ATTN - N_GU) + i), LA_N + LB["down"])]
                    for q, (a, b) in enumerate(pairs):
                        ins = mm(ring_lora.at(n)[:, i, :], L16[:, a:a + P], L16[:, b:b + 512],
                                 start=(q == 0), stop=(q == len(pairs) - 1))
                ins.then_inc(ring_lora.full(n), 1)

            waited = {"w": 0}

            def weights_ready(n):
                if waited["w"] < n - 3:
                    waited["w"] = n - 3
                    pe.wait_ge(S("w_low"), n - 3)

            for n in range(STEPS_A):
                if 4 <= n < N_HU:
                    lora(n)
                for tt in two_tiles(n - 2):
                    pe.wait_ge(S("Axn"), tt + 1)
                    transposes(ring_main, ("T", tt), XN_A[:, tt % 4, :])
                for kind, j, hf in taken_at.get(n, []):
                    tokens = slice(512 * hf, 512 * hf + 512)
                    key = (kind, j, hf)
                    if kind == "m":
                        weights_ready(5)
                        if (j, hf) == (0, 0):
                            ring_main.wait_read(pe, ("T", TT - 2))
                            ring_main.wait_read(pe, ("T", TT - 1))
                        ring_main.wait_free(pe, key)
                        product(ring_main.at(key), [halves(MW, k, slice(P * j, P * j + P)) for k in range(KC)],
                                [halves(XT, k, tokens) for k in range(KC)]).then_inc(ring_main.full(key), 1)
                    elif kind == "o":
                        weights_ready(7)
                        if (j, hf) == (0, 0):
                            for i in range(len(j_hf) - 4, len(j_hf)):
                                ring_main.wait_read(pe, ("m", *j_hf[i]))
                            pe.wait_ge(S("consts"), 16 * 6)
                        ring_main.wait_free(pe, key)
                        product(ring_main.at(key), [halves(OW, k, slice(P * j, P * j + P)) for k in range(KC)],
                                [halves(M16, k, tokens) for k in range(KC)],
                                [(I256, XT[0][:, j, tokens]), (I256, XT[1][:, j, tokens])]).then_inc(ring_main.full(key), 1)
                    else:
                        c = j // 2
                        weights_ready(N_ATTN + 2 * c + 1)
                        if (j, hf) == (0, 0):
                            for i in range(len(j_hf) - 4, len(j_hf)):
                                ring_main.wait_read(pe, ("o", *j_hf[i]))
                        for g, what in enumerate("gu"):
                            w = slice(256 * g + P * (j % 2), 256 * g + P * (j % 2) + P)
                            key = (what, j, hf)
                            ring_main.wait_free(pe, key)
                            product(ring_main.at(key), [halves(GUW[c], k, w) for k in range(KC)],
                                    [halves(X1T, k, tokens) for k in range(KC)]).then_inc(ring_main.full(key), 1)

            ring_main.wait_all_free(pe)
            ring_lora.wait_all_free(pe)
            weights_ready(N_HU - 1)
            pe.wait_ge(S("h_low"), OC * HF)

            def project(key):
                ring_p.wait_free(pe, key)
                if key[0] == "v":
                    dst, w, x = ring_p.at(key)[:, 0:HD], (VW, slice(0, HD)), slice(P * key[1], P * key[1] + P)
                elif key[0] == "k":
                    dst, w, x = ring_p.at(key), (KW, slice(0, P)), slice(512 * key[1], 512 * key[1] + 512)
                else:
                    dst, w, x = ring_p.at(key), (QW, slice(P * key[1], P * key[1] + P)), slice(512 * key[2], 512 * key[2] + 512)
                ws = [halves(w[0], k, w[1]) for k in range(KC)]
                xs = [halves(XT, k, x) for k in range(KC)]
                lhs, rhs = (xs, ws) if key[0] == "v" else (ws, xs)
                product(dst, lhs, rhs).then_inc(ring_p.full(key), 1)

            for s in range(STEPS_B):
                if 0 <= s - 6 < TT:
                    pe.wait_ge(S("Cxn"), s - 5)
                    transposes(ring_s, ("TC", s - 6), XN_C[:, (s - 6) % 2, :])
                if 0 <= s - 2 < TT:
                    pe.wait_ge(S("Bxn"), s - 1)
                    transposes(ring_s, ("TB", s - 2), XN_B[:, (s - 2) % 2, :])
                if s < TT:
                    tile = slice(P * s, P * s + P)
                    ring_d.wait_free(pe, s)
                    dst = ring_d.at(s)
                    pairs = [(H16[a][:, j, tile], DW[b][:, j, :]) for j in range(OC) for a, b in ((0, 0), (0, 1), (1, 0))]
                    for i, (l, r) in enumerate(pairs[:-1]):
                        mm(dst, l, r, start=(i == 0), stop=False)
                    for k in range(KC):
                        for half in range(2):
                            mm(dst[:, P * k:P * k + P], X1T[half][:, k, tile], I256, start=False, stop=False,
                               skip_group_check=True)
                    mm(dst, *pairs[-1], start=False, stop=True).then_inc(ring_d.full(s), 1)
                t = s - 2
                if 0 <= t < TT:
                    tile = slice(P * t, P * t + P)
                    if t == 0:
                        pe.wait_ge(S("piece"), N_FIRST)
                    ring_s.wait_read(pe, ("TB", t))
                    ring_s.wait_free(pe, ("r", t))
                    product(ring_s.at(("r", t))[:, 0:RN], [halves(XT, k, tile) for k in range(KC)],
                            [halves(RW, k, slice(0, RN)) for k in range(KC)]).then_inc(ring_s.full(("r", t)), 1)
                    ring_b.wait_free(pe, t)
                    dst = ring_b.at(t)
                    i = 0
                    for k in range(KC):
                        for a, b in ((0, 0), (0, 1), (1, 0)):
                            mm(dst, XT[a][:, k, tile], BW[b][:, k, :], start=(i == 0), stop=False)
                            i += 1
                    mm(dst, ONES, BB, start=False, stop=False)
                t = s - 3
                if 0 <= t < TT:
                    pe.wait_ge(S("hw"), t + 1)
                    ring_s.wait_free(pe, ("H", t))
                    nc.tensor.transpose(ring_s.at(("H", t))[:, 0:P], HWF[:, t % 2, :], IDF).then_inc(ring_s.full(("H", t)), 1)
                t = s - 4
                if 0 <= t < TT:
                    ring_s.wait_read(pe, ("H", t))
                    dst = ring_b.at(t)
                    hi, lo = HWT[:, t % 2, 0:P], HWT[:, t % 2, P:2 * P]
                    mm(dst, hi, LBW[0], start=False, stop=False)
                    mm(dst, hi, LBW[1], start=False, stop=False)
                    mm(dst, lo, LBW[0], start=False, stop=True).then_inc(ring_b.full(t), 1)

                if s in proj_at:
                    if s == TT + 2:
                        ring_d.wait_all_free(pe)
                        pe.wait_ge(S("piece"), NW)
                        for t in range(4):
                            ring_s.wait_read(pe, ("TC", t))
                    for key in proj_at[s]:
                        project(key)

            ring_b.wait_all_free(pe)
            ring_s.wait_all_free(pe)
            for key in proj[1]:
                project(key)
            ring_p.wait_all_free(pe)

            def max_scores(tt, h):
                b, qt = tt // 4, tt % 4
                key = (tt, h)
                w = P * (qt + 1)
                ring_max.wait_free(pe, key)
                q = QX[b][:, h, P * qt:P * qt + P]
                mm(ring_max.at(key)[:, 0:w], q, KX[:, 512 * b:512 * b + w], start=True, stop=True)
                mm(ring_max.at(key)[:, w - P:w], IDB, MASKQ, start=False, stop=True,
                   skip_group_check=True).then_inc(ring_max.full(key), 1)

            def max_transpose(tt):
                key = (tt, "t")
                for h in (HEADS - 2, HEADS - 1):
                    ring_max.wait_read(pe, (tt, h))
                ring_max.wait_free(pe, key)
                nc.tensor.transpose(ring_max.at(key)[0:HEADS, 0:P], MX[:, tt, :], IDF).then_inc(ring_max.full(key), 1)

            def score(b, hg, j):
                w = 512 - P * j
                for hp in range(2):
                    key = (b, hg, j, hp)
                    ring_sc.wait_free(pe, key)
                    for i in range(2):
                        h = 4 * hg + 2 * hp + i
                        dst = ring_sc.at(key)[:, i, :]
                        mm(dst[:, 0:w], KX[:, 512 * b + P * j:512 * b + P * j + P], QX[b][:, h, P * j:512], start=True, stop=True)
                        ins = mm(dst[:, 0:P], IDB, MASKK, start=False, stop=True, skip_group_check=True)
                    ins.then_inc(ring_sc.full(key), 1)

            def weigh(b, hg, j):
                i = (b * 8 + hg) * 4 + j
                w = 512 - P * j
                key = ("pv", b, hg)
                if j == 0:
                    ring_pv.wait_free(pe, key)
                for hp in range(2):
                    ring_sc.wait_read(pe, (b, hg, j, hp))
                for h in range(4):
                    ins = mm(ring_pv.at(key)[32 * h:32 * h + 32, P * j:512], V1[:, 4 * b + j, :], PT4[:, i % 2, h, 0:w],
                             start=(j == 0), stop=(j == 3), skip_group_check=True)
                    if h == 3:
                        ins.then_inc(ring_pv.full(key) if j == 3 else S("pv_done"), 1)

            def turn(b, hg):
                key = ("pt", b, hg)
                i = b * 8 + hg
                ring_pv.wait_free(pe, key)
                ring_pv.wait_read(pe, ("pv", b, hg))
                for qt in range(4):
                    ins = nc.tensor.transpose(ring_pv.at(key)[:, P * qt:P * qt + P], OT[:, i % 2, P * qt:P * qt + P], IDF)
                ins.then_inc(ring_pv.full(key), 1)

            pe.wait_ge(S("masks"), 3)
            pe.wait_ge(S("qx0"), 16 * (2 + 4 + 4 * KC))
            for tt in range(4):
                for h in range(HEADS):
                    max_scores(tt, h)
                max_transpose(tt)
            pe.wait_ge(S("qx1"), 16 * (1 + 4 + 4 * KC))
            for b in range(HF):
                if b == 0:
                    pe.wait_ge(S("m_in0"), 64)
                else:
                    pe.wait_ge(S("m_in1"), 64)
                for hg in range(8):
                    for j in range(4):
                        if b == 0:
                            for m in range(16 * hg + 4 * j, 16 * hg + 4 * j + 4):
                                max_scores(4 + m // HEADS, m % HEADS)
                        score(b, hg, j)
                        if j:
                            weigh(b, hg, j - 1)
                        elif (b, hg) != (0, 0):
                            weigh(*groups[b * 8 + hg - 1], 3)
                    if b == 0 and hg % 2 == 1:
                        max_transpose(4 + hg // 2)
                    if (b, hg) != (0, 0):
                        turn(*groups[b * 8 + hg - 1])
            weigh(HF - 1, 7, 3)
            turn(HF - 1, 7)

            ring_max.wait_all_free(pe)
            ring_sc.wait_all_free(pe)
            ring_pv.wait_all_free(pe)
            for s in range(STEPS_D):
                if s < TT:
                    transposes(ring_tail, ("aT", s), ATTN[:, s, :])
                if 0 <= s - 2 < TT:
                    t = s - 2
                    pe.wait_ge(S("Dxn"), t + 1)
                    transposes(ring_tail, ("TD", t), XN_B[:, t % 2, :])
                t = s - 3
                if t == 0:
                    pe.wait_ge(S("piece"), NW + NE)
                for e in range(NE if t >= 0 else 0):
                    key = ("e", e, t)
                    ring_tail.wait_free(pe, key)
                    product(ring_tail.at(key), [halves(XT, k, slice(P * t, P * t + P)) for k in range(KC)],
                            [halves(EW[e], k, slice(0, D)) for k in range(KC)],
                            [(ONES, BE[:, D * e:D * e + D])]).then_inc(ring_tail.full(key), 1)
                t = s - 2
                if 0 <= t < TT:
                    key = ("z", t)
                    ring_tail.wait_read(pe, ("TD", t))
                    ring_tail.wait_free(pe, key)
                    product(ring_tail.at(key)[:, 0:NE], [halves(XT, k, slice(P * t, P * t + P)) for k in range(KC)],
                            [halves(GW, k, slice(0, NE)) for k in range(KC)]).then_inc(ring_tail.full(key), 1)
                t = s
                if t < TT:
                    key = ("w", t)
                    ring_tail.wait_read(pe, ("aT", t))
                    ring_tail.wait_free(pe, key)
                    product(ring_tail.at(key), [halves(XT, k, slice(P * t, P * t + P)) for k in range(KC)],
                            [halves(WOW, k, slice(0, D)) for k in range(KC)]).then_inc(ring_tail.full(key), 1)


def broadcast(src, n):
    if len(src.shape) == 1:
        src = src.rearrange("(a o) -> a o", a=1)
    rows, width = src.shape
    return bass.AP(tensor=src.tensor, offset=src.offset, ap=[list(src.ap[0]), [0, n], list(src.ap[1])])


def repeat(src, n):
    return bass.AP(tensor=src.tensor, offset=src.offset, ap=[[0, n], list(src.ap[0]), list(src.ap[1])])


def kernel(**inputs):
    import numpy as np
    import concourse.bacc as bacc
    from concourse.bass_utils import run_bass_kernel_spmd

    a = {k: np.asarray(v) for k, v in inputs.items()}
    perm = (4 * np.arange(P)[None, :] + np.arange(KC)[:, None]).reshape(-1)

    def rows(w):
        return w[perm].reshape(KC, P, -1).transpose(1, 0, 2).reshape(P, -1)

    def plain_rows(w):
        return w.reshape(-1, P, w.shape[-1]).transpose(1, 0, 2).reshape(P, -1)

    def bias_rows(b):
        t = np.zeros((P, b.shape[-1]), np.float32)
        t[0] = t[32] = b
        return t

    x = a["L0_attn_x"].reshape(TT, P, D)[:, :, perm].transpose(1, 0, 2)
    ca = a["L0_attn_codes_attn"]
    cg = a["L0_attn_codes_gu"].reshape(2, OC // 2, 256, D)
    sg = a["L0_attn_scales_gu"].reshape(2, OC // 2, 256, 8)
    cd = a["L0_attn_codes_down"][perm].T
    wr, la = a["L0_ffn_W_router"].T, a["L0_ffn_lora_A"].transpose(1, 0, 2).reshape(D, NE * R)
    wqkv = a["L1_attn_Wqkv"]
    A, B = a["L0_attn_lora_A_h"], a["L0_attn_lora_B_attn"]
    bgu = a["L0_attn_lora_B_gu"].reshape(2, OC // 2, 256, R)
    pos = np.arange(512, dtype=np.float64)
    base = 2.0 ** (-2.0 ** (-(5 - 3)))
    slopes = (base ** np.arange(1, HEADS + 1, dtype=np.float64)).astype(np.float32).astype(np.float64)
    s_hi = slopes.astype(np.float16)
    s_lo = (slopes - s_hi).astype(np.float16)
    alibi_q = np.zeros((16, HEADS, 512), np.float16)
    for i, s in ((0, s_hi), (3, s_lo)):
        s = s.astype(np.float64)[:, None]
        alibi_q[i] = s
        alibi_q[i + 1] = -s * pos
        alibi_q[i + 2] = -s * pos - alibi_q[i + 1].astype(np.float64)
    alibi_k = np.zeros((16, T), np.float16)
    alibi_k[0] = alibi_k[3] = np.tile(pos, HF)
    alibi_k[[1, 2, 4, 5, 6]] = 1.0
    ones_rows = np.zeros((P, P), np.float16)
    ones_rows[[0, 32]] = 1.0

    data = {
        "x": x,
        "codes_attn": np.stack([rows(ca[m][perm].T) for m in range(4)]),
        "scales_attn": np.stack([a["L0_attn_scales_attn"][m][perm].T for m in range(4)]),
        "codes_gu": np.stack([rows(cg[:, c].reshape(512, D).T) for c in range(OC // 2)]),
        "scales_gu": np.stack([sg[:, c].reshape(512, 8).T for c in range(OC // 2)]),
        "codes_down": np.stack([plain_rows(cd[256 * d:256 * d + 256]) for d in range(N_DOWN)]),
        "scales_down": a["L0_attn_scales_down"][perm].T,
        "a_q": A[0][:, perm], "a_k": A[1][:, perm], "a_v": A[2][:, perm], "a_o": A[3][:, perm],
        "a_g": A[4][:, perm], "a_u": A[5][:, perm], "a_down": a["L0_attn_lora_A_down"],
        "b_q": B[0][perm].T, "b_k": B[1][perm].T, "b_v": B[2][perm].T, "b_o": B[3][perm].T,
        "b_g": bgu[0].transpose(2, 0, 1), "b_u": bgu[1].transpose(2, 0, 1),
        "b_down": a["L0_attn_lora_B_down"][perm].T,
        "w_base": rows(a["L0_ffn_W_base"][perm].T), "b_base": bias_rows(a["L0_ffn_b_base"][perm]),
        "w_rl": rows(np.concatenate([wr, la], axis=1)), "b_router": a["L0_ffn_b_router"],
        "lora_b": a["L0_ffn_lora_B"].reshape(NE * R, D)[:, perm],
        "w_q": rows(wqkv[:, :D]), "w_k": rows(np.tile(wqkv[:, D:D + HD], (1, NE))), "w_v": rows(wqkv[:, D + HD:]),
        "w_o": plain_rows(a["L1_attn_Wo"][:, perm]),
        "w_gate": rows(a["L1_ffn_W_gate"]), "b_gate": a["L1_ffn_b_gate"],
        "w_e": np.stack([rows(a["L1_ffn_W_e"][e][:, perm]) for e in range(NE)]),
        "b_e": bias_rows(a["L1_ffn_b_e"][:, perm].reshape(-1)),
        "ident": np.eye(P, dtype=np.float32), "ident256": np.eye(P, dtype=np.float16) * np.float16(WSCALE),
        "ones_rows": ones_rows, "inv_k": np.tile((1.0 / np.arange(1, NE + 1)).astype(np.float32), (P, 1)),
        "before": np.tile(np.tril(np.ones((NE, NE), np.float32), -1).reshape(1, -1), (P, 1)),
        "alibi_q": alibi_q, "alibi_k": alibi_k,
    }
    nc = bacc.Bacc("TRN2", target_bir_lowering=False, num_devices=1)
    arrays, handles = {}, {}
    for name, v in data.items():
        arrays[f"in_{name}"] = np.ascontiguousarray(v)
        handles[name] = nc.dram_tensor(f"in_{name}", arrays[f"in_{name}"].shape, mybir.dt.from_np(v.dtype), kind="ExternalInput").ap()
    out = nc.dram_tensor("out", (P, TT, D), F32, kind="ExternalOutput").ap()
    sandwich(nc, handles, out)
    r = run_bass_kernel_spmd(nc, [arrays], core_ids=[0])
    got = np.asarray(r.results[0]["out"])
    y = np.empty((TT, P, D), np.float32)
    y[:, :, perm] = got.transpose(1, 0, 2)
    return y.reshape(HF, 512, D)
```

```python
from contextlib import ExitStack

import concourse.bass as bass
from concourse import mybir

F32 = mybir.dt.float32
F16 = mybir.dt.float16
BF16 = mybir.dt.bfloat16
I32 = mybir.dt.int32
U32 = mybir.dt.uint32
ALU = mybir.AluOpType
ACT = mybir.ActivationFunctionType
AX_X = mybir.AxisListType.X

P = 128
T = 1024
TT = T // P
D = 512
KC = D // P
HF = T // 512
INTER = 1792
OC = INTER // P
HEADS, HD = 32, 16
NE = 8
R = 16
WSCALE = 256.0
EPS = 1e-5
NEG = -1e30
NF4 = [-1.0, -0.6961928009986877, -0.5250730514526367, -0.39491748809814453, -0.28444138169288635,
       -0.18477343022823334, -0.09105003625154495, 0.0, 0.07958029955625534, 0.16093020141124725,
       0.24611230194568634, 0.33791524171829224, 0.44070982933044434, 0.5626170039176941,
       0.7229568362236023, 1.0]

LA = {"qk": 0, "v": 512, "o": 1024, "gu": 1536, "down": 2048}
LA_N = 2048 + INTER
LB = {"qk": 0, "v": 512, "o": 1024, "gu": 1536, "down": 1536 + 2 * INTER}
LB_N = 2048 + 2 * INTER

N_ATTN, N_GU, N_DOWN = 8, 14, 7
N_HU = N_ATTN + N_GU + N_DOWN


def nf4_line(i, j):
    s = (NF4[j] - NF4[i]) / (j - i)
    return s, NF4[i] - s * i


POS = [nf4_line(8, 9), nf4_line(10, 11), nf4_line(12, 13), nf4_line(14, 15)]
MINUS = [tuple(-a for a in nf4_line(i, i + 1)) for i in (6, 4, 2, 0)]


class Ring:

    def __init__(self, sem, name, slots, keys):
        self.slots = slots
        self.n = len(slots)
        self.index = {k: i for i, k in enumerate(keys)}
        assert len(self.index) == len(keys)
        self.full_sems = [sem(f"{name}_full{s}") for s in range(self.n)]
        self.free_sems = [sem(f"{name}_free{s}") for s in range(self.n)]

    def at(self, key):
        return self.slots[self.index[key] % self.n]

    def full(self, key):
        return self.full_sems[self.index[key] % self.n]

    def free(self, key):
        return self.free_sems[self.index[key] % self.n]

    def wait_free(self, eng, key):
        use = self.index[key] // self.n
        if use:
            eng.wait_ge(self.free(key), use)

    def wait_full(self, eng, key):
        eng.wait_ge(self.full(key), self.index[key] // self.n + 1)

    def wait_read(self, eng, key):
        eng.wait_ge(self.free(key), self.index[key] // self.n + 1)

    def wait_all_free(self, eng):
        total = len(self.index)
        for s in range(self.n):
            uses = (total - s + self.n - 1) // self.n
            if uses:
                eng.wait_ge(self.free_sems[s], uses)


def sandwich(nc, I, out):
    ctx = ExitStack()
    with ctx:
        sems = {}

        def S(name):
            if name not in sems:
                sems[name] = ctx.enter_context(nc.semaphore(name))
            return sems[name]

        ARENA = 207 * 1024
        arena = ctx.enter_context(nc.sbuf_tensor("arena", [P, ARENA // 4], F32))
        K = 1024

        def at(offset, cols, dt=F32):
            size = cols * {F32: 4, I32: 4, U32: 4, F16: 2, BF16: 2}[dt]
            assert offset % 4 == 0 and size % 4 == 0 and offset + size <= ARENA, (offset, size)
            v = arena[:, offset // 4:(offset + size) // 4]
            return v if dt == F32 else v.bitcast(dt)

        def grid(offset, a, b, dt=F32):
            return at(offset, a * b, dt).rearrange("p (a b) -> p a b", a=a)

        X = grid(0, TT, D)
        M16 = [grid(0, KC, T, F16), grid(8 * K, KC, T, F16)]
        STAGE_FIRST = [at(24 * K, 2048)] + [at(16 * K + 2560 * i, 640) for i in range(3)]
        SG = grid(0, 4, 512)
        HFULL = grid(8 * K, 4, 512)
        XT = [grid(16 * K, KC, T, F16), grid(24 * K, KC, T, F16)]
        GUW = [[grid(o * K, KC, 512, F16) for o in halves_at]
               for halves_at in ((96, 100), (88, 92), (64, 68), (16, 20), (24, 28), (72, 100), (16, 20))]
        X1T = [grid(32 * K, KC, T, F16), grid(40 * K, KC, T, F16)]
        XN_A = grid(32 * K, 4, D)
        H16 = [grid(48 * K, OC, T, F16), grid(76 * K, OC, T, F16)]
        MW = [grid(48 * K, KC, D, F16), grid(52 * K, KC, D, F16)]
        OW = [grid(56 * K, KC, D, F16), grid(60 * K, KC, D, F16)]
        L32 = at(64 * K, LA_N + LB_N)
        DW = [grid(104 * K, OC, D, F16), grid(118 * K, OC, D, F16)]
        MSUM = grid(104 * K, KC, D)
        PB = grid(132 * K, 4, 1024)
        NB = grid(148 * K, 2, 1024)
        LN_ = grid(156 * K, 3, 1024)
        CODES = grid(168 * K, 2, 1024, I32)
        SC = grid(176 * K, 2, 1024)
        L16 = at(184 * K, LA_N + LB_N, F16)
        STAGE = at(140 * K, 2048)
        PT4 = at(132 * K, 4096).rearrange("p (s h t) -> p s h t", s=2, h=4)
        XN_C = grid(132 * K, 2, D)
        YN_B = grid(136 * K, 2, D)
        XN_B = grid(148 * K, 2, D)
        YN = grid(152 * K, 2, D)
        OT = grid(148 * K, 2, D)
        STAGE_E = [at(156 * K, 2048), at(164 * K, 2048)]
        o = 156 * K
        BW = [grid(o, KC, D, F16), grid(o + 4 * K, KC, D, F16)]
        o += 8 * K
        QW = [grid(o, KC, D, F16), grid(o + 4 * K, KC, D, F16)]
        o += 8 * K
        WOW = [grid(o, KC, D, F16), grid(o + 4 * K, KC, D, F16)]
        o += 8 * K
        BE = at(o, NE * D, F16)
        o += 8 * K
        RN = NE + NE * R
        RW = [grid(o, KC, RN, F16), grid(o + KC * RN * 2, KC, RN, F16)]
        o += KC * RN * 4
        LBW = [at(o, D, F16), at(o + K, D, F16)]
        o += 2 * K
        BB = at(o, D, F16)
        o += K
        KW = [grid(o, KC, P, F16), grid(o + K, KC, P, F16)]
        o += 2 * K
        VW = [grid(o, KC, HD, F16), grid(o + KC * HD * 2, KC, HD, F16)]
        o += KC * HD * 4
        GW = [grid(o, KC, NE, F16), grid(o + KC * NE * 2, KC, NE, F16)]
        o += KC * NE * 4
        assert o <= 199 * K
        HWF = grid(o, 2, P)
        o += K
        RSB = grid(o + K, 2, RN)
        HWT = grid(o, 2, 2 * P, F16)
        o += K
        o = 203 * K
        assert 184 * K + 2 * (LA_N + LB_N) <= o
        IDF = at(o, P)
        o += 4 * P
        I256 = at(o, P, F16)
        o += 2 * P
        ONES = at(o, P, F16)
        o += 2 * P
        IDB = at(o, P, BF16)
        o += 2 * P
        MASKQ = at(o, P, BF16)
        o += 2 * P
        MASKK = at(o, P, BF16)
        o += 2 * P
        SMALL = at(o, (ARENA - o) // 4)
        so = [0]

        def small(a, b=1):
            v = SMALL[:, so[0]:so[0] + a * b].rearrange("p (a b) -> p a b", a=a)
            so[0] += a * b
            return v

        norms = [(s, w) for s in "ABCD" for w in "xy"]
        slots = {k: 4 if k == ("A", "x") else 2 for k in norms}
        STAT = {k: small(slots[k], 6) for k in norms}
        MV = {k: small(slots[k], 2) for k in norms}
        SD = {k: small(slots[k], 1) for k in norms}
        RS = {k: small(slots[k], 1) for k in norms}
        NM = {k: small(slots[k], 1) for k in norms}
        RB = small(1, NE)[:, 0, :]
        GB = small(1, NE)[:, 0, :]
        INVK = small(1, NE)[:, 0, :]
        CUM = small(3, 4 + NE)
        ZB = small(6, NE)
        GS = small(TT, NE)
        LT = small(NE, NE)
        CMP = small(2, NE * NE)

        QX = [grid(32 * K + 32 * K * b, HEADS, 512, F16) for b in range(HF)]
        ATTN = grid(96 * K, TT, D)
        Q16 = [grid(112 * K, KC, T, F16), grid(120 * K, KC, T, F16)]
        K16 = [at(128 * K, T, F16), at(130 * K, T, F16)]
        KX = at(201 * K, T, F16)
        V1 = grid(152 * K, TT, 32)
        MX = grid(153 * K, TT, HEADS)
        MROW = at(154 * K, T, F16)
        RDEN = grid(128 * K, 2, 16)
        EW = [[grid((o + 4 * h) * K, KC, D, F16) for h in range(2)] for o in (112, 120, 32, 40, 48, 56, 64, 72)]
        YACC = grid(80 * K, 2, D)
        YE = grid(84 * K, 2, D)
        YZ = grid(88 * K, 2, D)

        psum = ctx.enter_context(nc.psum_tensor("psum", [P, 8, 512], F32))

        def banks(first, count, each=1):
            return [psum[:, i, :] if each == 1 else psum[:, i:i + each, :] for i in range(first, first + count * each, each)]

        j_hf = [(j, hf) for j in range(KC) for hf in range(HF)]
        main = [("T", tt) for tt in range(TT)] + [("m", *t) for t in j_hf] + [("o", *t) for t in j_hf]
        for oc in range(OC):
            for hf in range(HF):
                main += [("g", oc, hf), ("u", oc, hf)]
        ring_main = Ring(S, "main", banks(0, 4), main)
        ring_lora = Ring(S, "lora", banks(4, 2, 2), range(4, N_HU))
        ring_d = Ring(S, "down", banks(0, 2), range(TT))
        ring_b = Ring(S, "mix", banks(2, 4), range(TT))
        STEPS_B = TT + 2
        small_tiles = []
        for s in range(STEPS_B):
            small_tiles += [("TB", s - 1)] if 0 <= s - 1 < TT else []
            small_tiles += [("TC", s - 2)] if 0 <= s - 2 < TT else []
            small_tiles += [("r", s - 1), ("H", s - 1)] if 0 <= s - 1 < TT else []
        ring_s = Ring(S, "small", banks(6, 2), small_tiles)
        proj = [[("k", b)] + [("v", 4 * b + i) for i in range(4)] + [("q", j, b) for j in range(KC)] for b in range(HF)]
        ring_p = Ring(S, "proj", banks(0, 2), proj[0] + proj[1])
        proj_split = [key for p in proj for key in p if key[0] != "v"]
        proj_at = {(TT, i): keys for i, keys in enumerate((proj[0][:2], proj[0][2:4], proj[0][4:6], proj[0][6:7], proj[0][7:]))}
        def max_heads(tt):
            return 4 // (1, 2, 4, 4)[tt % 4]

        max_tiles = []
        for tt in range(TT):
            max_tiles += [(tt, h) for h in range(0, HEADS, max_heads(tt))] + [(tt, "t")]
        ring_max = Ring(S, "max", banks(4, 2), max_tiles)
        score_tiles = [[(b, hg, j, hp) for hg in range(8) for j in range(4) for hp in range(2)] for b in range(HF)]
        ring_sc = [Ring(S, "score0", banks(0, 2, 2), score_tiles[0]), Ring(S, "score1", banks(0, 3, 2), score_tiles[1])]
        N_BETWEEN = 8
        between = [(i // HEADS, i % HEADS) for i in range(N_BETWEEN * (len(proj[1]) - 1))]
        alone = [(tt, h) for tt in range(4) for h in range(HEADS)][len(between):]
        groups = [(b, hg) for b in range(HF) for hg in range(8)]
        ring_pv = Ring(S, "pv", banks(6, 2), [k for g in groups for k in (("pv", *g), ("pt", *g))])
        STEPS_D = TT + 3
        tail = []
        for s in range(STEPS_D):
            tail += [("aT", s)] if s < TT else []
            tail += [("TD", s - 2)] if 0 <= s - 2 < TT else []
            tail += [("e", e, s - 3) for e in range(NE)] if 0 <= s - 3 else []
            tail += [("z", s - 2)] if 0 <= s - 2 < TT else []
            tail += [("w", s)] if s < TT else []
        ring_tail = Ring(S, "tail", banks(0, 8), tail)

        pieces = [("base", I["w_base"], KC * D, BW), ("router", I["w_rl"], KC * RN, RW), ("lorab", I["lora_b"], D, LBW),
                  ("bias", I["b_base"], D, BB), ("q", I["w_q"], KC * D, QW), ("k", I["w_k"], KC * P, KW),
                  ("v", I["w_v"], KC * HD, VW), ("wo", I["w_o"], KC * D, WOW), ("gate", I["w_gate"], KC * NE, GW),
                  ("be0", I["b_e"][:, 0:2048], 2048, BE[:, 0:2048]), ("be1", I["b_e"][:, 2048:4096], 2048, BE[:, 2048:4096])]
        pieces += [(f"e{e}", I["w_e"][e], KC * D, EW[e]) for e in range(NE)]
        NW = len(pieces) - NE
        N_FIRST = 4

        def stage(i):
            if i >= NW:
                q = i - NW
                return STAGE_E[q % 2], S(f"stage_e{q % 2}"), q // 2 + 1, i - 2 if q >= 2 else None
            if i >= N_FIRST:
                return STAGE, S("stage"), i - N_FIRST + 1, i - 1 if i > N_FIRST else None
            return STAGE_FIRST[i], S("stage_f0" if i == 0 else "stage_f"), 1 if i == 0 else N_FIRST - 1, None

        lora_loads = []
        for name, row, col, n in (("a_q", 0, LA["qk"], D), ("a_k", R, LA["qk"], D), ("a_v", 0, LA["v"], D),
                                  ("a_o", 0, LA["o"], D), ("a_g", 0, LA["gu"], D), ("a_u", R, LA["gu"], D),
                                  ("a_down", 0, LA["down"], INTER), ("b_q", 0, LA_N + LB["qk"], D),
                                  ("b_k", R, LA_N + LB["qk"], D), ("b_v", 0, LA_N + LB["v"], D),
                                  ("b_o", 0, LA_N + LB["o"], D), ("b_down", 0, LA_N + LB["down"], D)):
            lora_loads.append((name, row, lambda p, col=col, n=n: L32[p:p + R, col:col + n]))
        for g, name in enumerate(("b_g", "b_u")):
            lora_loads.append((name, g * R, lambda p, g=g: L32[p:p + R, LA_N + LB["gu"]:LA_N + LB["down"]]
                               .rearrange("p (c g o) -> p c g o", c=OC // 2, g=2)[:, :, g, :]))

        taken_at = {}
        for i, t in enumerate(j_hf):
            taken_at.setdefault(N_ATTN + i // 4, []).append(("m", *t))
            taken_at.setdefault(N_ATTN + 3 + i // 4, []).append(("o", *t))
        for oc in range(OC):
            for hf in range(HF):
                taken_at.setdefault(N_ATTN + 5 + oc, []).append(("g", oc, hf))
        inner_at = {n: [t for t in ts if t[0] == "g"] for n, ts in taken_at.items()}
        STEPS_A = N_HU + 2
        assert max(taken_at) < STEPS_A

        def two_tiles(i):
            return range(2 * i, 2 * i + 2) if 0 <= i < TT // 2 else ()

        def flat(v):
            return v.rearrange("p a b -> p (a b)") if len(v.shape) == 3 else v

        def cols(n):
            return n // 2, n % 2

        def hu_weight(n, half):
            if n < N_ATTN:
                m, kh = cols(n)
                return (OW if m == 3 else MW)[half][:, 2 * kh:2 * kh + 2, :]
            if n < N_ATTN + N_GU:
                c, kh = cols(n - N_ATTN)
                return GUW[c][half][:, 2 * kh:2 * kh + 2, :]
            j = 2 * (n - N_ATTN - N_GU)
            return DW[half][:, j:j + 2, :]

        def n_scale_dmas(n):
            return sum(2 if i >= N_ATTN + N_GU else 1 for i in range(n % 2, n + 1, 2))

        q_dram = [nc.dram_tensor(f"q_half{i}", (D, T), F16, kind="Internal").ap() for i in range(2)]
        k_dram = [nc.dram_tensor(f"k_half{i}", (HD, T), F16, kind="Internal").ap() for i in range(2)]
        m_dram = nc.dram_tensor("minus_max", (HEADS, T), F16, kind="Internal").ap()

        block = ctx.enter_context(nc.Block())

        @block.sync
        def _(sp):
            def load_half_unit(n):
                c2 = CODES[:, n % 2, :]
                s2 = SC[:, n % 2, :]
                if n >= 2:
                    sp.wait_ge(S("line"), 8 * (n - 1))
                if n < N_ATTN:
                    m, kh = cols(n)
                    src, scale = I["codes_attn"][m][:, 1024 * kh:1024 * kh + 1024], I["scales_attn"][m]
                elif n < N_ATTN + N_GU:
                    c, kh = cols(n - N_ATTN)
                    src, scale = I["codes_gu"][c][:, 1024 * kh:1024 * kh + 1024], I["scales_gu"][c]
                else:
                    d = n - N_ATTN - N_GU
                    src, scale = I["codes_down"][d], None
                sp.dma_start(c2, src).then_inc(S(f"codes{n % 2}"), 16)
                if n >= 2:
                    sp.wait_ge(S("scaled"), n - 1)
                if scale is not None:
                    sp.dma_start(s2[:, 0:512], broadcast(scale, 16)).then_inc(S(f"scales{n % 2}"), 16)
                else:
                    for q in range(2):
                        sp.dma_start(s2[64 * q:64 * q + 64, :].rearrange("p (j o) -> p j o", j=2),
                                     repeat(I["scales_down"][4 * d + q:4 * d + 4:2], 64)).then_inc(S(f"scales{n % 2}"), 16)

            def load_piece(i):
                name, src, n, _ = pieces[i]
                slot, loaded, _, previous = stage(i)
                if previous is None:
                    if i == N_FIRST:
                        sp.wait_ge(S("w_low"), N_HU - 4)
                else:
                    sp.wait_ge(S("piece"), previous + 1)
                sp.dma_start(slot[:, 0:n], src).then_inc(loaded, 16)

            load_half_unit(0)
            for h in range(2):
                sp.dma_start(X[:, 4 * h:4 * h + 4, :], I["x"][:, 4 * h:4 * h + 4, :]).then_inc(S(f"x_in{h}"), 16)
                if h == 0:
                    sp.dma_start(IDF, I["ident"]).then_inc(S("ident_in"), 16)
                    load_half_unit(1)
            sp.dma_start(I256, I["ident256"]).then_inc(S("consts"), 16)
            sp.dma_start(ONES, I["ones_rows"]).then_inc(S("consts"), 16)
            sp.dma_start(INVK, I["inv_k"]).then_inc(S("consts"), 16)
            sp.dma_start(RB, broadcast(I["b_router"], P)).then_inc(S("consts"), 16)
            sp.dma_start(GB, broadcast(I["b_gate"], P)).then_inc(S("consts"), 16)
            sp.dma_start(flat(LT), I["before"]).then_inc(S("consts"), 16)
            sp.wait_ge(S("lora_zero_a"), 1)
            sp.wait_ge(S("lora_zero_b"), 1)
            for g in range(4):
                for name, row, dst in lora_loads:
                    sp.dma_start(dst(32 * g + row), I[name]).then_inc(S("lora_in"), 16)
                if g:
                    load_half_unit(1 + g)
            for n in range(5, N_HU):
                load_half_unit(n)
            ring_main.wait_full(sp, ("u", 9, HF - 1))
            load_piece(0)
            ring_main.wait_full(sp, ("u", OC - 1, HF - 1))
            for i in range(1, N_FIRST):
                load_piece(i)
            sp.wait_ge(S("h_low"), OC * HF)
            for h in range(2):
                sp.dma_start(X[:, 4 * h:4 * h + 4, :], I["x"][:, 4 * h:4 * h + 4, :]).then_inc(S(f"x_again{h}"), 16)

            for i in range(N_FIRST, NW):
                load_piece(i)

            with nc.allow_non_contiguous_dma(reason="rows of 1 KiB"):
                for b in range(HF):
                    tokens = slice(512 * b, 512 * b + 512)
                    ring_p.wait_read(sp, ("k", b))
                    for half in range(2):
                        sp.dma_start(k_dram[half][:, tokens], K16[half][0:HD, tokens]).then_inc(S(f"qk_out{b}"), 16)
                    for jj in range(0, KC, 2):
                        for j in (jj, jj + 1):
                            ring_p.wait_read(sp, ("q", j, b))
                        for half in range(2):
                            sp.dma_start(q_dram[half][P * jj:P * jj + 2 * P, tokens].rearrange("(j p) t -> p j t", p=P),
                                         Q16[half][:, jj:jj + 2, tokens]).then_inc(S(f"qk_out{b}"), 16)
                    sp.wait_ge(S("qx_zero"), b + 1)
                    sp.dma_start(QX[b][0:16], I["alibi_q"]).then_inc(S(f"qx{b}"), 16)
                    if b == 0:
                        sp.wait_ge(S("kx_zero"), 1)
                        sp.dma_start(KX[0:16], I["alibi_k"]).then_inc(S(f"qx{b}"), 16)
                    sp.wait_ge(S(f"qk_out{b}"), 16 * (2 + 4))
                    for row, half in ((16, 0), (32, 0), (48, 1), (64, 1)):
                        sp.dma_start(KX[row:row + 16, tokens], k_dram[half][:, tokens]).then_inc(S(f"qx{b}"), 16)
                    for h in range(0, HEADS, 16):
                        for row, half in ((16, 1), (32, 0), (48, 0), (64, 1)):
                            src = q_dram[half][HD * h:HD * (h + 16), tokens].rearrange("(h d) t -> d h t", d=HD)
                            sp.dma_start(QX[b][row:row + 16, h:h + 16, :], src).then_inc(S(f"qx{b}"), 16)
                load_piece(NW)
                load_piece(NW + 1)
                for tt in range(TT):
                    b, qt = tt // 4, tt % 4
                    ring_max.wait_read(sp, (tt, "t"))
                    sp.dma_start(m_dram[:, P * tt:P * tt + P], MROW[0:HEADS, P * tt:P * tt + P]).then_inc(S("m_out"), 16)
                    sp.wait_ge(S("m_out"), 16 * (tt + 1))
                    sp.dma_start(QX[b][6:7, :, P * qt:P * qt + P],
                                 m_dram[:, P * tt:P * tt + P].rearrange("(a h) t -> a h t", a=1)).then_inc(S(f"m_in{b}"), 16)
            for i in range(NW + 2, NW + NE):
                load_piece(i)
            for tt in range(TT):
                sp.wait_ge(S("Dx_new"), tt + 1)
                sp.dma_start(out[:, tt, :], X[:, tt, :]).then_inc(S("out"), 16)
            sp.wait_ge(S("out"), 16 * TT)

        @block.gpsimd
        def _(pool):
            nc.gpsimd.memset(L32[:, 0:LA_N], 0.0).then_inc(S("lora_zero_a"), 1)

            def scaled(n):
                pool.wait_ge(S("table"), n + 1)
                pool.wait_ge(S(f"scales{n % 2}"), 16 * n_scale_dmas(n))
                v = PB[:, n % 4, :].rearrange("p (k o) -> p k o", k=2)
                dst = MSUM[:, 2 * n:2 * n + 2, :] if n < 2 else v
                sc = SC[:, n % 2, :]
                s = sc.rearrange("p (k o) -> p k o", k=2) if n >= N_ATTN + N_GU else \
                    sc[:, 0:512].rearrange("p (a o) -> p a o", a=1).to_broadcast([P, 2, 512])
                nc.gpsimd.tensor_tensor(dst, v, s, ALU.mult).then_inc(S("scaled"), 1)

            def low(n):
                pool.wait_ge(S("w_high"), n - 3)
                nc.gpsimd.tensor_tensor(hu_weight(n, 1), PB[:, n % 4, :].rearrange("p (k o) -> p k o", k=2),
                                        hu_weight(n, 0), ALU.subtract).then_inc(S("w_low"), 1)

            n_low = [0]

            def lora_low(c_first, c_last):
                (a0, b0), (a1, b1) = c_first, c_last
                for p0, n_p, c0, c1 in ((32, 32, a0, a1), (96, 32, a0, a1), (64, 64, LA_N + b0, LA_N + b1)):
                    v16, v32 = L16[p0:p0 + n_p, c0:c1], L32[p0:p0 + n_p, c0:c1]
                    nc.gpsimd.tensor_tensor(v16, v32, v16, ALU.subtract).then_inc(S("lora_low"), 1)
                    n_low[0] += 1
                    pool.wait_ge(S("lora_low"), n_low[0])

            for n in range(STEPS_A):
                if 4 <= n - 2 < N_HU:
                    low(n - 2)
                if n < N_HU:
                    scaled(n)
                if n in (3, 5):
                    pool.wait_ge(S("scaled"), n + 1)
                if n == 3:
                    pool.wait_ge(S("lora_high"), 1)
                    lora_low((0, 0), (LA["gu"], LB["gu"]))
                if n == 5:
                    lora_low((LA["gu"], LB["gu"]), (LA_N, LB_N))
                for _, j, hf in inner_at.get(n - 1, []):
                    i = j * HF + hf
                    pool.wait_ge(S("h_high"), i + 1)
                    nc.gpsimd.tensor_tensor(H16[1][:, j, 512 * hf:512 * hf + 512], HFULL[:, i % 4, :],
                                            H16[0][:, j, 512 * hf:512 * hf + 512], ALU.subtract).then_inc(S("h_low"), 1)
                if n == 2:
                    nc.gpsimd.memset(IDB, 0.0).then_inc(S("cst"), 1)
                    nc.gpsimd.memset(MASKQ, 0.0).then_inc(S("cst"), 1)
                    nc.gpsimd.memset(MASKK, 0.0).then_inc(S("cst"), 1)
                    pool.wait_ge(S("cst"), 3)
                    nc.gpsimd.affine_select(out=IDB, in_=IDB, compare_op=ALU.not_equal, fill=1.0, base=0,
                                            pattern=[[-1, P]], channel_multiplier=1).then_inc(S("masks"), 1)
                    nc.gpsimd.affine_select(out=MASKQ, in_=MASKQ, compare_op=ALU.is_ge, fill=NEG, base=0,
                                            pattern=[[-1, P]], channel_multiplier=1).then_inc(S("masks"), 1)
                    nc.gpsimd.affine_select(out=MASKK, in_=MASKK, compare_op=ALU.is_ge, fill=NEG, base=0,
                                            pattern=[[1, P]], channel_multiplier=-1).then_inc(S("masks"), 1)
            ring_d.wait_full(pool, TT - 1)
            for b in range(HF):
                nc.gpsimd.memset(at(32 * K + 32 * K * b, 8192)[64:128, :], 0.0).then_inc(S("qx_zero"), 1)
            nc.gpsimd.memset(at(201 * K, 512)[64:128, :], 0.0).then_inc(S("kx_zero"), 1)

        @block.scalar
        def _(act):
            def deviation(s, w, tt, eps):
                act.wait_ge(S(s + w + "_stat"), 4 * tt + 2)
                nc.scalar.activation(SD[s, w][:, tt % 2, :], MV[s, w][:, tt % 2, 1:2], ACT.Sqrt, bias=eps).then_inc(S(s + w + "_sd"), 1)

            def normed(s, tt, src, out_tile, sig):
                act.wait_ge(S(s + "y_stat"), 4 * tt + 4)
                if tt >= 2:
                    act.wait_ge(S(s + "x_new"), tt - 1)
                nc.scalar.activation(out_tile, src, ACT.Identity, bias=NM[s, "y"][:, tt % 2, :],
                                     scale=RS[s, "y"][:, tt % 2, :]).then_inc(sig, 1)

            def ln_out(s, tt, src, eps, out_tile, sig):
                deviation(s, "y", tt, eps)
                normed(s, tt, src, out_tile, sig)

            def ln_in(s, tt, xn, ring, key):
                act.wait_ge(S(s + "x_stat"), 4 * tt + 4)
                if tt >= 2:
                    ring.wait_full(act, key(tt - 2))
                nc.scalar.activation(xn[:, tt % 2, :], X[:, tt, :], ACT.Identity, bias=NM[s, "x"][:, tt % 2, :],
                                     scale=RS[s, "x"][:, tt % 2, :]).then_inc(S(s + "xn"), 1)

            def high(dst, src, scale, sig):
                nc.scalar.activation(dst, src, ACT.Copy, scale=scale).then_inc(sig, 1)

            def t_high(s, tt, ring, key):
                ring.wait_full(act, key)
                high(XT[0][:, :, P * tt:P * tt + P], ring.at(key).rearrange("p (k t) -> p k t", k=KC), 1.0, S(s + "t_high"))

            def lines(n):
                act.wait_ge(S(f"codes{n % 2}"), 16 * (n // 2 + 1))
                if n >= 4 + 4:
                    act.wait_ge(S("w_low"), n - 7)
                elif n >= 4:
                    act.wait_ge(S("scaled"), n - 3)
                    if n >= 6:
                        act.wait_ge(S("sum"), n - 5)
                for i in range(8):
                    sgn, q = i % 2, i // 2
                    slope, offset = (MINUS if sgn else POS)[q]
                    k = 6 * n + i - 2
                    dst = PB[:, n % 4, :] if i == 0 else NB[:, n % 2, :] if i == 1 else LN_[:, k % 3, :]
                    if i >= 2 and k >= 3:
                        act.wait_ge(S("fold"), k - 2)
                    if i == 1 and n >= 2:
                        act.wait_ge(S("table"), n - 1)
                    nc.scalar.activation(dst, CODES[:, n % 2, :], ACT.Relu if q == 0 else ACT.Identity,
                                         bias=WSCALE * offset, scale=WSCALE * slope).then_inc(S("line"), 1)

            def piece_high(i):
                name, src, n, dst = pieces[i]
                slot, loaded, count, _ = stage(i)
                act.wait_ge(loaded, 16 * count)
                d = flat(dst[0]) if isinstance(dst, list) else dst
                high(d, slot[:, 0:n], WSCALE, S("piece_high"))

            def w_high(n):
                ring_lora.wait_read(act, n)
                unit = (n - N_ATTN) // 2
                if n == N_ATTN:
                    act.wait_ge(S("lora_low"), 6)
                if n - N_ATTN == 2 * unit and unit == 5:
                    ring_main.wait_full(act, ("u", 5, HF - 1))
                if unit == 3:
                    ring_main.wait_full(act, ("o", KC - 1, HF - 1))
                if unit == 6:
                    ring_main.wait_full(act, ("u", 7, HF - 1))
                if n == N_ATTN + N_GU:
                    act.wait_ge(S("sum"), 4)
                high(hu_weight(n, 0), PB[:, n % 4, :].rearrange("p (k o) -> p k o", k=2), 1.0, S("w_high"))

            for n in range(STEPS_A):
                if n < N_HU:
                    lines(n)
                for tt in two_tiles(n - 1):
                    act.wait_ge(S("Ax_stat"), 2 * tt + 2)
                    nc.scalar.activation(SD["A", "x"][:, tt % 4, :], MV["A", "x"][:, tt % 4, 1:2], ACT.Sqrt,
                                         bias=EPS).then_inc(S("Ax_sd"), 1)
                for tt in two_tiles(n - 2):
                    act.wait_ge(S("Ax_norm"), 2 * tt + 2)
                    if tt >= 4:
                        ring_main.wait_full(act, ("T", tt - 4))
                    nc.scalar.activation(XN_A[:, tt % 4, :], X[:, tt, :], ACT.Identity, bias=NM["A", "x"][:, tt % 4, :],
                                         scale=RS["A", "x"][:, tt % 4, :]).then_inc(S("Axn"), 1)
                for tt in two_tiles(n - 3):
                    t_high("A", tt, ring_main, ("T", tt))
                if n == 3:
                    act.wait_ge(S("lora_in"), 16 * 4 * len(lora_loads))
                    high(L16, L32, 1.0, S("lora_high"))
                if 4 <= n - 2 < N_HU:
                    w_high(n - 2)
                if n == N_HU:
                    act.wait_ge(S("fold"), 6 * N_HU)
                    piece_high(0)
                for _, j, hf in inner_at.get(n - 1, []):
                    ring_main.wait_read(act, ("u", j, hf))
                    high(H16[0][:, j, 512 * hf:512 * hf + 512], HFULL[:, (j * HF + hf) % 4, :], 1.0, S("h_high"))
                for kind, j, hf in taken_at.get(n, []):
                    key = (kind, j, hf)
                    tokens = slice(512 * hf, 512 * hf + 512)
                    ring_main.wait_full(act, key)
                    if kind == "m":
                        high(M16[0][:, j, tokens], ring_main.at(key), 1 / (3 * WSCALE), S("m_high"))
                    elif kind == "o":
                        high(X1T[0][:, j, tokens], ring_main.at(key), 1 / WSCALE, S("x1_high"))
                    else:
                        i = j * HF + hf
                        if i >= 4:
                            ring_main.wait_read(act, ("u", (i - 4) // HF, (i - 4) % HF))
                        nc.scalar.activation(SG[:, i % 4, :], ring_main.at(key), ACT.Silu,
                                             scale=1 / WSCALE).then_inc(ring_main.free(key), 1)

            for i in range(1, N_FIRST):
                piece_high(i)

            def take_projection(key):
                ring_p.wait_full(act, key)
                if key[0] == "v":
                    if key[1] == 0:
                        act.wait_ge(S("v1_ones"), 2)
                    nc.scalar.activation(V1[:, key[1], 0:HD], ring_p.at(key)[:, 0:HD], ACT.Copy,
                                         scale=1 / WSCALE).then_inc(ring_p.free(key), 1)
                elif key[0] == "k":
                    high(K16[0][:, 512 * key[1]:512 * key[1] + 512], ring_p.at(key), HD ** -0.5 / WSCALE, S("proj_high"))
                else:
                    high(Q16[0][:, key[1], 512 * key[2]:512 * key[2] + 512], ring_p.at(key), 1 / WSCALE, S("proj_high"))

            for s in range(STEPS_B):
                a, c = s - 1, s - 2
                has_a, has_c = 0 <= a < TT, 0 <= c < TT
                if has_a:
                    ring_d.wait_full(act, a)
                    deviation("A", "y", a, EPS * WSCALE ** 2)
                if has_c:
                    ring_b.wait_full(act, c)
                    deviation("B", "y", c, EPS * WSCALE ** 2)
                if has_a:
                    normed("A", a, ring_d.at(a), YN[:, a % 2, :], ring_d.free(a))
                if has_c:
                    normed("B", c, ring_b.at(c), YN_B[:, c % 2, :], ring_b.free(c))
                if has_a:
                    deviation("B", "x", a, EPS)
                if has_c:
                    deviation("C", "x", c, EPS)
                if has_a:
                    ln_in("B", a, XN_B, ring_s, lambda i: ("TB", i))
                if has_c:
                    ln_in("C", c, XN_C, ring_s, lambda i: ("TC", i))
                for key in proj_at.get((s, 0), []):
                    take_projection(key)
                if has_a:
                    t_high("B", a, ring_s, ("TB", a))
                if has_c:
                    t_high("C", c, ring_s, ("TC", c))
                for key in proj_at.get((s, 1), []):
                    take_projection(key)
                if has_a:
                    ring_s.wait_full(act, ("r", a))
                    if a >= 2:
                        act.wait_ge(S("hw"), a - 1)
                    nc.scalar.activation(RSB[:, a % 2, :], ring_s.at(("r", a))[:, 0:RN], ACT.Copy,
                                         scale=1 / WSCALE).then_inc(ring_s.free(("r", a)), 1)
                for key in proj_at.get((s, 2), []) + proj_at.get((s, 3), []):
                    take_projection(key)
                if 2 <= s < 2 + NW - N_FIRST:
                    piece_high(N_FIRST + s - 2)
                if has_a:
                    ring_s.wait_full(act, ("H", a))
                    if a >= 2:
                        ring_b.wait_full(act, a - 2)
                    high(HWT[:, a % 2, 0:P], ring_s.at(("H", a))[:, 0:P], 1.0, S("hw_high"))
                for key in proj_at.get((s, 4), []):
                    take_projection(key)

            def minus_max(tt):
                ring_max.wait_full(act, (tt, "t"))
                nc.scalar.activation(MROW[0:HEADS, P * tt:P * tt + P], ring_max.at((tt, "t"))[0:HEADS, 0:P],
                                     ACT.Copy, scale=-1.0).then_inc(ring_max.free((tt, "t")), 1)

            for i, key in enumerate(proj[1]):
                for tt, h in (between[N_BETWEEN * (i - 1):N_BETWEEN * i] if i else []):
                    if h == HEADS - 1:
                        minus_max(tt)
                take_projection(key)

            def probs(b, hg, j):
                i = (b * 8 + hg) * 4 + j
                w = 512 - P * j
                if i >= 2:
                    pb, phg, pj = (i - 2) // 32, (i - 2) // 4 % 8, (i - 2) % 4
                    if pj == 3:
                        ring_pv.wait_full(act, ("pv", pb, phg))
                    else:
                        act.wait_ge(S("pv_done"), 3 * (pb * 8 + phg) + pj + 1)
                for hp in range(2):
                    ring_sc[b].wait_full(act, (b, hg, j, hp))
                    nc.scalar.activation(PT4[:, i % 2, 2 * hp:2 * hp + 2, 0:w], ring_sc[b].at((b, hg, j, hp))[:, :, 0:w],
                                         ACT.Exp).then_inc(ring_sc[b].free((b, hg, j, hp)), 1)

            for tt, h in alone:
                if h == HEADS - 1:
                    minus_max(tt)
            for b in range(HF):
                for hg in range(8):
                    for j in range(4):
                        probs(b, hg, j)
                    if b == 0 and hg % 2 == 1:
                        minus_max(4 + hg // 2)

            def a_high(tt):
                ring_tail.wait_full(act, ("aT", tt))
                high(XT[0][:, :, P * tt:P * tt + P], ring_tail.at(("aT", tt)).rearrange("p (k t) -> p k t", k=KC), 1.0, S("a_high"))

            def last_ln(tt):
                act.wait_ge(S("Dy_stat"), 4 * tt + 2)
                nc.scalar.activation(SD["D", "y"][:, tt % 2, :], MV["D", "y"][:, tt % 2, 1:2], ACT.Sqrt, bias=EPS).then_inc(S("Dy_sd"), 1)
                act.wait_ge(S("Dy_stat"), 4 * tt + 4)
                if tt >= 2:
                    act.wait_ge(S("Dx_new"), tt - 1)
                nc.scalar.activation(YZ[:, tt % 2, :], YACC[:, tt % 2, :], ACT.Identity, bias=NM["D", "y"][:, tt % 2, :],
                                     scale=RS["D", "y"][:, tt % 2, :]).then_inc(S("Dyn"), 1)

            for s in range(STEPS_D):
                if s < TT:
                    a_high(s)
                if 0 <= s - 2 < TT:
                    t_high("D", s - 2, ring_tail, ("TD", s - 2))
                t = s - 1
                if 0 <= t < TT:
                    ring_tail.wait_full(act, ("w", t))
                    ln_out("C", t, ring_tail.at(("w", t)), EPS * WSCALE ** 2, YN[:, t % 2, :], ring_tail.free(("w", t)))
                    deviation("D", "x", t, EPS)
                    ln_in("D", t, XN_B, ring_tail, lambda i: ("TD", i))
                t = s - 3
                for e in range(NE if t >= 0 else 0):
                    i = t * (NE - 1) + e - 1
                    if e == 0:
                        act.wait_ge(S("gates"), t + 1)
                        if t >= 2:
                            act.wait_ge(S("Dyn"), t - 1)
                    elif i >= 2:
                        act.wait_ge(S("acc"), i - 1)
                    ring_tail.wait_full(act, ("e", e, t))
                    nc.scalar.activation(YE[:, i % 2, :] if e else YACC[:, t % 2, :], ring_tail.at(("e", e, t)),
                                         ACT.Relu, scale=GS[:, t, e:e + 1]).then_inc(ring_tail.free(("e", e, t)), 1)
                    if e == 2 and t:
                        last_ln(t - 1)
            last_ln(TT - 1)

        @block.vector
        def _(dve):
            V = nc.vector

            def stats(s, w, tt, src):
                moments(s, w, tt, src)
                norm(s, w, tt)

            def moments(s, w, tt, src):
                done = S(s + w + "_stat")
                V.bn_stats(STAT[s, w][:, tt % 2, :], src).then_inc(done, 1)
                dve.wait_ge(done, 4 * tt + 1)
                V.bn_aggr(MV[s, w][:, tt % 2, :], STAT[s, w][:, tt % 2, :]).then_inc(done, 1)

            def norm(s, w, tt):
                i = tt % 2
                done = S(s + w + "_stat")
                dve.wait_ge(S(s + w + "_sd"), tt + 1)
                V.reciprocal(RS[s, w][:, i, :], SD[s, w][:, i, :]).then_inc(done, 1)
                dve.wait_ge(done, 4 * tt + 3)
                V.scalar_tensor_tensor(out=NM[s, w][:, i, :], in0=MV[s, w][:, i, 0:1], scalar=-1.0, in1=RS[s, w][:, i, :],
                                       op0=ALU.mult, op1=ALU.mult).then_inc(done, 1)

            def add_residual(s, tt, yn):
                V.tensor_tensor(X[:, tt, :], X[:, tt, :], yn[:, tt % 2, :], ALU.add).then_inc(S(s + "x_new"), 1)
                dve.wait_ge(S(s + "x_new"), tt + 1)

            def low(dst, src, scale, hi, sig):
                V.scalar_tensor_tensor(out=dst, in0=src, scalar=scale, in1=hi, op0=ALU.mult,
                                       op1=ALU.subtract).then_inc(sig, 1)

            def t_low(s, tt, ring, key):
                cols_ = slice(P * tt, P * tt + P)
                dve.wait_ge(S(s + "t_high"), tt + 1)
                low(XT[1][:, :, cols_], ring.at(key).rearrange("p (k t) -> p k t", k=KC), 1.0,
                    XT[0][:, :, cols_], ring.free(key))

            V.memset(L32[:, LA_N:LA_N + LB_N], 0.0).then_inc(S("lora_zero_b"), 1)
            V.memset(CUM, 0.0).then_inc(S("cum_zero"), 1)
            def fold(n):
                for i in range(2, 8):
                    k = 6 * n + i - 2
                    acc = NB[:, n % 2, :] if i % 2 else PB[:, n % 4, :]
                    dve.wait_ge(S("line"), 8 * n + i + 1)
                    if i >= 4:
                        dve.wait_ge(S("fold"), k - 1)
                    V.tensor_tensor(acc, acc, LN_[:, k % 3, :], ALU.max).then_inc(S("fold"), 1)
                dve.wait_ge(S("fold"), 6 * n + 6)
                V.tensor_tensor(PB[:, n % 4, :], PB[:, n % 4, :], NB[:, n % 2, :], ALU.subtract).then_inc(S("table"), 1)

            def piece_low(i):
                name, src, n, dst = pieces[i]
                dve.wait_ge(S("piece_high"), i + 1)
                if isinstance(dst, list):
                    low(flat(dst[1]), stage(i)[0][:, 0:n], WSCALE, flat(dst[0]), S("piece"))
                else:
                    low(dst[32:64, :], stage(i)[0][32:64, 0:n], WSCALE, dst[32:64, :], S("piece"))

            def add_lora(n):
                v = PB[:, n % 4, :].rearrange("p (k o) -> p k o", k=2)
                m = MSUM[:, 2 * (n % 2):2 * (n % 2) + 2, :]
                dve.wait_ge(S("scaled"), n + 1)
                if n in (2, 3):
                    V.tensor_tensor(m, m, v, ALU.add).then_inc(S("sum"), 1)
                    return
                if n in (4, 5):
                    dve.wait_ge(S("sum"), n - 3)
                    V.tensor_tensor(v, v, m, ALU.add).then_inc(S("sum"), 1)
                    dve.wait_ge(S("sum"), n - 1)
                ring_lora.wait_full(dve, n)
                V.scalar_tensor_tensor(out=v, in0=ring_lora.at(n), scalar=WSCALE, in1=v, op0=ALU.mult,
                                       op1=ALU.add).then_inc(ring_lora.free(n), 1)

            for n in range(STEPS_A):
                if n < N_HU:
                    fold(n)
                if 2 <= n - 1 < N_HU:
                    add_lora(n - 1)
                if n == N_HU:
                    piece_low(0)
                for tt in two_tiles(n - 3):
                    t_low("A", tt, ring_main, ("T", tt))
                for tt in two_tiles(n - 1):
                    i = tt % 4
                    dve.wait_ge(S("Ax_sd"), tt + 1)
                    V.reciprocal(RS["A", "x"][:, i, :], SD["A", "x"][:, i, :]).then_inc(S("Ax_norm"), 1)
                    dve.wait_ge(S("Ax_norm"), 2 * tt + 1)
                    V.scalar_tensor_tensor(out=NM["A", "x"][:, i, :], in0=MV["A", "x"][:, i, 0:1], scalar=-1.0,
                                           in1=RS["A", "x"][:, i, :], op0=ALU.mult, op1=ALU.mult).then_inc(S("Ax_norm"), 1)
                for tt in two_tiles(n):
                    if tt % 4 == 0:
                        dve.wait_ge(S(f"x_in{tt // 4}"), 16)
                    V.bn_stats(STAT["A", "x"][:, tt % 4, :], X[:, tt, :]).then_inc(S("Ax_stat"), 1)
                    dve.wait_ge(S("Ax_stat"), 2 * tt + 1)
                    V.bn_aggr(MV["A", "x"][:, tt % 4, :], STAT["A", "x"][:, tt % 4, :]).then_inc(S("Ax_stat"), 1)
                for kind, j, hf in taken_at.get(n, []):
                    key = (kind, j, hf)
                    tokens = slice(512 * hf, 512 * hf + 512)
                    i = j * HF + hf
                    if kind == "m":
                        dve.wait_ge(S("m_high"), i + 1)
                        low(M16[1][:, j, tokens], ring_main.at(key), 1 / (3 * WSCALE), M16[0][:, j, tokens], ring_main.free(key))
                    elif kind == "o":
                        dve.wait_ge(S("x1_high"), i + 1)
                        low(X1T[1][:, j, tokens], ring_main.at(key), 1 / WSCALE, X1T[0][:, j, tokens], ring_main.free(key))
                    else:
                        u = ("u", j, hf)
                        ring_main.wait_read(dve, key)
                        ring_main.wait_full(dve, u)
                        if i >= 4:
                            dve.wait_ge(S("h_low"), i - 3)
                        V.scalar_tensor_tensor(out=HFULL[:, i % 4, :], in0=ring_main.at(u), scalar=1 / WSCALE,
                                               in1=SG[:, i % 4, :], op0=ALU.mult, op1=ALU.mult).then_inc(ring_main.free(u), 1)

            def split_expert(e):
                slot, loaded, count, _ = stage(NW + e)
                dve.wait_ge(loaded, 16 * count)
                if e == 0:
                    dve.wait_ge(S("qk_out0"), 16 * (2 + 4))
                    dve.wait_ge(S("qk_out1"), 16 * (2 + 4))
                if e == 2:
                    ring_sc[0].wait_full(dve, (0, 7, 3, 1))
                if e == NE - 2:
                    ring_sc[1].wait_full(dve, (1, 7, 3, 1))
                V.tensor_scalar(flat(EW[e][0]), slot, WSCALE, None, ALU.mult).then_inc(S("expert_high"), 1)
                dve.wait_ge(S("expert_high"), e + 1)
                low(flat(EW[e][1]), slot, WSCALE, flat(EW[e][0]), S("piece"))

            for i in range(1, N_FIRST):
                piece_low(i)

            def split_projection(key):
                i = proj_split.index(key)
                dve.wait_ge(S("proj_high"), i + 1)
                if key[0] == "k":
                    c = slice(512 * key[1], 512 * key[1] + 512)
                    low(K16[1][:, c], ring_p.at(key), HD ** -0.5 / WSCALE, K16[0][:, c], ring_p.free(key))
                else:
                    c = slice(512 * key[2], 512 * key[2] + 512)
                    low(Q16[1][:, key[1], c], ring_p.at(key), 1 / WSCALE, Q16[0][:, key[1], c], ring_p.free(key))

            def sparsemax(t):
                z, zs, f, tau, w = (ZB[:, i, :] for i in range(5))
                count = [8 * t]

                def done(ins):
                    count[0] += 1
                    ins.then_inc(S("sparse"), 1)
                    dve.wait_ge(S("sparse"), count[0])

                ring_s.wait_read(dve, ("r", t))
                r = RSB[:, t % 2, :]
                if t == 0:
                    dve.wait_ge(S("cum_zero"), 1)
                    dve.wait_ge(S("consts"), 16 * 6)
                done(V.tensor_tensor(z, r[:, 0:NE], RB, ALU.add))
                done(V.max(CUM[:, 0, 4:4 + NE], z))
                done(V.tensor_tensor(CUM[:, 1, 4:4 + NE], CUM[:, 0, 4:4 + NE], CUM[:, 0, 3:3 + NE], ALU.add))
                done(V.tensor_tensor(CUM[:, 2, 4:4 + NE], CUM[:, 1, 4:4 + NE], CUM[:, 1, 2:2 + NE], ALU.add))
                done(V.tensor_tensor(zs, CUM[:, 2, 4:4 + NE], CUM[:, 2, 0:NE], ALU.add))
                done(V.scalar_tensor_tensor(out=f, in0=zs, scalar=-1.0, in1=INVK, op0=ALU.add, op1=ALU.mult))
                done(V.tensor_reduce(tau[:, 0:1], f, AX_X, ALU.max))
                done(V.tensor_scalar(w, z, tau[:, 0:1], 0.0, ALU.subtract, ALU.max))
                if t >= 2:
                    ring_s.wait_full(dve, ("H", t - 2))
                V.tensor_tensor(HWF[:, t % 2, :].rearrange("p (e r) -> p e r", e=NE),
                                r[:, NE:RN].rearrange("p (e r) -> p e r", e=NE),
                                w.rearrange("p (e a) -> p e a", a=1).to_broadcast([P, NE, R]), ALU.mult).then_inc(S("hw"), 1)

            dve.wait_ge(S("x_again0"), 16)
            dve.wait_ge(S("x_again1"), 16)
            def split_projections(keys):
                for key in keys:
                    if key[0] != "v":
                        split_projection(key)

            for s in range(STEPS_B):
                a, c = s - 1, s - 2
                has_a, has_c = 0 <= a < TT, 0 <= c < TT
                if has_a:
                    ring_d.wait_full(dve, a)
                    moments("A", "y", a, ring_d.at(a))
                if has_c:
                    ring_b.wait_full(dve, c)
                    moments("B", "y", c, ring_b.at(c))
                if has_a:
                    norm("A", "y", a)
                if has_c:
                    norm("B", "y", c)
                if has_a:
                    ring_d.wait_read(dve, a)
                    add_residual("A", a, YN)
                    moments("B", "x", a, X[:, a, :])
                if has_c:
                    ring_b.wait_read(dve, c)
                    add_residual("B", c, YN_B)
                    moments("C", "x", c, X[:, c, :])
                if has_a:
                    norm("B", "x", a)
                if has_c:
                    norm("C", "x", c)
                if s == TT:
                    V.memset(V1[:, :, HD:HD + 1], 1.0).then_inc(S("v1_ones"), 1)
                    V.memset(V1[:, :, HD + 1:32], 0.0).then_inc(S("v1_ones"), 1)
                split_projections(proj_at.get((s, 0), []))
                if has_a:
                    t_low("B", a, ring_s, ("TB", a))
                if has_c:
                    t_low("C", c, ring_s, ("TC", c))
                split_projections(proj_at.get((s, 1), []))
                if has_a:
                    sparsemax(a)
                split_projections(proj_at.get((s, 2), []) + proj_at.get((s, 3), []))
                if 2 <= s < 2 + NW - N_FIRST:
                    piece_low(N_FIRST + s - 2)
                if has_a:
                    dve.wait_ge(S("hw_high"), a + 1)
                    low(HWT[:, a % 2, P:2 * P], ring_s.at(("H", a))[:, 0:P], 1.0, HWT[:, a % 2, 0:P], ring_s.free(("H", a)))
                split_projections(proj_at.get((s, 4), []))

            def row_max(tt, h):
                g = max_heads(tt)
                if h % g == g - 1:
                    key, w = (tt, h - g + 1), P * (tt % 4 + 1)
                    ring_max.wait_full(dve, key)
                    V.tensor_reduce(MX[:, tt, h - g + 1:h + 1], ring_max.at(key)[:, 0:g * w].rearrange("p (g w) -> p g w", g=g),
                                    AX_X, ALU.max).then_inc(ring_max.free(key), 1)

            for i, key in enumerate(proj[1]):
                for t in (between[N_BETWEEN * (i - 1):N_BETWEEN * i] if i else []):
                    row_max(*t)
                split_projections([key])

            def sums(b, hg):
                i = b * 8 + hg
                ring_pv.wait_full(dve, ("pv", b, hg))
                if i >= 2:
                    ring_pv.wait_full(dve, ("pt", *groups[i - 2]))
                V.tensor_copy(OT[:, i % 2, :], ring_pv.at(("pv", b, hg))).then_inc(ring_pv.free(("pv", b, hg)), 1)

            def divide(b, hg):
                i = b * 8 + hg
                ring_pv.wait_full(dve, ("pt", b, hg))
                pt = ring_pv.at(("pt", b, hg)).rearrange("p (g d) -> p g d", d=32)
                V.reciprocal(RDEN[:, i % 2, :].rearrange("p (g a) -> p g a", a=1), pt[:, :, HD:HD + 1]).then_inc(S("rden"), 1)
                dve.wait_ge(S("rden"), i + 1)
                for qt in range(4):
                    o_ = ATTN[:, 4 * b + qt, 64 * hg:64 * hg + 64].rearrange("p (h d) -> p h d", d=HD)
                    ins = V.tensor_tensor(o_, pt[:, 4 * qt:4 * qt + 4, 0:HD],
                                          RDEN[:, i % 2, 4 * qt:4 * qt + 4].rearrange("p (g a) -> p g a", a=1)
                                          .to_broadcast([P, 4, HD]), ALU.mult)
                    ins.then_inc(ring_pv.free(("pt", b, hg)) if qt == 3 else S("divided"), 1)

            for t in alone:
                row_max(*t)
            for b in range(HF):
                for hg in range(8):
                    i = b * 8 + hg
                    for q in range(16 if b == 0 else 0):
                        m = 16 * hg + q
                        row_max(4 + m // HEADS, m % HEADS)
                        if q == 3 and i >= 1:
                            sums(*groups[i - 1])
                    if b:
                        sums(*groups[i - 1])
                    if i >= 2:
                        divide(*groups[i - 2])
                    if b == 1 and hg < NE - 2:
                        split_expert(hg)
            sums(*groups[-1])
            divide(*groups[-2])
            divide(*groups[-1])

            def gate(tt):
                count = [6 * tt]

                def done(ins):
                    count[0] += 1
                    ins.then_inc(S("rank"), 1)
                    dve.wait_ge(S("rank"), count[0])

                z, rank = ZB[:, 5, :], ZB[:, 0, :]
                a, b_ = (CMP[:, i, :].rearrange("p (e j) -> p e j", e=NE) for i in range(2))
                zj = z.rearrange("p (a j) -> p a j", a=1).to_broadcast([P, NE, NE])
                ze = z.rearrange("p (e a) -> p e a", a=1).to_broadcast([P, NE, NE])
                ring_tail.wait_full(dve, ("z", tt))
                V.scalar_tensor_tensor(out=z, in0=ring_tail.at(("z", tt))[:, 0:NE], scalar=1 / WSCALE, in1=GB,
                                       op0=ALU.mult, op1=ALU.add).then_inc(ring_tail.free(("z", tt)), 1)
                ring_tail.wait_read(dve, ("z", tt))
                done(V.tensor_tensor(a, zj, ze, ALU.is_gt))
                done(V.tensor_tensor(b_, zj, ze, ALU.is_equal))
                done(V.tensor_tensor(b_, b_, LT, ALU.mult))
                done(V.tensor_tensor(a, a, b_, ALU.add))
                done(V.tensor_reduce(rank, a, AX_X, ALU.add))
                done(V.tensor_scalar(GS[:, tt, :], rank, 1.5, 0.5 / WSCALE, ALU.is_lt, ALU.mult))
                V.tensor_copy(rank, GS[:, tt, :]).then_inc(S("gates"), 1)

            def last(tt):
                dve.wait_ge(S("acc"), (NE - 1) * (tt + 1))
                stats("D", "y", tt, YACC[:, tt % 2, :])
                dve.wait_ge(S("Dyn"), tt + 1)
                add_residual("D", tt, YZ)

            for s in range(STEPS_D):
                if s < TT:
                    cols_ = slice(P * s, P * s + P)
                    dve.wait_ge(S("a_high"), s + 1)
                    low(XT[1][:, :, cols_], ring_tail.at(("aT", s)).rearrange("p (k t) -> p k t", k=KC), 1.0,
                        XT[0][:, :, cols_], ring_tail.free(("aT", s)))
                if 0 <= s - 2 < TT:
                    t_low("D", s - 2, ring_tail, ("TD", s - 2))
                t = s - 1
                if 0 <= t < TT:
                    ring_tail.wait_full(dve, ("w", t))
                    stats("C", "y", t, ring_tail.at(("w", t)))
                    ring_tail.wait_read(dve, ("w", t))
                    add_residual("C", t, YN)
                    stats("D", "x", t, X[:, t, :])
                if s == 2:
                    split_expert(NE - 2)
                    split_expert(NE - 1)
                t = s - 3
                for e in range(NE if t >= 0 else 0):
                    if e:
                        i = t * (NE - 1) + e - 1
                        ring_tail.wait_read(dve, ("e", e, t))
                        if e == 1:
                            ring_tail.wait_read(dve, ("e", 0, t))
                        else:
                            dve.wait_ge(S("acc"), i)
                        V.tensor_tensor(YACC[:, t % 2, :], YACC[:, t % 2, :], YE[:, i % 2, :], ALU.add).then_inc(S("acc"), 1)
                    if e == 2 and t:
                        last(t - 1)
                if 0 <= s - 2 < TT:
                    gate(s - 2)
            last(TT - 1)

        @block.tensor
        def _(pe):
            mm = nc.tensor.matmul

            def transposes(ring, key, src):
                ring.wait_free(pe, key)
                for k in range(KC):
                    ins = nc.tensor.transpose(ring.at(key)[:, P * k:P * k + P], src[:, P * k:P * k + P], IDF)
                ins.then_inc(ring.full(key), 1)

            def product(dst, lhs, rhs, more=()):
                pairs = [(l[a], r[b]) for l, r in zip(lhs, rhs) for a, b in ((0, 0), (0, 1), (1, 0))]
                pairs += list(more)
                for i, (l, r) in enumerate(pairs):
                    ins = mm(dst, l, r, start=(i == 0), stop=(i == len(pairs) - 1))
                return ins

            def halves(w, k, c):
                return w[0][:, k, c], w[1][:, k, c]

            pe.wait_ge(S("ident_in"), 16)
            def lora(n):
                ring_lora.wait_free(pe, n)
                if n in (4, N_ATTN):
                    pe.wait_ge(S("lora_low"), 3 if n == 4 else 6)
                for i in range(2):
                    if n < N_ATTN:
                        m, kh = cols(n)
                        names = ("qk", "v") if m == 2 else ("o",)
                        pairs = [(LA[w] + P * (2 * kh + i), LA_N + LB[w]) for w in names]
                    elif n < N_ATTN + N_GU:
                        c, kh = cols(n - N_ATTN)
                        pairs = [(LA["gu"] + P * (2 * kh + i), LA_N + LB["gu"] + 512 * c)]
                    else:
                        pairs = [(LA["down"] + P * (2 * (n - N_ATTN - N_GU) + i), LA_N + LB["down"])]
                    for q, (a, b) in enumerate(pairs):
                        ins = mm(ring_lora.at(n)[:, i, :], L16[:, a:a + P], L16[:, b:b + 512],
                                 start=(q == 0), stop=(q == len(pairs) - 1))
                ins.then_inc(ring_lora.full(n), 1)

            waited = {"w": 0}

            def weights_ready(n):
                if waited["w"] < n - 3:
                    waited["w"] = n - 3
                    pe.wait_ge(S("w_low"), n - 3)

            for n in range(STEPS_A):
                if 4 <= n < N_HU:
                    lora(n)
                for tt in two_tiles(n - 2):
                    pe.wait_ge(S("Axn"), tt + 1)
                    transposes(ring_main, ("T", tt), XN_A[:, tt % 4, :])
                for kind, j, hf in taken_at.get(n + 1, []):
                    tokens = slice(512 * hf, 512 * hf + 512)
                    key = (kind, j, hf)
                    if kind == "m":
                        weights_ready(5)
                        if (j, hf) == (0, 0):
                            ring_main.wait_read(pe, ("T", TT - 2))
                            ring_main.wait_read(pe, ("T", TT - 1))
                        ring_main.wait_free(pe, key)
                        product(ring_main.at(key), [halves(MW, k, slice(P * j, P * j + P)) for k in range(KC)],
                                [halves(XT, k, tokens) for k in range(KC)]).then_inc(ring_main.full(key), 1)
                    elif kind == "o":
                        weights_ready(7)
                        if (j, hf) == (0, 0):
                            for i in range(len(j_hf) - 4, len(j_hf)):
                                ring_main.wait_read(pe, ("m", *j_hf[i]))
                            pe.wait_ge(S("consts"), 16 * 6)
                        ring_main.wait_free(pe, key)
                        product(ring_main.at(key), [halves(OW, k, slice(P * j, P * j + P)) for k in range(KC)],
                                [halves(M16, k, tokens) for k in range(KC)],
                                [(I256, XT[0][:, j, tokens]), (I256, XT[1][:, j, tokens])]).then_inc(ring_main.full(key), 1)
                    else:
                        c = j // 2
                        weights_ready(N_ATTN + 2 * c + 1)
                        if (j, hf) == (0, 0):
                            for i in range(len(j_hf) - 4, len(j_hf)):
                                ring_main.wait_read(pe, ("o", *j_hf[i]))
                        for g, what in enumerate("gu"):
                            w = slice(256 * g + P * (j % 2), 256 * g + P * (j % 2) + P)
                            key = (what, j, hf)
                            ring_main.wait_free(pe, key)
                            product(ring_main.at(key), [halves(GUW[c], k, w) for k in range(KC)],
                                    [halves(X1T, k, tokens) for k in range(KC)]).then_inc(ring_main.full(key), 1)

            ring_main.wait_all_free(pe)
            pe.wait_ge(S("h_low"), OC * HF)

            def project(key, between=()):
                ring_p.wait_free(pe, key)
                if key[0] == "v":
                    dst, w, x = ring_p.at(key)[:, 0:HD], (VW, slice(0, HD)), slice(P * key[1], P * key[1] + P)
                elif key[0] == "k":
                    dst, w, x = ring_p.at(key), (KW, slice(0, P)), slice(512 * key[1], 512 * key[1] + 512)
                else:
                    dst, w, x = ring_p.at(key), (QW, slice(P * key[1], P * key[1] + P)), slice(512 * key[2], 512 * key[2] + 512)
                ws = [halves(w[0], k, w[1]) for k in range(KC)]
                xs = [halves(XT, k, x) for k in range(KC)]
                lhs, rhs = (xs, ws) if key[0] == "v" else (ws, xs)
                pairs = [(l[a], r[b]) for l, r in zip(lhs, rhs) for a, b in ((0, 0), (0, 1), (1, 0))]
                for i, (l, r) in enumerate(pairs):
                    ins = mm(dst, l, r, start=(i == 0), stop=(i == len(pairs) - 1))
                    if i == len(pairs) - 1:
                        ins.then_inc(ring_p.full(key), 1)
                    if i % 3 == 2:
                        for t in between[i // 3 * len(between) // KC:(i // 3 + 1) * len(between) // KC]:
                            max_scores(*t)

            def down_parts(s):
                tile = slice(P * s, P * s + P)
                dst = ring_d.at(s)
                pairs = [(dst, H16[a][:, j, tile], DW[b][:, j, :]) for j in range(OC) for a, b in ((0, 0), (0, 1), (1, 0))]
                x1 = [(dst[:, P * k:P * k + P], X1T[half][:, k, tile], I256) for k in range(KC) for half in range(2)]
                return pairs[:-1] + x1 + pairs[-1:]

            def project_all(keys):
                for key in keys:
                    if key[0] != "q" and key[1] == 0:
                        ring_d.wait_read(pe, TT - 2 if key[0] == "k" else TT - 1)
                        if key[0] == "k":
                            pe.wait_ge(S("piece"), N_FIRST + TT - 2)
                            for t in range(4):
                                ring_s.wait_read(pe, ("TC", t))
                    project(key)

            n_early = 3 * (OC - 4)
            weights_ready(N_HU - 3)
            for s in range(2):
                for i, part in enumerate(down_parts(s)[:n_early]):
                    mm(*part, start=(i == 0), stop=False, skip_group_check=True)
            weights_ready(N_HU - 1)
            ring_lora.wait_all_free(pe)

            for s in range(STEPS_B):
                a, c = s - 1, s - 2
                has_a, has_c = 0 <= a < TT, 0 <= c < TT
                parts = down_parts(s) if s < TT else []
                cuts = (0, 5, 31, 41, len(parts))

                def down(part):
                    if part == 0 and parts:
                        ring_d.wait_free(pe, s)
                    for i in range(cuts[part], cuts[part + 1]) if parts else ():
                        if s < 2 and i < n_early:
                            continue
                        ins = mm(*parts[i], start=(i == 0), stop=(i == len(parts) - 1), skip_group_check=True)
                    if part == 3 and parts:
                        ins.then_inc(ring_d.full(s), 1)

                down(0)
                if has_c:
                    ring_s.wait_read(pe, ("H", c))
                    hi, lo = HWT[:, c % 2, 0:P], HWT[:, c % 2, P:2 * P]
                    mm(ring_b.at(c), hi, LBW[0], start=False, stop=False)
                    mm(ring_b.at(c), hi, LBW[1], start=False, stop=False)
                    mm(ring_b.at(c), lo, LBW[0], start=False, stop=True).then_inc(ring_b.full(c), 1)
                down(1)
                project_all(proj_at.get((s, 0), []))
                if has_a:
                    pe.wait_ge(S("Bxn"), a + 1)
                    transposes(ring_s, ("TB", a), XN_B[:, a % 2, :])
                if has_c:
                    pe.wait_ge(S("Cxn"), c + 1)
                    transposes(ring_s, ("TC", c), XN_C[:, c % 2, :])
                down(2)
                project_all(proj_at.get((s, 1), []))
                if has_a:
                    tile = slice(P * a, P * a + P)
                    if a == 0:
                        pe.wait_ge(S("piece"), N_FIRST)
                    ring_s.wait_read(pe, ("TB", a))
                    ring_s.wait_free(pe, ("r", a))
                    product(ring_s.at(("r", a))[:, 0:RN], [halves(XT, k, tile) for k in range(KC)],
                            [halves(RW, k, slice(0, RN)) for k in range(KC)]).then_inc(ring_s.full(("r", a)), 1)
                down(3)
                project_all(proj_at.get((s, 2), []))
                if has_a:
                    ring_b.wait_free(pe, a)
                    i = 0
                    for k in range(KC):
                        for x, w in ((0, 0), (0, 1), (1, 0)):
                            mm(ring_b.at(a), XT[x][:, k, tile], BW[w][:, k, :], start=(i == 0), stop=False)
                            i += 1
                    mm(ring_b.at(a), ONES, BB, start=False, stop=False)
                project_all(proj_at.get((s, 3), []))
                if has_a:
                    pe.wait_ge(S("hw"), a + 1)
                    ring_s.wait_free(pe, ("H", a))
                    nc.tensor.transpose(ring_s.at(("H", a))[:, 0:P], HWF[:, a % 2, :], IDF).then_inc(ring_s.full(("H", a)), 1)
                project_all(proj_at.get((s, 4), []))

            def max_scores(tt, h):
                b, qt = tt // 4, tt % 4
                g = max_heads(tt)
                key = (tt, h - h % g)
                w = P * (qt + 1)
                dst = ring_max.at(key)[:, w * (h % g):w * (h % g) + w]
                if h % g == 0:
                    ring_max.wait_free(pe, key)
                mm(dst, QX[b][:, h, P * qt:P * qt + P], KX[:, 512 * b:512 * b + w], start=True, stop=True)
                ins = mm(dst[:, w - P:w], IDB, MASKQ, start=False, stop=True, skip_group_check=True)
                if h % g == g - 1:
                    ins.then_inc(ring_max.full(key), 1)

            def max_transpose(tt):
                key = (tt, "t")
                g = max_heads(tt)
                for h in (HEADS - 2 * g, HEADS - g):
                    ring_max.wait_read(pe, (tt, h))
                ring_max.wait_free(pe, key)
                nc.tensor.transpose(ring_max.at(key)[0:HEADS, 0:P], MX[:, tt, :], IDF).then_inc(ring_max.full(key), 1)

            def score(b, hg, j, pairs=(0, 1)):
                w = 512 - P * j
                for hp in pairs:
                    key = (b, hg, j, hp)
                    ring_sc[b].wait_free(pe, key)
                    for i in range(2):
                        h = 4 * hg + 2 * hp + i
                        dst = ring_sc[b].at(key)[:, i, :]
                        mm(dst[:, 0:w], KX[:, 512 * b + P * j:512 * b + P * j + P], QX[b][:, h, P * j:512], start=True, stop=True)
                        ins = mm(dst[:, 0:P], IDB, MASKK, start=False, stop=True, skip_group_check=True)
                    ins.then_inc(ring_sc[b].full(key), 1)

            def weigh(b, hg, j, pairs=(0, 1)):
                i = (b * 8 + hg) * 4 + j
                w = 512 - P * j
                key = ("pv", b, hg)
                if j == 0 and pairs[0] == 0:
                    ring_pv.wait_free(pe, key)
                for h in (h for hp in pairs for h in (2 * hp, 2 * hp + 1)):
                    if h % 2 == 0:
                        ring_sc[b].wait_read(pe, (b, hg, j, h // 2))
                    ins = mm(ring_pv.at(key)[32 * h:32 * h + 32, P * j:512], V1[:, 4 * b + j, :], PT4[:, i % 2, h, 0:w],
                             start=(j == 0), stop=(j == 3), skip_group_check=True)
                    if h == 3:
                        ins.then_inc(ring_pv.full(key) if j == 3 else S("pv_done"), 1)

            def turn(b, hg):
                key = ("pt", b, hg)
                i = b * 8 + hg
                ring_pv.wait_free(pe, key)
                ring_pv.wait_read(pe, ("pv", b, hg))
                for qt in range(4):
                    ins = nc.tensor.transpose(ring_pv.at(key)[:, P * qt:P * qt + P], OT[:, i % 2, P * qt:P * qt + P], IDF)
                ins.then_inc(ring_pv.full(key), 1)

            ring_b.wait_all_free(pe)
            for t in range(4, TT):
                ring_s.wait_read(pe, ("TC", t))
            pe.wait_ge(S("piece"), NW)
            for i, key in enumerate(proj[1]):
                if i == 1:
                    pe.wait_ge(S("masks"), 3)
                    pe.wait_ge(S("qx0"), 16 * (2 + 4 + 8))
                mine = between[N_BETWEEN * (i - 1):N_BETWEEN * i] if i else []
                project(key, mine)
                if mine and mine[-1][1] == HEADS - 1:
                    max_transpose(mine[-1][0])
            for tt, h in alone:
                max_scores(tt, h)
                if h == HEADS - 1:
                    max_transpose(tt)
            ring_p.wait_all_free(pe)
            ring_s.wait_all_free(pe)
            pe.wait_ge(S("qx1"), 16 * (1 + 4 + 8))
            for b in range(HF):
                pe.wait_ge(S(f"m_in{b}"), 64)
                if b:
                    ring_sc[0].wait_all_free(pe)
                    ring_max.wait_all_free(pe)
                for hg in range(8):
                    for j in range(4):
                        i = (b * 8 + hg) * 4 + j - 1
                        before = (i // 32, i // 4 % 8, i % 4)
                        for pair in range(2):
                            if b == 0:
                                m = 16 * hg + 4 * j + pair
                                max_scores(4 + m // HEADS, m % HEADS)
                            score(b, hg, j, (pair,))
                        for pair in range(2):
                            if b == 0:
                                m = 16 * hg + 4 * j + 2 + pair
                                max_scores(4 + m // HEADS, m % HEADS)
                            if i >= 0:
                                weigh(*before, (pair,))
                    if b == 0 and hg % 2 == 1:
                        max_transpose(4 + hg // 2)
                    if (b, hg) != (0, 0):
                        turn(*groups[b * 8 + hg - 1])
            weigh(HF - 1, 7, 3)
            turn(HF - 1, 7)

            ring_sc[1].wait_all_free(pe)
            ring_pv.wait_all_free(pe)
            for s in range(STEPS_D):
                if s < TT:
                    transposes(ring_tail, ("aT", s), ATTN[:, s, :])
                if 0 <= s - 2 < TT:
                    t = s - 2
                    pe.wait_ge(S("Dxn"), t + 1)
                    transposes(ring_tail, ("TD", t), XN_B[:, t % 2, :])
                t = s - 3
                for e in range(NE if t >= 0 else 0):
                    if t == 0:
                        pe.wait_ge(S("piece"), NW + e + 1)
                    key = ("e", e, t)
                    ring_tail.wait_free(pe, key)
                    product(ring_tail.at(key), [halves(XT, k, slice(P * t, P * t + P)) for k in range(KC)],
                            [halves(EW[e], k, slice(0, D)) for k in range(KC)],
                            [(ONES, BE[:, D * e:D * e + D])]).then_inc(ring_tail.full(key), 1)
                t = s - 2
                if 0 <= t < TT:
                    key = ("z", t)
                    ring_tail.wait_read(pe, ("TD", t))
                    ring_tail.wait_free(pe, key)
                    product(ring_tail.at(key)[:, 0:NE], [halves(XT, k, slice(P * t, P * t + P)) for k in range(KC)],
                            [halves(GW, k, slice(0, NE)) for k in range(KC)]).then_inc(ring_tail.full(key), 1)
                t = s
                if t < TT:
                    key = ("w", t)
                    ring_tail.wait_read(pe, ("aT", t))
                    ring_tail.wait_free(pe, key)
                    product(ring_tail.at(key), [halves(XT, k, slice(P * t, P * t + P)) for k in range(KC)],
                            [halves(WOW, k, slice(0, D)) for k in range(KC)]).then_inc(ring_tail.full(key), 1)


def broadcast(src, n):
    if len(src.shape) == 1:
        src = src.rearrange("(a o) -> a o", a=1)
    rows, width = src.shape
    return bass.AP(tensor=src.tensor, offset=src.offset, ap=[list(src.ap[0]), [0, n], list(src.ap[1])])


def repeat(src, n):
    return bass.AP(tensor=src.tensor, offset=src.offset, ap=[[0, n], list(src.ap[0]), list(src.ap[1])])


def kernel(**inputs):
    import numpy as np
    import concourse.bacc as bacc
    from concourse.bass_utils import run_bass_kernel_spmd

    a = {k: np.asarray(v) for k, v in inputs.items()}
    perm = (4 * np.arange(P)[None, :] + np.arange(KC)[:, None]).reshape(-1)

    def rows(w):
        return w[perm].reshape(KC, P, -1).transpose(1, 0, 2).reshape(P, -1)

    def plain_rows(w):
        return w.reshape(-1, P, w.shape[-1]).transpose(1, 0, 2).reshape(P, -1)

    def bias_rows(b):
        t = np.zeros((P, b.shape[-1]), np.float32)
        t[0] = t[32] = b
        return t

    x = a["L0_attn_x"].reshape(TT, P, D)[:, :, perm].transpose(1, 0, 2)
    ca = a["L0_attn_codes_attn"]
    cg = a["L0_attn_codes_gu"].reshape(2, OC // 2, 256, D)
    sg = a["L0_attn_scales_gu"].reshape(2, OC // 2, 256, 8)
    cd = a["L0_attn_codes_down"][perm].T
    wr, la = a["L0_ffn_W_router"].T, a["L0_ffn_lora_A"].transpose(1, 0, 2).reshape(D, NE * R)
    wqkv = a["L1_attn_Wqkv"]
    A, B = a["L0_attn_lora_A_h"], a["L0_attn_lora_B_attn"]
    bgu = a["L0_attn_lora_B_gu"].reshape(2, OC // 2, 256, R)
    pos = np.arange(512, dtype=np.float64)
    base = 2.0 ** (-2.0 ** (-(5 - 3)))
    slopes = (base ** np.arange(1, HEADS + 1, dtype=np.float64)).astype(np.float32).astype(np.float64)
    s_hi = slopes.astype(np.float16)
    s_lo = (slopes - s_hi).astype(np.float16)
    alibi_q = np.zeros((16, HEADS, 512), np.float16)
    for i, s in ((0, s_hi), (3, s_lo)):
        s = s.astype(np.float64)[:, None]
        alibi_q[i] = s
        alibi_q[i + 1] = -s * pos
        alibi_q[i + 2] = -s * pos - alibi_q[i + 1].astype(np.float64)
    alibi_k = np.zeros((16, T), np.float16)
    alibi_k[0] = alibi_k[3] = np.tile(pos, HF)
    alibi_k[[1, 2, 4, 5, 6]] = 1.0
    ones_rows = np.zeros((P, P), np.float16)
    ones_rows[[0, 32]] = 1.0

    data = {
        "x": x,
        "codes_attn": np.stack([rows(ca[m][perm].T) for m in range(4)]),
        "scales_attn": np.stack([a["L0_attn_scales_attn"][m][perm].T for m in range(4)]),
        "codes_gu": np.stack([rows(cg[:, c].reshape(512, D).T) for c in range(OC // 2)]),
        "scales_gu": np.stack([sg[:, c].reshape(512, 8).T for c in range(OC // 2)]),
        "codes_down": np.stack([plain_rows(cd[256 * d:256 * d + 256]) for d in range(N_DOWN)]),
        "scales_down": a["L0_attn_scales_down"][perm].T,
        "a_q": A[0][:, perm], "a_k": A[1][:, perm], "a_v": A[2][:, perm], "a_o": A[3][:, perm],
        "a_g": A[4][:, perm], "a_u": A[5][:, perm], "a_down": a["L0_attn_lora_A_down"],
        "b_q": B[0][perm].T, "b_k": B[1][perm].T, "b_v": B[2][perm].T, "b_o": B[3][perm].T,
        "b_g": bgu[0].transpose(2, 0, 1), "b_u": bgu[1].transpose(2, 0, 1),
        "b_down": a["L0_attn_lora_B_down"][perm].T,
        "w_base": rows(a["L0_ffn_W_base"][perm].T), "b_base": bias_rows(a["L0_ffn_b_base"][perm]),
        "w_rl": rows(np.concatenate([wr, la], axis=1)), "b_router": a["L0_ffn_b_router"],
        "lora_b": a["L0_ffn_lora_B"].reshape(NE * R, D)[:, perm],
        "w_q": rows(wqkv[:, :D]), "w_k": rows(np.tile(wqkv[:, D:D + HD], (1, NE))), "w_v": rows(wqkv[:, D + HD:]),
        "w_o": plain_rows(a["L1_attn_Wo"][:, perm]),
        "w_gate": rows(a["L1_ffn_W_gate"]), "b_gate": a["L1_ffn_b_gate"],
        "w_e": np.stack([rows(a["L1_ffn_W_e"][e][:, perm]) for e in range(NE)]),
        "b_e": bias_rows(a["L1_ffn_b_e"][:, perm].reshape(-1)),
        "ident": np.eye(P, dtype=np.float32), "ident256": np.eye(P, dtype=np.float16) * np.float16(WSCALE),
        "ones_rows": ones_rows, "inv_k": np.tile((1.0 / np.arange(1, NE + 1)).astype(np.float32), (P, 1)),
        "before": np.tile(np.tril(np.ones((NE, NE), np.float32), -1).reshape(1, -1), (P, 1)),
        "alibi_q": alibi_q, "alibi_k": alibi_k,
    }
    nc = bacc.Bacc("TRN2", target_bir_lowering=False, num_devices=1)
    arrays, handles = {}, {}
    for name, v in data.items():
        arrays[f"in_{name}"] = np.ascontiguousarray(v)
        handles[name] = nc.dram_tensor(f"in_{name}", arrays[f"in_{name}"].shape, mybir.dt.from_np(v.dtype), kind="ExternalInput").ap()
    out = nc.dram_tensor("out", (P, TT, D), F32, kind="ExternalOutput").ap()
    sandwich(nc, handles, out)
    r = run_bass_kernel_spmd(nc, [arrays], core_ids=[0])
    got = np.asarray(r.results[0]["out"])
    y = np.empty((TT, P, D), np.float32)
    y[:, :, perm] = got.transpose(1, 0, 2)
    return y.reshape(HF, 512, D)
```
